# Optimizing a Trainium2 kernel written in Bass

```python
import numpy as np
import jax
import jax.numpy as jnp

def _softmax(x, axis=-1):
    return jax.nn.softmax(x, axis=axis)

def _gelu(x):
    return jax.nn.gelu(x, approximate=True)

def _silu(x):
    return jax.nn.silu(x)

def _sigmoid(x):
    return jax.nn.sigmoid(x)

def _layernorm(x, axis=-1, eps=1e-05):
    m = jnp.mean(x, axis=axis, keepdims=True)
    v = jnp.var(x, axis=axis, keepdims=True)
    return (x - m) / jnp.sqrt(v + eps)

def _scatter_add(tgt, idx, src, axis=0):
    return tgt.at[idx].add(src)

def _segment_sum(src, seg, n):
    return jax.ops.segment_sum(src, seg, n)
kernel_name = 'mk_xattn_ffn_d2_seqx_r8_a4a175'

def setup_inputs(seed: int=0):
    np.random.seed(seed)
    _w = jnp.asarray

    def _rec_inputs():
        import jax
        import jax.numpy as jnp
        _rk = jax.random.key(seed)
        x = 0.002226 + 0.9996 * jax.random.normal(jax.random.fold_in(_rk, 1), (64, 64, 128), jnp.float32)
        _lenS = 64 - jax.random.randint(jax.random.fold_in(_rk, 7), (64,), 0, max(1, 64 // 4) + 1, jnp.int32)
        _lenS2 = 64 - jax.random.randint(jax.random.fold_in(_rk, 8), (64,), 0, max(1, 64 // 4) + 1, jnp.int32)
        _ctx_1024P = jax.random.normal(jax.random.fold_in(_rk, 11), (64, 16, 128), jnp.float32)
        _ctx_1024c = jax.random.dirichlet(jax.random.fold_in(_rk, 511), 0.3 * jnp.ones((16,), jnp.float32), (64, 64))
        _ctx_1024t = jnp.einsum('bsk,bkd->bsd', _ctx_1024c, _ctx_1024P)
        _ctx_1024t = _ctx_1024t * jax.lax.rsqrt(jnp.mean(jnp.square(_ctx_1024t)) + 1e-12) * 0.953939
        ctx_1024 = -0.000125008 + 0.999885 * (_ctx_1024t + 0.3 * jax.random.normal(jax.random.fold_in(_rk, 611), (64, 64, 128), jnp.float32))
        fside_BxSxS2_0 = jax.random.uniform(jax.random.fold_in(_rk, 12), (64, 64, 64), jnp.float32, 0.0, 1)
        _validS = jnp.arange(64)[None, :] < _lenS[:, None]
        _validS2 = jnp.arange(64)[None, :] < _lenS2[:, None]
        _causal = jnp.tril(jnp.ones((64, 64), dtype=bool))
        mask_BxSxS2_ik1 = jnp.where(jnp.broadcast_to(_validS2[:, None, :], (64, 64, 64)), 1, 0).astype(jnp.int32)
        return (x, ctx_1024, fside_BxSxS2_0, mask_BxSxS2_ik1)
    x, ctx_1024, fside_BxSxS2_0, mask_BxSxS2_ik1 = _rec_inputs()

    def _L0_xattn_setup():
        import jax, jax.numpy as jnp
        import numpy as np
        EPS = 1e-05

        def layer_norm(x, g, b):
            mu = jnp.mean(x, axis=-1, keepdims=True)
            var = jnp.var(x, axis=-1, keepdims=True)
            return (x - mu) * jax.lax.rsqrt(var + EPS) * g + b
        key = jax.random.key(seed)
        ks = jax.random.split(key, 8)
        dim, heads, dim_head = (128, 16, 64)
        inner = heads * dim_head
        b, n, m = (8, 512, 64)
        s = dim ** (-0.5)
        return {'x': jax.random.normal(ks[0], (b, n, dim), jnp.float32), 'latents': jax.random.normal(ks[1], (b, m, dim), jnp.float32), 'ln_m_g': jnp.ones((dim,), jnp.float32), 'ln_m_b': jnp.zeros((dim,), jnp.float32), 'ln_l_g': jnp.ones((dim,), jnp.float32), 'ln_l_b': jnp.zeros((dim,), jnp.float32), 'Wq': jax.random.normal(ks[2], (dim, inner), jnp.float32) * s, 'Wkv': jax.random.normal(ks[3], (dim, 2 * inner), jnp.float32) * s, 'Wout': jax.random.normal(ks[4], (inner, dim), jnp.float32) * s}
    _L0_xattn_all = _L0_xattn_setup()
    _L0_xattn_in = {k: v for k, v in _L0_xattn_all.items() if k in ('ln_m_g', 'ln_m_b', 'ln_l_g', 'ln_l_b', 'Wq', 'Wkv', 'Wout')}
    del _L0_xattn_all

    def _L0_ffn_setup():
        import jax, jax.numpy as jnp
        import numpy as np
        N_EXPERT_CAPACITY = 2
        key = jax.random.key(seed)
        k1, k2, k3, k4 = jax.random.split(key, 4)
        B, S, D, E, F = (8, 128, 128, 8, 256)
        x = jax.random.normal(k1, (B, S, D), dtype=jnp.float32)
        choice_w = jax.random.uniform(k2, (E, D), dtype=jnp.float32, minval=-1.0, maxval=1.0) * (1.0 / np.sqrt(D))
        w1 = jax.random.uniform(k3, (E, D, F), dtype=jnp.float32, minval=-1.0, maxval=1.0) * (1.0 / np.sqrt(D))
        w2 = jax.random.uniform(k4, (E, F, D), dtype=jnp.float32, minval=-1.0, maxval=1.0) * (1.0 / np.sqrt(F))
        return {'x': x, 'choice_w': choice_w, 'w1': w1, 'w2': w2}
    _L0_ffn_all = _L0_ffn_setup()
    _L0_ffn_in = {k: v for k, v in _L0_ffn_all.items() if k in ('choice_w', 'w1', 'w2')}
    del _L0_ffn_all

    def _L1_xattn_setup():
        import jax, jax.numpy as jnp
        import numpy as np
        NUM_HEADS = 16
        HIDDEN = 128
        B, S = (2, 256)

        def _split_heads(x, H):
            b, s, d = x.shape
            return x.reshape(b, s, H, d // H).transpose(0, 2, 1, 3)
        key = jax.random.key(seed)
        ks = jax.random.split(key, 14)
        D = HIDDEN
        scale = 1.0 / np.sqrt(D)
        inp = {'query': jax.random.normal(ks[0], (B, S, D), jnp.float32), 'key_in': jax.random.normal(ks[1], (B, S, D), jnp.float32), 'value': jax.random.normal(ks[2], (B, S, D), jnp.float32), 'group_prob': jax.random.uniform(ks[3], (B, S, S), jnp.float32), 'mask': jax.random.randint(ks[4], (B, S, S), 0, 2, jnp.int32), 'wq_k': jax.random.normal(ks[5], (D, D), jnp.float32) * scale, 'wq_b': jnp.zeros((D,), jnp.float32), 'wk_k': jax.random.normal(ks[6], (D, D), jnp.float32) * scale, 'wk_b': jnp.zeros((D,), jnp.float32), 'wv_k': jax.random.normal(ks[7], (D, D), jnp.float32) * scale, 'wv_b': jnp.zeros((D,), jnp.float32), 'wo_k': jax.random.normal(ks[8], (D, D), jnp.float32) * scale, 'wo_b': jnp.zeros((D,), jnp.float32)}
        return inp
    _L1_xattn_all = _L1_xattn_setup()
    _L1_xattn_in = {k: v for k, v in _L1_xattn_all.items() if k in ('wq_k', 'wq_b', 'wk_k', 'wk_b', 'wv_k', 'wv_b', 'wo_k', 'wo_b')}
    del _L1_xattn_all

    def _L1_ffn_setup():
        import jax, jax.numpy as jnp
        import numpy as np
        B, S, D = (2, 256, 128)
        E, K, F = (16, 2, 64)
        FS = 128
        key = jax.random.key(seed)
        ks = jax.random.split(key, 8)

        def w(k, shape, fan_in):
            return jax.random.normal(k, shape, jnp.float32) / np.sqrt(fan_in).astype(np.float32)
        return {'x': jax.random.normal(ks[0], (B, S, D), jnp.float32), 'Wr': w(ks[1], (D, E), D), 'Wg': w(ks[2], (E, D, F), D), 'Wu': w(ks[3], (E, D, F), D), 'Wd': w(ks[4], (E, F, D), F), 'Sg': w(ks[5], (D, FS), D), 'Su': w(ks[6], (D, FS), D), 'Sd': w(ks[7], (FS, D), FS)}
    _L1_ffn_all = _L1_ffn_setup()
    _L1_ffn_in = {k: v for k, v in _L1_ffn_all.items() if k in ('Wr', 'Wg', 'Wu', 'Wd', 'Sg', 'Su', 'Sd')}
    del _L1_ffn_all
    return {'x': x, 'ctx_1024': ctx_1024, 'fside_BxSxS2_0': fside_BxSxS2_0, 'mask_BxSxS2_ik1': mask_BxSxS2_ik1, 'L0_xattn_ln_m_g': _L0_xattn_in['ln_m_g'], 'L0_xattn_ln_m_b': _L0_xattn_in['ln_m_b'], 'L0_xattn_ln_l_g': _L0_xattn_in['ln_l_g'], 'L0_xattn_ln_l_b': _L0_xattn_in['ln_l_b'], 'L0_xattn_Wq': _L0_xattn_in['Wq'], 'L0_xattn_Wkv': _L0_xattn_in['Wkv'], 'L0_xattn_Wout': _L0_xattn_in['Wout'], 'L0_ffn_choice_w': _L0_ffn_in['choice_w'], 'L0_ffn_w1': _L0_ffn_in['w1'], 'L0_ffn_w2': _L0_ffn_in['w2'], 'L1_xattn_wq_k': _L1_xattn_in['wq_k'], 'L1_xattn_wq_b': _L1_xattn_in['wq_b'], 'L1_xattn_wk_k': _L1_xattn_in['wk_k'], 'L1_xattn_wk_b': _L1_xattn_in['wk_b'], 'L1_xattn_wv_k': _L1_xattn_in['wv_k'], 'L1_xattn_wv_b': _L1_xattn_in['wv_b'], 'L1_xattn_wo_k': _L1_xattn_in['wo_k'], 'L1_xattn_wo_b': _L1_xattn_in['wo_b'], 'L1_ffn_Wr': _L1_ffn_in['Wr'], 'L1_ffn_Wg': _L1_ffn_in['Wg'], 'L1_ffn_Wu': _L1_ffn_in['Wu'], 'L1_ffn_Wd': _L1_ffn_in['Wd'], 'L1_ffn_Sg': _L1_ffn_in['Sg'], 'L1_ffn_Su': _L1_ffn_in['Su'], 'L1_ffn_Sd': _L1_ffn_in['Sd']}

def reference(x, ctx_1024, fside_BxSxS2_0, mask_BxSxS2_ik1, L0_xattn_ln_m_g, L0_xattn_ln_m_b, L0_xattn_ln_l_g, L0_xattn_ln_l_b, L0_xattn_Wq, L0_xattn_Wkv, L0_xattn_Wout, L0_ffn_choice_w, L0_ffn_w1, L0_ffn_w2, L1_xattn_wq_k, L1_xattn_wq_b, L1_xattn_wk_k, L1_xattn_wk_b, L1_xattn_wv_k, L1_xattn_wv_b, L1_xattn_wo_k, L1_xattn_wo_b, L1_ffn_Wr, L1_ffn_Wg, L1_ffn_Wu, L1_ffn_Wd, L1_ffn_Sg, L1_ffn_Su, L1_ffn_Sd):
    import jax
    import jax.numpy as jnp

    def _L0_xattn_ref(x, latents, ln_m_g, ln_m_b, ln_l_g, ln_l_b, Wq, Wkv, Wout):
        import jax, jax.numpy as jnp
        import numpy as np
        EPS = 1e-05

        def layer_norm(x, g, b):
            mu = jnp.mean(x, axis=-1, keepdims=True)
            var = jnp.var(x, axis=-1, keepdims=True)
            return (x - mu) * jax.lax.rsqrt(var + EPS) * g + b
        heads, dim_head = (16, 64)
        scale = dim_head ** (-0.5)
        x = layer_norm(x, ln_m_g, ln_m_b)
        lat = layer_norm(latents, ln_l_g, ln_l_b)
        b, m, _ = lat.shape
        q = lat @ Wq
        kv_input = jnp.concatenate([x, lat], axis=1)
        kv = kv_input @ Wkv
        k, v = jnp.split(kv, 2, axis=-1)

        def split_heads(t):
            return t.reshape(t.shape[0], t.shape[1], heads, dim_head).transpose(0, 2, 1, 3)
        q, k, v = (split_heads(q), split_heads(k), split_heads(v))
        dots = jnp.einsum('bhid,bhjd->bhij', q, k) * scale
        attn = jax.nn.softmax(dots, axis=-1)
        out = jnp.einsum('bhij,bhjd->bhid', attn, v)
        out = out.transpose(0, 2, 1, 3).reshape(b, m, heads * dim_head)
        return out @ Wout

    def _L0_ffn_ref(x, choice_w, w1, w2):
        import jax, jax.numpy as jnp
        import numpy as np
        N_EXPERT_CAPACITY = 2
        B, S, D = x.shape
        E = choice_w.shape[0]
        k = S * N_EXPERT_CAPACITY // E
        probs = jax.nn.softmax(jnp.einsum('bsd,ed->bse', x, choice_w), axis=-1)
        G, I = jax.lax.top_k(jnp.swapaxes(probs, -1, -2), k)
        x_in = jnp.take_along_axis(x[:, None, :, :], I[..., None], axis=2)
        h = jax.nn.silu(jnp.einsum('bekd,edf->bekf', x_in, w1))
        x_mlp = jnp.einsum('bekf,efd->bekd', h, w2)
        b_idx = jnp.arange(B)[:, None, None]
        out = jnp.zeros_like(x).at[b_idx, I].add(G[..., None] * x_mlp)
        return out

    def _L1_xattn_ref(query, key_in, value, group_prob, mask, wq_k, wq_b, wk_k, wk_b, wv_k, wv_b, wo_k, wo_b):
        import jax, jax.numpy as jnp
        import numpy as np
        NUM_HEADS = 16
        HIDDEN = 128
        B, S = (2, 256)

        def _split_heads(x, H):
            b, s, d = x.shape
            return x.reshape(b, s, H, d // H).transpose(0, 2, 1, 3)
        H = NUM_HEADS
        dh = query.shape[-1] // H
        q = _split_heads(query @ wq_k + wq_b, H)
        k = _split_heads(key_in @ wk_k + wk_b, H)
        v = _split_heads(value @ wv_k + wv_b, H)
        logits = jnp.einsum('bhqd,bhkd->bhqk', q, k) / jnp.sqrt(jnp.asarray(dh, q.dtype))
        neg = (1.0 - mask.astype(q.dtype)) * -1000000000.0
        logits = logits + neg[:, None, :, :]
        attn = jax.nn.softmax(logits, axis=-1)
        attn = attn * group_prob[:, None, :, :]
        out = jnp.einsum('bhqk,bhkd->bhqd', attn, v)
        out = out.transpose(0, 2, 1, 3).reshape(query.shape[0], -1, H * dh)
        return out @ wo_k + wo_b

    def _L1_ffn_ref(x, Wr, Wg, Wu, Wd, Sg, Su, Sd):
        import jax, jax.numpy as jnp
        import numpy as np
        B, S, D = (2, 256, 128)
        E, K, F = (16, 2, 64)
        FS = 128
        b, s, d = x.shape
        T = b * s
        xf = x.reshape(T, d)
        shared = jax.nn.silu(xf @ Sg) * (xf @ Su) @ Sd
        probs = jax.nn.softmax(xf @ Wr, axis=-1)
        topk_p, topk_i = jax.lax.top_k(probs, K)
        n_exp = Wr.shape[1]
        cw = jnp.zeros((T, n_exp), x.dtype).at[jnp.arange(T)[:, None], topk_i].add(topk_p)

        def step(acc, ew):
            wg, wu, wd, c = ew
            y = jax.nn.silu(xf @ wg) * (xf @ wu) @ wd
            return (acc + y * c[:, None], None)
        routed, _ = jax.lax.scan(step, jnp.zeros_like(xf), (Wg, Wu, Wd, cw.T))
        return (routed + shared).reshape(b, s, d)
    x = x + _L0_xattn_ref(ctx_1024, _layernorm(x, axis=-1), L0_xattn_ln_m_g, L0_xattn_ln_m_b, L0_xattn_ln_l_g, L0_xattn_ln_l_b, L0_xattn_Wq, L0_xattn_Wkv, L0_xattn_Wout)
    x = x + _L0_ffn_ref(_layernorm(x, axis=-1), L0_ffn_choice_w, L0_ffn_w1, L0_ffn_w2)
    x = x + _L1_xattn_ref(_layernorm(x, axis=-1), ctx_1024, ctx_1024, fside_BxSxS2_0, mask_BxSxS2_ik1, L1_xattn_wq_k, L1_xattn_wq_b, L1_xattn_wk_k, L1_xattn_wk_b, L1_xattn_wv_k, L1_xattn_wv_b, L1_xattn_wo_k, L1_xattn_wo_b)
    x = x + _L1_ffn_ref(_layernorm(x, axis=-1), L1_ffn_Wr, L1_ffn_Wg, L1_ffn_Wu, L1_ffn_Wd, L1_ffn_Sg, L1_ffn_Su, L1_ffn_Sd)
    return x

_drawn_inputs = setup_inputs


def setup_inputs(seed=0):
    import zlib

    import numpy as np

    out = dict(_drawn_inputs(seed))
    spreads = {'L0_xattn_ln_m_g': (1.0, 0.2),
     'L0_xattn_ln_m_b': (0.0, 0.1),
     'L0_xattn_ln_l_g': (1.0, 0.2),
     'L0_xattn_ln_l_b': (0.0, 0.1),
     'L1_xattn_wq_b': (0.0, 0.512),
     'L1_xattn_wk_b': (0.0, 0.8),
     'L1_xattn_wv_b': (0.0, 0.1),
     'L1_xattn_wo_b': (0.0, 0.1)}
    factors = {}
    for name, (base, spread) in spreads.items():
        noise = np.random.default_rng([zlib.crc32(name.encode()), seed]).standard_normal(out[name].shape)
        drawn = base * np.exp(spread * noise) if base else spread * noise
        out[name] = jnp.asarray(drawn.astype(out[name].dtype))
    for name, factor in factors.items():
        out[name] = (out[name] * factor).astype(out[name].dtype)
    return out
```

```python
from contextlib import ExitStack

import concourse.bass as bass
from concourse import mybir

F32 = mybir.dt.float32
FR = mybir.dt.float32r
I32 = mybir.dt.int32
U32 = mybir.dt.uint32
ALU = mybir.AluOpType
ACT = mybir.ActivationFunctionType
AX = mybir.AxisListType.X

P = 128
EPS = 1e-5


class Clock:

    def __init__(self, eng, step=1, keys=()):
        self.eng, self.step, self.keys, self.regs = eng, step, dict(keys), {}

    def enter(self, u):
        self.u, self.regs = u, {}
        for mul, add in ((per * self.step, add) for per, adds in self.keys.items() for add in adds):
            self.regs[mul, add] = self.eng.to_reg(u * mul + add if add else u * mul)

    def leave(self):
        self.regs = {}

    def ge(self, sem, per, tile, k, alone=False):
        u, c = tile
        if u is None:
            if per * c + k > 0:
                self.eng.wait_ge(sem, per * c + k)
            return
        key = (per * self.step, per * c + k)
        self.eng.wait_ge(sem, self.regs[key])
        if alone:
            self.eng.nop(nofuse=True)


def at(tile, d):
    return (tile[0], tile[1] + d)


def live(tile, lo, hi):
    return tile[0] is not None or lo <= tile[1] < hi


def build_identity(nc, eng, ident, made):
    eng.memset(ident[:], 0.0).then_inc(made, 1)
    eng.wait_ge(made, 1)
    eng.affine_select(out=ident[:], in_=ident[:], compare_op=ALU.not_equal, fill=1.0, base=0,
                      pattern=[[-1, P]], channel_multiplier=1).then_inc(made, 1)


def fold_weights(nc, A, resid, kvraw, ident, wts):
    D, INNER = A["wq"].shape
    DH = 64
    H = INNER // DH
    NB, S, _ = A["x"].shape
    with ExitStack() as ctx:
        def sb(name, shape, dt=F32):
            return ctx.enter_context(nc.sbuf_tensor(name, shape, dt))

        def sem(name):
            return ctx.enter_context(nc.semaphore(name))

        wq = sb("wq_raw", [D, INNER])
        wkv = sb("wkv_raw", [D, 2 * INNER])
        wo = sb("wo_raw", [P, INNER // P, D])
        wqT = sb("wqT", [P, H // 2, D])
        wkT = sb("wkT", [P, H // 2, D])
        wvT = sb("wvT", [P, H // 2, D])
        bank = [ctx.enter_context(nc.psum_tensor(f"fold_ps{i}", [P, 512], F32)) for i in range(2)]
        s_wq, s_wkv, s_wo, s_in = sem("s_wq"), sem("s_wkv"), sem("s_wo"), sem("s_in")
        s_ident = sem("s_ident")
        s_wT = sem("s_wT")
        s_wTc = sem("s_wTc")
        s_prod = sem("s_prod")
        s_fold = sem("s_fold")
        NT = 3 * H // 8
        NP = 2 * H // 4
        block = ctx.enter_context(nc.Block())

        @block.sync
        def _(sp):
            sp.dma_start(wq[:], A["wq"]).then_inc(s_wq, 16)
            sp.dma_start(wkv[:], A["wkv"]).then_inc(s_wkv, 16)
            sp.dma_start(wo[:], A["wout"].rearrange("(t p) n -> p t n", p=P)).then_inc(s_wo, 16)
            kv = kvraw[:].rearrange("p (b d) -> p b d", d=D)
            sp.dma_start(kv[0:S], A["ctx"].rearrange("b s d -> s b d")).then_inc(s_in, 16)
            sp.dma_start(kv[S:2 * S], A["x"].rearrange("b s d -> s b d")).then_inc(s_in, 16)
            sp.dma_start(resid[:].rearrange("p (t d) -> p t d", d=D),
                         A["x"].rearrange("(t b) s d -> (b s) t d", b=2)).then_inc(s_in, 16)
            sp.dma_start(wts["gain"][0:S], A["ln_m_g"].partition_broadcast(S)).then_inc(s_in, 16)
            sp.dma_start(wts["gain"][S:2 * S], A["ln_l_g"].partition_broadcast(S)).then_inc(s_in, 16)
            sp.dma_start(wts["shift"][0:S], A["ln_m_b"].partition_broadcast(S)).then_inc(s_in, 16)
            sp.dma_start(wts["shift"][S:2 * S], A["ln_l_b"].partition_broadcast(S)).then_inc(s_in, 16)
            sp.wait_ge(s_in, 7 * 16)

        @block.gpsimd
        def _(pool):
            build_identity(nc, nc.gpsimd, ident, s_ident)

        def source(n):
            kind, half = n // (H // 8), n % (H // 8)
            src, off = [(wq, 0), (wkv, 0), (wkv, INNER)][kind]
            return src, off + half * 512, [wqT, wkT, wvT][kind][:, half * 4:half * 4 + 4, :]

        @block.tensor
        def _(pe):
            pe.wait_ge(s_ident, 2)
            for n in range(NT):
                src, off, _ = source(n)
                pe.wait_ge(s_wq if n < H // 8 else s_wkv, 16)
                if n >= 2:
                    pe.wait_ge(s_wTc, n - 1)
                for k in range(4):
                    mm = nc.tensor.transpose(bank[n % 2][:, k * P:(k + 1) * P],
                                             src[:, off + k * P:off + (k + 1) * P], ident[:])
                mm.then_inc(s_wT, 1)
            pe.wait_ge(s_wTc, NT)
            pe.wait_ge(s_wo, 16)
            for n in range(NP):
                if n >= 2:
                    pe.wait_ge(s_fold, n - 1)
                for k in range(4):
                    q = n % (NP // 2)
                    h = 8 * (q // 2) + 2 * k + q % 2
                    r = slice((h % 2) * DH, (h % 2) * DH + DH)
                    if n < NP // 2:
                        mm = nc.tensor.matmul(bank[n % 2][:, k * P:(k + 1) * P], wqT[r, h // 2, :],
                                              wkT[r, h // 2, :], start=True, stop=True)
                    else:
                        mm = nc.tensor.matmul(bank[n % 2][:, k * P:(k + 1) * P], wvT[r, h // 2, :],
                                              wo[r, h // 2, :], start=True, stop=True)
                mm.then_inc(s_prod, 1)

        def folded(n):
            q = n % (NP // 2)
            name, scale = ("A", -float(DH) ** -0.5) if n < NP // 2 else ("V", 1.0)
            dst = wts[name][:].rearrange("p (g k e d) -> p g k e d", g=2, k=4, e=2)[:, q // 2, :, q % 2, :]
            return dst, scale

        @block.scalar
        def _(act):
            for n in range(NT):
                act.wait_ge(s_wT, n + 1)
                nc.scalar.activation(source(n)[2], bank[n % 2][:].rearrange("p (a b) -> p a b", a=4),
                                     ACT.Copy).then_inc(s_wTc, 1)
            for n in range(NP):
                act.wait_ge(s_prod, n + 1)
                dst, scale = folded(n)
                nc.scalar.activation(dst, bank[n % 2][:].rearrange("p (k d) -> p k d", k=4), ACT.Copy,
                                     scale=scale).then_inc(s_fold, 1)


def perceiver(nc, A, resid, kvraw, ident, wts):
    D, S, H = P, 64, 16
    NT = A["x"].shape[0] // 2
    with ExitStack() as ctx:
        def sb(name, shape, dt=F32):
            return ctx.enter_context(nc.sbuf_tensor(name, shape, dt))

        def sem(name):
            return ctx.enter_context(nc.semaphore(name))

        st = sb("ln_stats", [P, 2, 6])
        mv = sb("ln_meanvar", [P, 2, 2])
        ve = sb("ln_vareps", [P, 2])
        rstd = sb("ln_rstd", [P, 2])
        mhalf = sb("minus_half", [P, 2])
        kn = sb("kv_normed", [P, 2, D])
        kg = sb("kv_gained", [P, 2, D])
        kvf = sb("kv_full", [P, 2, 2, D])
        kvh = [sb(f"kv_hi{i}", [P, 2, D], FR) for i in range(2)]
        kvl = [sb(f"kv_lo{i}", [P, 2, D], FR) for i in range(2)]
        kvT = [sb(f"kvT{i}", [P, 2, P]) for i in range(2)]
        q = [sb(f"q{i}", [P, 2, H, S]) for i in range(2)]
        nmax = [sb(f"neg_max{i}", [P, 4]) for i in range(2)]
        zsum = [sb(f"exp_sum{i}", [P, 4]) for i in range(2)]
        rz = [sb(f"exp_rsum{i}", [P, 4]) for i in range(2)]
        pe_ = [sb(f"exp{i}", [P, 4, P]) for i in range(2)]
        pn = [sb(f"probs{i}", [P, 4, P]) for i in range(2)]
        pth = [sb(f"probsT_hi{i}", [P, 512], FR) for i in range(2)]
        ptl = [sb(f"probsT_lo{i}", [P, 512], FR) for i in range(2)]
        uT = [sb(f"uT{i}", [P, H, 2, S]) for i in range(2)]

        def pb(name):
            return ctx.enter_context(nc.psum_tensor(name, [P, 512], F32))
        sbank, tbank, ubank = ([pb(f"{n}{i}") for i in range(2)] for n in ("ps_s", "ps_t", "ps_u"))
        qbank, mbank = pb("ps_q"), pb("ps_m")

        s_half = sem("s_half")
        s_ln = sem("s_ln")
        s_rs = sem("s_rs")
        s_kv = sem("s_kv")
        s_kvt = sem("s_kvt")
        s_ktc = sem("s_ktc")
        s_kvl = sem("s_kvl")
        s_q = sem("s_q")
        s_qc = sem("s_qc")
        s_s = sem("s_s")
        s_mx = sem("s_mx")
        s_e = sem("s_e")
        s_rz = sem("s_rz")
        s_pn = sem("s_pn")
        s_t = sem("s_t")
        s_th = sem("s_th")
        s_tl = sem("s_tl")
        s_u = sem("s_u")
        s_uc = sem("s_uc")
        s_y = sem("s_y")
        s_x = sem("s_x")

        def chunk(i, j):
            return at(i, j // 4), j % 4

        def parts(k):
            return k % 2, k // 2

        def tile_cols(tile, width):
            u, c = tile
            return slice(c * width, (c + 1) * width) if u is None else bass.ds(u * (2 * width) + c * width, width)

        LO, HI = 0, NT

        def on(tile):
            return live(tile, LO, HI)

        def schedule(clock, body):
            for i in range(-3, 4):
                body((None, i))
            with clock.eng.Fori(2, NT // 2 - 2) as u:
                clock.enter(u)
                body((u, 0))
                body((u, 1))
                clock.leave()
            for i in range(NT - 4, NT + 2):
                body((None, i))

        block = ctx.enter_context(nc.Block())

        @block.tensor
        def _(pe):
            c = Clock(pe, 2, KEYS["perceiver", "PE"])

            def body(i):
                for j in range(4):
                    tt, kt = chunk(i, j - 2)
                    if on(tt):
                        c.ge(s_pn, 4, tt, kt + 1)
                        c.ge(s_tl, 4, tt, kt - 1)
                        for b in range(4):
                            mm = nc.tensor.transpose(tbank[kt % 2][:, b * P:(b + 1) * P], pn[kt % 2][:, b, :], ident[:])
                        mm.then_inc(s_t, 1)
                    if on(i):
                        b, g = parts(j)
                        r = i[1] % 2
                        c.ge(s_qc, 4, i, 2 * g + 2)
                        c.ge(s_e, 4, i, j - 1)
                        for k in range(4):
                            h = 8 * g + 2 * k
                            out = sbank[j % 2][:, k * P:(k + 1) * P]
                            mm = nc.tensor.matmul(out, q[r][:, b, h:h + 2, :], kvT[r][:, b, :], start=True, stop=True)
                        mm.then_inc(s_s, 1)
                    tu, ku = chunk(i, j - 3)
                    if on(tu):
                        b, g = parts(ku)
                        r = tu[1] % 2
                        c.ge(s_kvl, 2, tu, 2)
                        c.ge(s_tl, 4, tu, ku + 1)
                        c.ge(s_uc, 4, tu, ku - 1)
                        out = ubank[ku % 2][:]
                        nc.tensor.matmul(out, kvh[r][:, b, :], pth[ku % 2][:], start=True, stop=False)
                        nc.tensor.matmul(out, kvh[r][:, b, :], ptl[ku % 2][:], start=False, stop=False)
                        nc.tensor.matmul(out, kvl[r][:, b, :], pth[ku % 2][:], start=False, stop=True).then_inc(s_u, 1)
                    tq = at(i, 1)
                    if on(tq):
                        r = tq[1] % 2
                        c.ge(s_ktc, 1, tq, 1)
                        c.ge(s_qc, 4, tq, j)
                        for k in range(4):
                            h = 4 * j + k
                            out = qbank[:, k * P:(k + 1) * P]
                            mm = nc.tensor.matmul(out, wts["A"][:, h * P:(h + 1) * P], kvT[r][:, :, S:2 * S],
                                                  start=True, stop=True)
                        mm.then_inc(s_q, 1)
                    ty = at(i, -2)
                    if j < 2 and on(ty):
                        r = ty[1] % 2
                        if j == 0:
                            c.ge(s_uc, 4, ty, 4)
                            c.ge(s_x, 1, ty, 0)
                            if live(i, -3, NT - 1):
                                c.ge(s_ktc, 1, ty, 4)
                        for h in range(j * H // 2, (j + 1) * H // 2):
                            out = mbank[:, 0:D]
                            mm = nc.tensor.matmul(out, uT[r][:, h, :, :], wts["V"][:, h * P:(h + 1) * P],
                                                  start=(h == 0), stop=(h == H - 1))
                        if j == 1:
                            mm.then_inc(s_y, 1)
                    tk = at(i, 2)
                    if j == 2 and on(tk):
                        c.ge(s_kv, 2, tk, 2)
                        c.ge(s_x, 1, tk, -3)
                        for b in range(2):
                            mm = nc.tensor.transpose(mbank[:, b * P:(b + 1) * P], kvf[:, tk[1] % 2, b, :], ident[:])
                        mm.then_inc(s_kvt, 1)
            schedule(c, body)

        @block.scalar
        def _(act):
            c = Clock(act, 2, KEYS["perceiver", "ACT"])

            def body(i):
                for j in range(4):
                    tk = at(i, 2)
                    if j == 3 and on(tk):
                        c.ge(s_kvt, 1, tk, 1)
                        c.ge(s_s, 4, tk, -4)
                        nc.scalar.activation(kvT[tk[1] % 2][:], mbank[:, 0:2 * P].rearrange("p (b k) -> p b k", b=2),
                                             ACT.Copy).then_inc(s_ktc, 1)
                    tt, kt = chunk(i, j - 2)
                    if on(tt):
                        c.ge(s_t, 4, tt, kt + 1)
                        c.ge(s_u, 4, tt, kt - 1)
                        nc.scalar.activation(pth[kt % 2][:], tbank[kt % 2][:], ACT.Copy).then_inc(s_th, 1)
                    if on(i):
                        c.ge(s_mx, 4, i, j + 1)
                        c.ge(s_pn, 4, i, j - 1)
                        for k in range(4):
                            e = nc.scalar.activation(pe_[j % 2][:, k, :], sbank[j % 2][:, k * P:(k + 1) * P], ACT.Exp,
                                                     bias=nmax[j % 2][:, k:k + 1], scale=-1.0,
                                                     accum_out=zsum[j % 2][:, k:k + 1])
                        e.then_inc(s_e, 1)
                    tu, ku = chunk(i, j - 3)
                    if on(tu):
                        b, g = parts(ku)
                        c.ge(s_u, 4, tu, ku + 1)
                        c.ge(s_y, 1, tu, -1)
                        nc.scalar.activation(uT[tu[1] % 2][:, 8 * g:8 * g + 8, b, :],
                                             ubank[ku % 2][:].rearrange("p (h s) -> p h s", s=S),
                                             ACT.Copy).then_inc(s_uc, 1)
            schedule(c, body)

        @block.vector
        def _(dve):
            c = Clock(dve, 2, KEYS["perceiver", "DVE"])

            def body(i):
                for j in range(4):
                    if on(i):
                        c.ge(s_s, 4, i, j + 1)
                        c.ge(s_e, 4, i, j - 1)
                        nc.vector.tensor_reduce(nmax[j % 2][:], sbank[j % 2][:].rearrange("p (a b) -> p a b", a=4),
                                                AX, ALU.min).then_inc(s_mx, 1)
                    tk = at(i, 2)
                    tr, kr = chunk(i, j - 1)
                    if on(tr):
                        c.ge(s_e, 4, tr, kr + 1)
                        c.ge(s_pn, 4, tr, kr - 1)
                        nc.vector.reciprocal(rz[kr % 2][:], zsum[kr % 2][:]).then_inc(s_rz, 1)
                    tt, kt = chunk(i, j - 2)
                    if on(tt):
                        c.ge(s_th, 4, tt, kt + 1)
                        nc.vector.tensor_tensor(ptl[kt % 2][:], tbank[kt % 2][:], pth[kt % 2][:].bitcast(F32),
                                                ALU.subtract).then_inc(s_tl, 1)
                    tq = at(i, 1)
                    if on(tq):
                        c.ge(s_q, 4, tq, j + 1)
                        nc.vector.tensor_copy(q[tq[1] % 2][:, :, 4 * j:4 * j + 4, :],
                                              qbank[:].rearrange("p (h b s) -> p b h s", h=4, b=2)).then_inc(s_qc, 1)
                    ty = at(i, -2)
                    if j == 2 and on(ty):
                        cols = tile_cols(ty, D)
                        c.ge(s_y, 1, ty, 1)
                        nc.vector.tensor_tensor(resid[:, cols], mbank[:, 0:D], resid[:, cols], ALU.add).then_inc(s_x, 1)
                    tl = at(i, 3)
                    if on(tl) and j == 0:
                        cols = tile_cols(tl, 2 * D)
                        raw = kvraw[:, cols].rearrange("p (b d) -> p b d", b=2)
                        for b in range(2):
                            nc.vector.bn_stats(st[:, b, :], raw[:, b, :]).then_inc(s_ln, 1)
                        c.ge(s_ln, 12, tl, 2, alone=True)
                        for b in range(2):
                            nc.vector.bn_aggr(mv[:, b, :], st[:, b, :]).then_inc(s_ln, 1)
                    if on(tl) and j == 2:
                        cols = tile_cols(tl, 2 * D)
                        raw = kvraw[:, cols].rearrange("p (b d) -> p b d", b=2)
                        c.ge(s_ln, 12, tl, 4)
                        c.ge(s_rs, 4, tl, 2)
                        c.ge(s_kv, 2, tl, 0)
                        for b in range(2):
                            nc.vector.tensor_scalar(kn[:, b, :], raw[:, b, :], mv[:, b, 0:1], rstd[:, b:b + 1],
                                                    ALU.subtract, ALU.mult).then_inc(s_ln, 1)
                        c.ge(s_ln, 12, tl, 6)
                        for b in range(2):
                            nc.vector.bn_stats(st[S:P, b, :], kn[S:P, b, :]).then_inc(s_ln, 1)
                        c.ge(s_ln, 12, tl, 8, alone=True)
                        for b in range(2):
                            nc.vector.bn_aggr(mv[S:P, b, :], st[S:P, b, :]).then_inc(s_ln, 1)
                    if on(tl) and j == 3:
                        c.ge(s_ln, 12, tl, 10)
                        c.ge(s_rs, 4, tl, 4)
                        for b in range(2):
                            nc.vector.tensor_scalar(kn[S:P, b, :], kn[S:P, b, :], mv[S:P, b, 0:1], rstd[S:P, b:b + 1],
                                                    ALU.subtract, ALU.mult).then_inc(s_ln, 1)
            schedule(c, body)

        @block.gpsimd
        def _(pool):
            c = Clock(pool, 2, KEYS["perceiver", "Pool"])
            nc.gpsimd.memset(mhalf[:], -0.5).then_inc(s_half, 1)
            pool.wait_ge(s_half, 1)

            def body(i):
                for j in range(4):
                    tn, kn_ = chunk(i, j - 1)
                    if on(tn):
                        c.ge(s_rz, 4, tn, kn_ + 1)
                        c.ge(s_t, 4, tn, kn_ - 1)
                        nc.gpsimd.tensor_tensor(pn[kn_ % 2][:], pe_[kn_ % 2][:],
                                                rz[kn_ % 2][:].unsqueeze(2).to_broadcast((P, 4, P)),
                                                ALU.mult).then_inc(s_pn, 1)
                    tl = at(i, 3)
                    if on(tl) and j == 0:
                        c.ge(s_ln, 12, tl, 4, alone=True)
                        nc.gpsimd.tensor_scalar(ve[:], mv[:, :, 1], EPS, None, ALU.add).then_inc(s_rs, 1)
                        c.ge(s_rs, 4, tl, 1)
                        nc.gpsimd.tensor_tensor(rstd[:], ve[:], mhalf[:], ALU.pow).then_inc(s_rs, 1)
                    if on(tl) and j == 2:
                        c.ge(s_ln, 12, tl, 10, alone=True)
                        nc.gpsimd.tensor_scalar(ve[:], mv[:, :, 1], EPS, None, ALU.add).then_inc(s_rs, 1)
                        c.ge(s_rs, 4, tl, 3)
                        nc.gpsimd.tensor_tensor(rstd[:], ve[:], mhalf[:], ALU.pow).then_inc(s_rs, 1)
                    tk = at(i, 2)
                    if on(tk) and j == 0:
                        c.ge(s_ln, 12, tk, 12)
                        nc.gpsimd.tensor_tensor(kg[:], kn[:], wts["gain"][:].unsqueeze(1).to_broadcast((P, 2, D)),
                                                ALU.mult).then_inc(s_kv, 1)
                        c.ge(s_kv, 2, tk, 1)
                        c.ge(s_kvl, 2, tk, -2)
                        c.ge(s_kvt, 1, tk, -1)
                        nc.gpsimd.tensor_tensor(kvf[:, tk[1] % 2], kg[:], wts["shift"][:].unsqueeze(1).to_broadcast((P, 2, D)),
                                                ALU.add).then_inc(s_kv, 1)
                    tq = at(i, 1)
                    if j == 3 and on(tq):
                        r = tq[1] % 2
                        c.ge(s_kv, 2, tq, 2)
                        c.ge(s_u, 4, tq, -4, alone=True)
                        nc.gpsimd.tensor_copy(kvh[r][:], kvf[:, r]).then_inc(s_kvl, 1)
                        c.ge(s_kvl, 2, tq, 1)
                        nc.gpsimd.tensor_tensor(kvl[r][:], kvf[:, r], kvh[r][:].bitcast(F32),
                                                ALU.subtract).then_inc(s_kvl, 1)
            schedule(c, body)


def norm_and_score(nc, tag, resid, ident, score_src, E, z, logits, split=None, after=None):
    D = P
    NG = resid.shape[1] // (4 * D)
    with ExitStack() as ctx:
        def sb(name, shape, dt=F32):
            return ctx.enter_context(nc.sbuf_tensor(tag + name, shape, dt))

        def sem(name):
            return ctx.enter_context(nc.semaphore(tag + name))

        w = sb("w_score", [P, E])
        st = [sb(f"st{i}", [P, 4, 6]) for i in range(2)]
        mv = [sb(f"mv{i}", [P, 4, 2]) for i in range(2)]
        ve = [sb(f"ve{i}", [P, 4]) for i in range(2)]
        rstd = [sb(f"rstd{i}", [P, 4]) for i in range(2)]
        mhalf = sb("mhalf", [P, 4])
        zT = [sb(f"zT{i}", [P, 512]) for i in range(2)]
        tb = [ctx.enter_context(nc.psum_tensor(tag + f"tb{i}", [P, 512], F32)) for i in range(2)]
        lb = [ctx.enter_context(nc.psum_tensor(tag + f"lb{i}", [P, 512], F32)) for i in range(2)]
        s_w = sem("s_w")
        s_half = sem("s_half")
        s_ln = sem("s_ln")
        s_rs = sem("s_rs")
        s_t = sem("s_t")
        s_tc = sem("s_tc")
        s_lo = sem("s_lo")
        s_l = sem("s_l")
        s_lc = sem("s_lc")
        x3 = resid[:].rearrange("p (t d) -> p t d", d=D)
        z3 = z[:].rearrange("p (t d) -> p t d", d=D)
        block = ctx.enter_context(nc.Block())

        @block.sync
        def _(sp):
            if score_src.shape[1] == E:
                sp.dma_start(w[:], score_src).then_inc(s_w, 16)
            else:
                with nc.allow_non_contiguous_dma(reason="the small scoring matrix, transposed once"):
                    sp.dma_start(w[:], score_src.rearrange("e d -> d e")).then_inc(s_w, 16)

        @block.gpsimd
        def _(pool):
            nc.gpsimd.memset(mhalf[:], -0.5).then_inc(s_half, 1)
            pool.wait_ge(s_half, 1)
            for g in range(NG):
                pool.wait_ge(s_ln, 12 * g + 4 if g else 8)
                nc.gpsimd.tensor_scalar(ve[g % 2][:], mv[g % 2][:, :, 1], EPS, None, ALU.add).then_inc(s_rs, 1)
                pool.wait_ge(s_rs, 2 * g + 1)
                nc.gpsimd.tensor_tensor(rstd[g % 2][:], ve[g % 2][:], mhalf[:], ALU.pow).then_inc(s_rs, 1)

        @block.vector
        def _(dve):
            def stats(g):
                base = 0 if g == 0 else 12 * g - 4
                for k in range(4):
                    nc.vector.bn_stats(st[g % 2][:, k, :], x3[:, 4 * g + k, :]).then_inc(s_ln, 1)
                dve.wait_ge(s_ln, base + 4)
                for k in range(4):
                    nc.vector.bn_aggr(mv[g % 2][:, k, :], st[g % 2][:, k, :]).then_inc(s_ln, 1)

            def lo(g):
                dve.wait_ge(s_tc, 2 * g + 2)
                hi, low = (s[:, g * 512:(g + 1) * 512] for s in split)
                nc.vector.tensor_tensor(low, tb[g % 2][:], hi.bitcast(F32), ALU.subtract).then_inc(s_lo, 1)

            stats(0)
            for g in range(NG):
                if g + 1 < NG:
                    stats(g + 1)
                dve.wait_ge(s_rs, 2 * g + 2)
                for k in range(4):
                    nc.vector.tensor_scalar(z3[:, 4 * g + k, :], x3[:, 4 * g + k, :], mv[g % 2][:, k, 0:1],
                                            rstd[g % 2][:, k:k + 1], ALU.subtract, ALU.mult).then_inc(s_ln, 1)
                if split and g >= 1:
                    lo(g - 1)
            if split:
                lo(NG - 1)

        def normed(g):
            return 12 * (g + 2) - 4 if g + 1 < NG else 12 * NG

        @block.tensor
        def _(pe):
            def score(g):
                if g == 0:
                    pe.wait_ge(s_w, 16)
                pe.wait_ge(s_tc, (2 if split else 1) * g + 1)
                if g >= 2:
                    pe.wait_ge(s_lc, g - 1)
                for k in range(4):
                    mm = nc.tensor.matmul(lb[g % 2][:, k * E:(k + 1) * E], zT[g % 2][:, k * P:(k + 1) * P], w[:],
                                          start=True, stop=True)
                mm.then_inc(s_l, 1)

            for g in range(NG):
                pe.wait_ge(s_ln, normed(g))
                if g >= 2:
                    pe.wait_ge(s_lo if split else s_tc, g - 1)
                for k in range(4):
                    mm = nc.tensor.transpose(tb[g % 2][:, k * P:(k + 1) * P], z3[:, 4 * g + k, :], ident[:])
                mm.then_inc(s_t, 1)
                if g >= 1:
                    score(g - 1)
            score(NG - 1)

        @block.scalar
        def _(act):
            def out(g):
                act.wait_ge(s_l, g + 1)
                nc.scalar.activation(logits[:, g * 4 * E:(g + 1) * 4 * E], lb[g % 2][:, 0:4 * E],
                                     ACT.Copy).then_inc(s_lc, 1)

            for g in range(NG):
                act.wait_ge(s_t, g + 1)
                if g >= 2:
                    act.wait_ge(s_l, g - 1)
                nc.scalar.activation(zT[g % 2][:], tb[g % 2][:], ACT.Copy).then_inc(s_tc, 1)
                if split:
                    nc.scalar.activation(split[0][:, g * 512:(g + 1) * 512], tb[g % 2][:], ACT.Copy).then_inc(s_tc, 1)
                if g >= 1:
                    out(g - 1)
            out(NG - 1)


def softmax_rows(nc, tag, logits, E, NTL):
    with ExitStack() as ctx:
        mx = ctx.enter_context(nc.sbuf_tensor(tag + "mx", [P, NTL], F32))
        sm = ctx.enter_context(nc.sbuf_tensor(tag + "sm", [P, NTL], F32))
        rs = ctx.enter_context(nc.sbuf_tensor(tag + "rs", [P, NTL], F32))
        s_v = ctx.enter_context(nc.semaphore(tag + "s_v"))
        s_a = ctx.enter_context(nc.semaphore(tag + "s_a"))
        lg = logits[:].rearrange("p (t e) -> p t e", e=E)
        block = ctx.enter_context(nc.Block())

        @block.vector
        def _(dve):
            nc.vector.tensor_reduce(mx[:], lg, AX, ALU.max).then_inc(s_v, 1)
            dve.wait_ge(s_v, 1)
            nc.vector.tensor_tensor(lg, lg, mx[:].unsqueeze(2).to_broadcast((P, NTL, E)), ALU.subtract).then_inc(s_v, 1)
            dve.wait_ge(s_a, 1)
            nc.vector.tensor_reduce(sm[:], lg, AX, ALU.add).then_inc(s_v, 1)
            dve.wait_ge(s_v, 3)
            nc.vector.reciprocal(rs[:], sm[:]).then_inc(s_v, 1)
            dve.wait_ge(s_v, 4)
            nc.vector.tensor_tensor(lg, lg, rs[:].unsqueeze(2).to_broadcast((P, NTL, E)), ALU.mult).then_inc(s_v, 1)

        @block.scalar
        def _(act):
            act.wait_ge(s_v, 2)
            nc.scalar.activation(logits[:], logits[:], ACT.Exp).then_inc(s_a, 1)



def choose_tokens(nc, tag, ident, probs, cw):
    S, K = 64, 16
    with ExitStack() as ctx:
        def sb(name, shape, dt=F32):
            return ctx.enter_context(nc.sbuf_tensor(tag + name, shape, dt))

        def sem(name):
            return ctx.enter_context(nc.semaphore(tag + name))
        pT = sb("pT", [P, 4, S])
        w = [sb(f"left{i}", [P, 4, S]) for i in range(2)]
        m8 = [sb(f"best{i}", [P, 4, 8]) for i in range(2)]
        tb = [ctx.enter_context(nc.psum_tensor(tag + f"tb{i}", [P, 512], F32)) for i in range(2)]
        s_pt = sem("s_pt")
        s_ptc = sem("s_ptc")
        s_v = sem("s_v")
        s_ct = sem("s_ct")
        block = ctx.enter_context(nc.Block())

        @block.tensor
        def _(pe):
            for g in range(2):
                mm = nc.tensor.transpose(tb[0][:, g * P:(g + 1) * P], probs[:, g * P:(g + 1) * P], ident[:])
            mm.then_inc(s_pt, 1)
            pe.wait_ge(s_v, 18)
            for g in range(2):
                mm = nc.tensor.transpose(tb[1][:, g * P:(g + 1) * P], w[0][:, 2 * g:2 * g + 2, :], ident[:])
            mm.then_inc(s_ct, 1)

        @block.scalar
        def _(act):
            act.wait_ge(s_pt, 1)
            nc.scalar.activation(pT[:], tb[0][:, 0:2 * P].rearrange("p (c s) -> p c s", c=4), ACT.Copy).then_inc(s_ptc, 1)
            act.wait_ge(s_ct, 1)
            nc.scalar.activation(cw[:], tb[1][:, 0:2 * P], ACT.Copy)

        @block.vector
        def _(dve):
            dve.wait_ge(s_ptc, 1)
            src = pT
            for r in range(K // 8):
                for c in range(4):
                    nc.vector.max(m8[r][:, c, :], src[:, c, :]).then_inc(s_v, 1)
                dve.wait_ge(s_v, 8 * r + 4)
                for c in range(4):
                    nc.vector.match_replace(w[r][:, c, :], m8[r][:, c, :], src[:, c, :], -1.0).then_inc(s_v, 1)
                dve.wait_ge(s_v, 8 * r + 8)
                src = w[r]
            nc.vector.tensor_scalar(w[1][:], w[1][:], -1.0, None, ALU.is_equal).then_inc(s_v, 1)
            dve.wait_ge(s_v, 17)
            nc.vector.tensor_tensor(w[0][:], w[1][:], pT[:], ALU.mult).then_inc(s_v, 1)


def choose_experts(nc, tag, ident, probs, cw):
    E, K = 16, 2
    NT = probs.shape[1] // E
    with ExitStack() as ctx:
        m8 = ctx.enter_context(nc.sbuf_tensor(tag + "best", [P, NT, 8], F32))
        left = ctx.enter_context(nc.sbuf_tensor(tag + "left", [P, NT, E], F32))
        s_v = ctx.enter_context(nc.semaphore(tag + "s_v"))
        pr = probs[:].rearrange("p (t e) -> p t e", e=E)
        block = ctx.enter_context(nc.Block())

        @block.vector
        def _(dve):
            for t in range(NT):
                nc.vector.max(m8[:, t, :], pr[:, t, :]).then_inc(s_v, 1)
            dve.wait_ge(s_v, NT)
            nc.vector.memset(m8[:, :, K:8], -5.0).then_inc(s_v, 1)
            dve.wait_ge(s_v, NT + 1)
            for t in range(NT):
                nc.vector.match_replace(left[:, t, :], m8[:, t, :], pr[:, t, :], -1.0).then_inc(s_v, 1)
            dve.wait_ge(s_v, 2 * NT + 1)
            nc.vector.tensor_scalar(left[:], left[:], -1.0, None, ALU.is_equal).then_inc(s_v, 1)
            dve.wait_ge(s_v, 2 * NT + 2)
            nc.vector.tensor_tensor(cw[:].rearrange("p (t e) -> p t e", e=E), left[:], pr, ALU.mult)


def transpose_weights(nc, tag, ident, cw, E, parts):
    NG = parts[0].shape[1] // 512
    hi, lo = parts
    with ExitStack() as ctx:
        tb = [ctx.enter_context(nc.psum_tensor(tag + f"wt{i}", [P, 512], F32)) for i in range(2)]
        s_t = ctx.enter_context(nc.semaphore(tag + "s_wt"))
        s_h = ctx.enter_context(nc.semaphore(tag + "s_wh"))
        s_l = ctx.enter_context(nc.semaphore(tag + "s_wl"))
        block = ctx.enter_context(nc.Block())

        @block.tensor
        def _(pe):
            for g in range(NG):
                if g >= 2:
                    pe.wait_ge(s_l, g - 1)
                for k in range(4):
                    t = 4 * g + k
                    mm = nc.tensor.transpose(tb[g % 2][0:E, k * P:(k + 1) * P], cw[:, t * E:(t + 1) * E], ident[:])
                mm.then_inc(s_t, 1)

        @block.scalar
        def _(act):
            for g in range(NG):
                act.wait_ge(s_t, g + 1)
                nc.scalar.activation(hi[:, g * 512:(g + 1) * 512], tb[g % 2][0:E, :], ACT.Copy).then_inc(s_h, 1)

        @block.vector
        def _(dve):
            for g in range(NG):
                dve.wait_ge(s_h, g + 1)
                cols = slice(g * 512, (g + 1) * 512)
                nc.vector.tensor_tensor(lo[:, cols], tb[g % 2][0:E, :], hi[:, cols].bitcast(F32),
                                        ALU.subtract).then_inc(s_l, 1)


def experts(nc, tag, resid, ident, zT, cwT, E, up_src, down_src, shared):
    D, NG = P, zT[0].shape[1] // 512
    F = up_src[0].shape[2]
    gated = len(up_src) == 2
    steps = E * F // P + (1 if shared else 0)
    G = 2 if steps % 2 else 1
    SU = G * steps
    NU = NG // G
    LAG, RING = (2, 2) if gated else (3, 4)
    with ExitStack() as ctx:
        def sb(name, shape, dt=F32):
            return ctx.enter_context(nc.sbuf_tensor(tag + name, shape, dt))

        def sem(name):
            return ctx.enter_context(nc.semaphore(tag + name))

        def pb(name):
            return ctx.enter_context(nc.psum_tensor(tag + name, [P, 512], F32))

        sel = sb("sel", [E, E * F], FR)
        ups = [[sb(f"up{i}_hi", [P, steps * P], FR), sb(f"up{i}_lo", [P, steps * P], FR)] for i in range(len(up_src))]
        down = [sb("down_hi", [P, steps * P], FR), sb("down_lo", [P, steps * P], FR)]
        with ExitStack() as c2:
            raw = [c2.enter_context(nc.sbuf_tensor(tag + f"raw{i}", [P, steps * P], F32)) for i in range(len(up_src) + 1)]
            self_ = c2.enter_context(nc.sbuf_tensor(tag + "sel32", [E, E, F], F32))
            s_w = c2.enter_context(nc.semaphore(tag + "s_w"))
            s_hi = c2.enter_context(nc.semaphore(tag + "s_hi"))
            s_sel = c2.enter_context(nc.semaphore(tag + "s_sel"))
            block = c2.enter_context(nc.Block())

            @block.sync
            def _(sp):
                for r, src in zip(raw[:-1], up_src):
                    sp.dma_start(r[:, 0:E * F].rearrange("p (e f) -> p e f", f=F), src).then_inc(s_w, 16)
                sp.dma_start(raw[-1][:, 0:E * F].rearrange("p (s d) -> p s d", d=P), down_src).then_inc(s_w, 16)
                for r, src in zip(raw, shared or ()):
                    sp.dma_start(r[:, E * F:], src).then_inc(s_w, 16)

            @block.scalar
            def _(act):
                act.wait_ge(s_w, 16 * (len(raw) * (2 if shared else 1)))
                for r, (hi, _) in zip(raw, ups + [down]):
                    nc.scalar.activation(hi[:], r[:], ACT.Copy).then_inc(s_hi, 1)
                act.wait_ge(s_sel, 2)
                nc.scalar.activation(sel[:].rearrange("p (e f) -> p e f", f=F), self_[:], ACT.Copy)

            @block.vector
            def _(dve):
                for n, (r, (hi, lo)) in enumerate(zip(raw, ups + [down])):
                    dve.wait_ge(s_hi, n + 1)
                    nc.vector.tensor_tensor(lo[:], r[:], hi[:].bitcast(F32), ALU.subtract)

            @block.gpsimd
            def _(pool):
                nc.gpsimd.memset(self_[:], 0.0).then_inc(s_sel, 1)
                pool.wait_ge(s_sel, 1)
                nc.gpsimd.affine_select(out=self_[:], in_=self_[:], compare_op=ALU.not_equal, fill=1.0, base=0,
                                        pattern=[[-1, E], [0, F]], channel_multiplier=1).then_inc(s_sel, 1)

        act_out = [sb(f"silu{i}", [P, 512]) for i in range(2)]
        prod = [sb(f"prod{i}", [P, 512]) for i in range(2)]
        hid = [sb(f"hid{i}", [P, 512]) for i in range(2)]
        hh = [sb(f"hid_hi{i}", [P, 512], FR) for i in range(RING)]
        hl = [sb(f"hid_lo{i}", [P, 512], FR) for i in range(RING)]
        yT = sb("yT", [P, 512])
        gb = [pb(f"gate{i}") for i in range(2)]
        ub = [pb(f"up{i}") for i in range(2)] if gated else None
        cb = [pb(f"weight{i}") for i in range(2)]
        yb, tb = pb("y"), pb("t")
        s_g = sem("s_g")
        s_ucp = sem("s_up")
        s_si = sem("s_si")
        s_pr = sem("s_pr")
        s_hd = sem("s_hd")
        s_hi = sem("s_hi2")
        s_lo = sem("s_lo2")
        s_d = sem("s_d")
        s_yc = sem("s_yc")
        s_t = sem("s_yt")
        s_x = sem("s_x")

        def group_of(tile, s):
            u, c = tile
            k = s // steps
            return slice((c * G + k) * 512, (c * G + k + 1) * 512) if u is None else \
                bass.ds(u * (G * 512) + (c * G + k) * 512, 512)

        def norm(tile, s):
            return at(tile, s // SU), s % SU

        def on(tile):
            return live(tile, 0, NU)

        def schedule(clock, body):
            body((None, 0))
            with clock.eng.Fori(1, NU) as u:
                clock.enter(u)
                body((u, 0))
                clock.leave()
            body((None, NU))

        TLAG = 2
        AFTER = LAG + TLAG
        block = ctx.enter_context(nc.Block())

        @block.tensor
        def _(pe):
            c = Clock(pe, 1, {SU: range(-8, SU + 3), G: range(-3, G + 2)})

            def body(i):
                for s in range(SU):
                    if on(i):
                        cols = group_of(i, s)
                        m = s % steps
                        r = s % 2
                        w = slice(m * P, (m + 1) * P)
                        weighted = not (shared and m == steps - 1)
                        c.ge(s_si, SU, i, s - 1)
                        for b, (wp, zp) in enumerate(((0, 0), (0, 1), (1, 0))):
                            mm = nc.tensor.matmul(gb[r][:], ups[0][wp][:, w], zT[zp][:, cols], start=(b == 0), stop=(b == 2))
                        mm.then_inc(s_g, 1)
                        c.ge(s_hd, SU, i, s - 1, alone=not gated)
                        if gated:
                            for b, (wp, zp) in enumerate(((0, 0), (0, 1), (1, 0))):
                                mm = nc.tensor.matmul(ub[r][:], ups[1][wp][:, w], zT[zp][:, cols], start=(b == 0), stop=(b == 2))
                        if weighted:
                            for b in range(2):
                                mm = nc.tensor.matmul(cb[r][:], sel[:, w], cwT[b][:, cols], start=(b == 0), stop=(b == 1))
                        mm.then_inc(s_ucp, 1)
                    td, kd = norm(i, s - LAG)
                    if on(td):
                        m = kd % steps
                        w = slice(m * P, (m + 1) * P)
                        c.ge(s_lo, SU, td, kd + 1)
                        if m == 0:
                            c.ge(s_yc, G, td, kd // steps)
                        for b, (wp, h) in enumerate(((0, hh), (0, hl), (1, hh))):
                            mm = nc.tensor.matmul(yb[:], down[wp][:, w], h[kd % RING][:], start=(m == 0 and b == 0),
                                                  stop=(m == steps - 1 and b == 2))
                        mm.then_inc(s_d, 1)
                    ty, ky = norm(i, s - AFTER)
                    if on(ty) and ky % steps == steps - 1:
                        k = ky // steps
                        c.ge(s_yc, G, ty, k + 1)
                        c.ge(s_x, G, ty, k)
                        for b in range(4):
                            mm = nc.tensor.transpose(tb[:, b * P:(b + 1) * P], yT[:, b * P:(b + 1) * P], ident[:])
                        mm.then_inc(s_t, 1)
                    if not on(i) and i[1] == NU and s >= AFTER:
                        break
            schedule(c, body)

        @block.scalar
        def _(act):
            c = Clock(act, 1, {SU: range(-8, SU + 3), G: range(-3, G + 2)})

            def body(i):
                for s in range(SU):
                    if on(i):
                        c.ge(s_g, SU, i, s + 1)
                        c.ge(s_hd, SU, i, s - 1)
                        nc.scalar.activation(act_out[s % 2][:], gb[s % 2][:], ACT.Silu).then_inc(s_si, 1)
                    th, kh = norm(i, s - 1)
                    if on(th):
                        c.ge(s_hd, SU, th, kh + 1)
                        c.ge(s_d, SU, th, kh + 1 - RING)
                        nc.scalar.activation(hh[kh % RING][:], hid[kh % 2][:], ACT.Copy).then_inc(s_hi, 1)
                    ty, ky = norm(i, s - LAG)
                    if on(ty) and ky % steps == steps - 1:
                        c.ge(s_d, SU, ty, ky + 1)
                        c.ge(s_t, G, ty, ky // steps)
                        nc.scalar.activation(yT[:], yb[:], ACT.Copy).then_inc(s_yc, 1)
            schedule(c, body)

        @block.vector
        def _(dve):
            c = Clock(dve, 1, {SU: range(-8, SU + 3), G: range(-3, G + 2)})

            def body(i):
                for s in range(SU):
                    if on(i):
                        r = s % 2
                        weighted = not (shared and s % steps == steps - 1)
                        c.ge(s_si, SU, i, s + 1)
                        c.ge(s_ucp, SU, i, s + 1)
                        c.ge(s_lo, SU, i, s - 1)
                        first = hid[r] if not weighted else prod[r]
                        if gated:
                            mm = nc.vector.tensor_tensor(first[:], ub[r][:], act_out[r][:], ALU.mult)
                            if weighted:
                                mm.then_inc(s_pr, 1)
                                c.ge(s_pr, G * (steps - 1), i, s + 1 - s // steps)
                        if weighted:
                            src = prod[r] if gated else act_out[r]
                            mm = nc.vector.tensor_tensor(hid[r][:], cb[r][:], src[:], ALU.mult)
                        mm.then_inc(s_hd, 1)
                    ty, ky = norm(i, s - AFTER)
                    if on(ty) and ky % steps == steps - 1:
                        c.ge(s_t, G, ty, ky // steps + 1)
                        cols = group_of(ty, ky)
                        nc.vector.tensor_tensor(resid[:, cols], tb[:], resid[:, cols], ALU.add).then_inc(s_x, 1)
            if gated and shared:
                c.keys[G * (steps - 1)] = range(1, G * (steps - 1) + 1)
            schedule(c, body)

        @block.gpsimd
        def _(pool):
            c = Clock(pool, 1, {SU: range(-8, SU + 3)})

            def body(i):
                for s in range(SU):
                    th, kh = norm(i, s - 1)
                    if on(th):
                        c.ge(s_hi, SU, th, kh + 1)
                        nc.gpsimd.tensor_tensor(hl[kh % RING][:], hid[kh % 2][:], hh[kh % RING][:].bitcast(F32),
                                                ALU.subtract).then_inc(s_lo, 1)
            schedule(c, body)


def mixture(nc, A, tag, resid, ident, score_src, E, choose, up_src, down_src, shared):
    NT = resid.shape[1] // P
    with ExitStack() as ctx:
        def sb(name, shape, dt=F32):
            return ctx.enter_context(nc.sbuf_tensor(tag + name, shape, dt))
        zT = [sb(f"zT_{n}", [P, NT * P], FR) for n in ("hi", "lo")]
        cwT = [sb(f"cwT_{n}", [E, NT * P], FR) for n in ("hi", "lo")]
        with ExitStack() as c2:
            def sb2(name, shape):
                return c2.enter_context(nc.sbuf_tensor(tag + name, shape, F32))
            z = sb2("z", [P, NT * P])
            logits = sb2("logits", [P, NT * E])
            cw = sb2("cw", [P, NT * E])
            norm_and_score(nc, tag + "ns_", resid, ident, score_src, E, z, logits, split=zT)
            softmax_rows(nc, tag + "sm_", logits, E, NT)
            choose(nc, tag + "ch_", ident, logits, cw)
            transpose_weights(nc, tag + "tw_", ident, cw, E, cwT)
        experts(nc, tag + "ex_", resid, ident, zT, cwT, E, up_src, down_src, shared)


def attention_constants(nc, A, ident, K):
    H, S = 16, 64
    DH = P // H
    with ExitStack() as ctx:
        def sb(name, shape, dt=F32):
            return ctx.enter_context(nc.sbuf_tensor("ac_" + name, shape, dt))

        def sem(name):
            return ctx.enter_context(nc.semaphore("ac_" + name))
        mask = sb("mask", [P, 64, S], I32)
        heads = sb("heads", [P, H])
        pairs = sb("pairs", [P, H // 2])
        bq, bk, wo = sb("bq", [P, 1]), sb("bk", [P, 1]), sb("wo", [P, P])
        s_mask = sem("s_mask")
        s_small = sem("s_small")
        s_in = sem("s_in")
        s_v = sem("s_v")
        block = ctx.enter_context(nc.Block())

        @block.sync
        def _(sp):
            with nc.allow_non_contiguous_dma(reason="one bias a partition"):
                sp.dma_start(bq[:], A["aq_b"].unsqueeze(1)).then_inc(s_small, 16)
                sp.dma_start(bk[:], A["ak_b"].unsqueeze(1)).then_inc(s_small, 16)
            sp.dma_start(wo[:], A["ao_w"]).then_inc(s_small, 16)
            for j in range(2):
                sp.dma_start(mask[j * S:(j + 1) * S], A["mask"].rearrange("b q k -> q b k")).then_inc(s_mask, 16)
            for j in range(2):
                sp.dma_start(K["gp"][j * S:(j + 1) * S], A["gp"].rearrange("b q k -> q b k")).then_inc(s_in, 16)
            sp.dma_start(K["ctx"][:], A["ctx"].rearrange("(t b) s d -> (b s) t d", b=2)).then_inc(s_in, 16)
            sp.dma_start(K["wq"][:], A["aq_w"]).then_inc(s_in, 16)
            sp.dma_start(K["wk"][:], A["ak_w"]).then_inc(s_in, 16)
            sp.dma_start(K["wv"][:], A["av_w"]).then_inc(s_in, 16)
            sp.dma_start(K["bv"][:], A["av_b"].partition_broadcast(P)).then_inc(s_in, 16)
            sp.dma_start(K["bo"][:], A["ao_b"].partition_broadcast(P)).then_inc(s_in, 16)
            sp.wait_ge(s_in, 8 * 16)

        @block.vector
        def _(dve):
            nc.vector.tensor_reduce(heads[:], ident[:].rearrange("p (h d) -> p h d", h=H), AX, ALU.add).then_inc(s_v, 1)
            dve.wait_ge(s_v, 1)
            nc.vector.tensor_reduce(K["jj"][:], heads[:].rearrange("p (a j) -> p j a", j=2), AX, ALU.add).then_inc(s_v, 1)
            nc.vector.tensor_reduce(pairs[:], heads[:].rearrange("p (a j) -> p a j", j=2), AX, ALU.add).then_inc(s_v, 1)
            dve.wait_ge(s_v, 3)
            nc.vector.tensor_reduce(K["jp"][:], pairs[:].rearrange("p (r j) -> p j r", j=2), AX, ALU.add).then_inc(s_v, 1)
            dve.wait_ge(s_small, 3 * 16)
            for j in range(2):
                nc.vector.tensor_scalar(K["wo"][:, j, :], wo[:], K["jj"][:, j:j + 1], None, ALU.mult)
            nc.vector.tensor_scalar(K["sq"][:], K["jj"][:], float(DH) ** -0.5, None, ALU.mult).then_inc(s_v, 1)
            dve.wait_ge(s_v, 5)
            nc.vector.tensor_scalar(K["bq"][:], K["sq"][:], bq[:], None, ALU.mult)
            nc.vector.tensor_scalar(K["bk"][:], K["jp"][:], bk[:], None, ALU.mult)
            for r in range(2):
                nc.vector.memset(K[f"vb{r}"][:], 0.0)
            dve.wait_ge(s_mask, 2 * 16)
            nc.vector.tensor_scalar(K["neg"][:], mask[:], -1.0, 1e9, ALU.add, ALU.mult)


def attention(nc, A, resid, ident, K):
    D, S, H = P, 64, 16
    NQ = resid.shape[1] // (2 * D)
    with ExitStack() as ctx:
        def sb(name, shape, dt=F32):
            return ctx.enter_context(nc.sbuf_tensor("at_" + name, shape, dt))

        def sem(name):
            return ctx.enter_context(nc.semaphore("at_" + name))

        def pb(name):
            return ctx.enter_context(nc.psum_tensor("at_" + name, [P, 512], F32))

        st, mv = sb("ln_stats", [P, 2, 6]), sb("ln_meanvar", [P, 2, 2])
        ve, rstd, mhalf = sb("ln_vareps", [P, 2]), sb("ln_rstd", [P, 2]), sb("minus_half", [P, 2])
        z = sb("z", [P, 2, D])
        cstage = sb("ctx_tiles", [P, 2, D])
        zT = sb("zT", [P, 256])
        ctxT = sb("ctxT", [P, 4, 2, S])
        qx = [sb(f"qx{i}", [P, 4, 2, S]) for i in range(2)]
        kx = [sb(f"kx{i}", [P, 4, 2, S]) for i in range(2)]
        vb = [K["vb0"], K["vb1"]]
        sm = [sb(f"scores{i}", [P, 4, 2, S]) for i in range(2)]
        mx = [sb(f"max{i}", [P, 4, 2]) for i in range(2)]
        ex = [sb(f"exp{i}", [P, 4, 2, S]) for i in range(2)]
        pg = [sb(f"probs{i}", [P, 4, 2, S]) for i in range(2)]
        pT = [sb(f"probsT{i}", [P, 512]) for i in range(2)]
        zs = [sb(f"exp_sum{i}", [P, 4, 4, 2]) for i in range(2)]
        rz = sb("exp_rsum", [P, 32])
        on = sb("out_normed", [P, 4, D])
        oT = sb("outT", [P, 2, 4, S])
        sbank, tbank = ([pb(f"{n}{i}") for i in range(2)] for n in ("ps_s", "ps_t"))
        obank, prep, qkbank, ybank = pb("ps_o"), pb("ps_prep"), pb("ps_qk"), pb("ps_y")

        s_half = sem("s_half")
        s_ln = sem("s_ln")
        s_rs = sem("s_rs")
        s_bo = sem("s_bo")
        s_cs = sem("s_cs")
        s_zt = sem("s_zt")
        s_ztc = sem("s_ztc")
        s_qk = sem("s_qk")
        s_qx = sem("s_qx")
        s_v = sem("s_v")
        s_vb = sem("s_vb")
        s_s = sem("s_s")
        s_ma = sem("s_ma")
        s_mx = sem("s_mx")
        s_sub = sem("s_sub")
        s_e = sem("s_e")
        s_sum = sem("s_sum")
        s_gp = sem("s_gp")
        s_t = sem("s_t")
        s_ptc = sem("s_ptc")
        s_pv = sem("s_pv")
        s_rz = sem("s_rz")
        s_on = sem("s_on")
        s_ot = sem("s_ot")
        s_otc = sem("s_otc")
        s_y = sem("s_y")
        s_x = sem("s_x")

        def step(i, j):
            return at(i, j // 4), j % 4

        def quad_cols(q, width):
            u, c = q
            return slice(c * width, (c + 1) * width) if u is None else bass.ds(u * (2 * width) + c * width, width)

        def quad_batches(q):
            u, c = q
            return slice(4 * c, 4 * c + 4) if u is None else bass.ds(u * 8 + 4 * c, 4)

        def ctx_tiles(q):
            u, c = q
            return slice(2 * c, 2 * c + 2) if u is None else bass.ds(u * 4 + 2 * c, 2)

        def on_(q):
            return live(q, 0, NQ)

        def schedule(clock, body):
            for i in range(-2, 4):
                body((None, i))
            with clock.eng.Fori(2, NQ // 2 - 1) as u:
                clock.enter(u)
                body((u, 0))
                body((u, 1))
                clock.leave()
            for i in range(NQ - 2, NQ + 2):
                body((None, i))

        block = ctx.enter_context(nc.Block())

        @block.tensor
        def _(pe):
            c = Clock(pe, 2, KEYS["attention", "PE"])

            def body(i):
                for j in range(4):
                    tt, kt = step(i, j - 2)
                    if on_(tt):
                        c.ge(s_gp, 4, tt, kt + 1)
                        c.ge(s_ptc, 4, tt, kt - 1)
                        for b in range(4):
                            mm = nc.tensor.transpose(tbank[kt % 2][:, b * P:(b + 1) * P], pg[kt % 2][:, b], ident[:])
                        mm.then_inc(s_t, 1)
                    if on_(i):
                        r = i[1] % 2
                        rows = slice(32 * j, 32 * j + 32)
                        if j == 0:
                            c.ge(s_qx, 4, i, 4)
                        c.ge(s_ma, 4, i, j - 1)
                        for b in range(4):
                            mm = nc.tensor.matmul(sbank[j % 2][:, b * P:(b + 1) * P], qx[r][rows, b], kx[r][rows, b],
                                                  start=True, stop=True)
                        mm.then_inc(s_s, 1)
                    ti = at(i, 1)
                    if j == 0 and on_(ti):
                        c.ge(s_ln, 6, ti, 6)
                        c.ge(s_vb, 2, ti, 0)
                        c.ge(s_cs, 1, ti, 1)
                        for t in range(2):
                            nc.tensor.transpose(prep[:, t * P:(t + 1) * P], z[:, t], ident[:])
                        for t in range(2):
                            mm = nc.tensor.transpose(prep[:, (2 + t) * P:(3 + t) * P], cstage[:, t], ident[:])
                        mm.then_inc(s_zt, 1)
                    if j == 1 and on_(ti):
                        c.ge(s_ztc, 1, ti, 1)
                        c.ge(s_qx, 4, ti, 0)
                        nc.tensor.matmul(qkbank[:, 0:256], K["wq"][:], zT[:], start=True, stop=True)
                        nc.tensor.matmul(qkbank[:, 256:512], K["wk"][:], ctxT[:, :, 0, :], start=True, stop=True).then_inc(s_qk, 1)
                    if j == 2 and on_(ti):
                        for b in range(4):
                            mm = nc.tensor.matmul(prep[:, b * P:(b + 1) * P], ctxT[:, b], K["wv"][:], start=True, stop=True)
                        mm.then_inc(s_v, 1)
                    tv, kv = step(i, j - 3)
                    if on_(tv):
                        c.ge(s_ptc, 4, tv, kv + 1)
                        if kv == 0:
                            c.ge(s_vb, 2, tv, 2)
                            c.ge(s_on, 1, tv, 0)
                        for b in range(4):
                            lo = b * P + 32 * kv
                            mm = nc.tensor.matmul(obank[:, lo:lo + 32], pT[kv % 2][:, b * P:(b + 1) * P],
                                                  vb[tv[1] % 2][:, b, 32 * kv:32 * kv + 32], start=True, stop=True)
                        mm.then_inc(s_pv, 1)
                    ty = at(i, -2)
                    if j == 0 and on_(ty):
                        c.ge(s_on, 1, ty, 1)
                        c.ge(s_x, 1, ty, 0)
                        for b in range(4):
                            mm = nc.tensor.transpose(ybank[:, b * P:(b + 1) * P], on[:, b], ident[:])
                        mm.then_inc(s_ot, 1)
                    if j == 1 and on_(ty):
                        c.ge(s_otc, 1, ty, 1)
                        for t in range(2):
                            for jj in range(2):
                                mm = nc.tensor.matmul(ybank[:, t * P:(t + 1) * P], oT[:, jj, 2 * t:2 * t + 2, :],
                                                      K["wo"][:, jj, :], start=(jj == 0), stop=(jj == 1))
                        mm.then_inc(s_y, 1)
            schedule(c, body)

        @block.scalar
        def _(act):
            c = Clock(act, 2, KEYS["attention", "ACT"])

            def body(i):
                for j in range(4):
                    tt, kt = step(i, j - 2)
                    if on_(tt):
                        c.ge(s_t, 4, tt, kt + 1)
                        c.ge(s_pv, 4, tt, kt - 1)
                        nc.scalar.activation(pT[kt % 2][:], tbank[kt % 2][:], ACT.Copy).then_inc(s_ptc, 1)
                    ti = at(i, 1)
                    if j == 0 and on_(ti):
                        c.ge(s_zt, 1, ti, 1)
                        c.ge(s_v, 1, ti, 0)
                        nc.scalar.activation(zT[:], prep[:, 0:256], ACT.Copy)
                        nc.scalar.activation(ctxT[:], prep[:, 256:512].rearrange("p (b s) -> p b s", b=4).unsqueeze(2)
                                             .to_broadcast((P, 4, 2, S)), ACT.Copy).then_inc(s_ztc, 1)
                    tc = at(i, 2)
                    if j == 3 and on_(tc):
                        c.ge(s_zt, 1, tc, 0)
                        nc.scalar.activation(cstage[:], K["ctx"][:, ctx_tiles(tc), :], ACT.Copy).then_inc(s_cs, 1)
                    if j == 1 and on_(ti):
                        c.ge(s_qk, 1, ti, 1)
                        r = ti[1] % 2
                        for k in range(2):
                            for dst, off, scale, bias in ((qx, 0, "sq", "bq"), (kx, 256, "jp", "bk")):
                                nc.scalar.activation(dst[r][:, :, k, :],
                                                     qkbank[:, off:off + 256].rearrange("p (b s) -> p b s", b=4),
                                                     ACT.Identity, bias=K[bias][:, k:k + 1],
                                                     scale=K[scale][:, k:k + 1]).then_inc(s_qx, 1)
                    ty = at(i, -2)
                    if j == 0 and on_(ty):
                        c.ge(s_ot, 1, ty, 1)
                        c.ge(s_y, 1, ty, 0)
                        nc.scalar.activation(oT[:], ybank[:].rearrange("p (b j s) -> p j b s", b=4, j=2),
                                             ACT.Copy).then_inc(s_otc, 1)
                    if on_(i):
                        c.ge(s_sub, 4, i, j + 1)
                        c.ge(s_gp, 4, i, j - 1)
                        c.ge(s_sum, 4, i, j - 1)
                        nc.scalar.activation(ex[j % 2][:], sm[j % 2][:], ACT.Exp).then_inc(s_e, 1)
            schedule(c, body)

        @block.vector
        def _(dve):
            c = Clock(dve, 2, KEYS["attention", "DVE"])

            def body(i):
                for j in range(4):
                    if on_(i):
                        c.ge(s_s, 4, i, j + 1)
                        c.ge(s_e, 4, i, j - 1)
                        neg = K["neg"][:, quad_batches(i), :].unsqueeze(2).to_broadcast((P, 4, 2, S))
                        nc.vector.tensor_tensor(sm[j % 2][:], sbank[j % 2][:].rearrange("p (b j s) -> p b j s", b=4, j=2),
                                                neg, ALU.add).then_inc(s_ma, 1)
                        c.ge(s_ma, 4, i, j + 1)
                        nc.vector.tensor_reduce(mx[j % 2][:], sm[j % 2][:], AX, ALU.max).then_inc(s_mx, 1)
                    ts, ks = step(i, j - 1)
                    if on_(ts):
                        c.ge(s_e, 4, ts, ks + 1)
                        nc.vector.tensor_reduce(zs[ts[1] % 2][:, :, ks, :], ex[ks % 2][:], AX, ALU.add).then_inc(s_sum, 1)
                    tp = at(i, -1)
                    if j == 1 and on_(tp):
                        c.ge(s_sum, 4, tp, 4)
                        nc.vector.reciprocal(rz[:], zs[tp[1] % 2][:].rearrange("p b r j -> p (b r j)")).then_inc(s_rz, 1)
                    if j == 3 and on_(tp):
                        c.ge(s_pv, 4, tp, 4)
                        c.ge(s_rz, 1, tp, 1)
                        c.ge(s_ot, 1, tp, 0)
                        nc.vector.tensor_tensor(on[:].rearrange("p b (g e) -> p (b g) e", e=16),
                                                obank[:].rearrange("p (g e) -> p g e", e=16),
                                                rz[:].unsqueeze(2).to_broadcast((P, 32, 16)), ALU.mult).then_inc(s_on, 1)
                    ti = at(i, 1)
                    if j == 3 and on_(ti):
                        c.ge(s_v, 1, ti, 1)
                        if live(tp, 0, NQ):
                            c.ge(s_pv, 4, tp, 4)
                        for jp in range(2):
                            rows = slice(jp * S, (jp + 1) * S)
                            src = prep[rows, :].rearrange("p (b r j e) -> p b r j e", b=4, r=4, j=2)[:, :, :, jp, :]
                            dst = vb[ti[1] % 2][rows].rearrange("p b (r j e) -> p b r j e", r=4, j=2)[:, :, :, jp, :]
                            bias = K["bv"][rows].rearrange("p (r j e) -> p r j e", r=4, j=2)[:, :, jp, :]
                            nc.vector.tensor_tensor(dst, src, bias.unsqueeze(1).to_broadcast((S, 4, 4, 16)),
                                                    ALU.add).then_inc(s_vb, 1)
                    ty = at(i, -2)
                    if j == 2 and on_(ty):
                        c.ge(s_y, 1, ty, 1)
                        c.ge(s_bo, 1, ty, 1)
                        cols = quad_cols(ty, 2 * D)
                        nc.vector.tensor_tensor(resid[:, cols], ybank[:, 0:256], resid[:, cols], ALU.add).then_inc(s_x, 1)
                    tl = at(i, 2)
                    if on_(tl) and j in (0, 2):
                        x = resid[:, quad_cols(tl, 2 * D)].rearrange("p (t d) -> p t d", t=2)
                        if j == 0:
                            for t in range(2):
                                nc.vector.bn_stats(st[:, t, :], x[:, t, :]).then_inc(s_ln, 1)
                            c.ge(s_ln, 6, tl, 2, alone=True)
                            for t in range(2):
                                nc.vector.bn_aggr(mv[:, t, :], st[:, t, :]).then_inc(s_ln, 1)
                        else:
                            c.ge(s_rs, 2, tl, 2)
                            c.ge(s_zt, 1, tl, 0)
                            for t in range(2):
                                nc.vector.tensor_scalar(z[:, t, :], x[:, t, :], mv[:, t, 0:1], rstd[:, t:t + 1],
                                                        ALU.subtract, ALU.mult).then_inc(s_ln, 1)
            schedule(c, body)

        @block.gpsimd
        def _(pool):
            c = Clock(pool, 2, KEYS["attention", "Pool"])
            nc.gpsimd.memset(mhalf[:], -0.5).then_inc(s_half, 1)
            pool.wait_ge(s_half, 1)

            def body(i):
                for j in range(4):
                    ts, ks = step(i, j - 1)
                    if on_(ts):
                        c.ge(s_e, 4, ts, ks + 1)
                        c.ge(s_t, 4, ts, ks - 1, alone=True)
                        gp = K["gp"][:, quad_batches(ts), :].unsqueeze(2).to_broadcast((P, 4, 2, S))
                        nc.gpsimd.tensor_tensor(pg[ks % 2][:], ex[ks % 2][:], gp, ALU.mult).then_inc(s_gp, 1)
                    if on_(i):
                        c.ge(s_mx, 4, i, j + 1)
                        nc.gpsimd.tensor_tensor(sm[j % 2][:], sm[j % 2][:],
                                                mx[j % 2][:].unsqueeze(3).to_broadcast((P, 4, 2, S)),
                                                ALU.subtract).then_inc(s_sub, 1)
                    tl = at(i, 2)
                    if on_(tl) and j == 1:
                        c.ge(s_ln, 6, tl, 4, alone=True)
                        nc.gpsimd.tensor_scalar(ve[:], mv[:, :, 1], EPS, None, ALU.add).then_inc(s_rs, 1)
                        c.ge(s_rs, 2, tl, 1)
                        nc.gpsimd.tensor_tensor(rstd[:], ve[:], mhalf[:], ALU.pow).then_inc(s_rs, 1)
                    if on_(tl) and j == 3:
                        c.ge(s_ln, 6, tl, 6, alone=True)
                        x = resid[:, quad_cols(tl, 2 * D)].rearrange("p (t d) -> p t d", t=2)
                        nc.gpsimd.tensor_tensor(x, x, K["bo"][:].unsqueeze(1).to_broadcast((P, 2, D)),
                                                ALU.add).then_inc(s_bo, 1)
            schedule(c, body)


def second_attention(nc, A, resid, ident):
    with ExitStack() as ctx:
        shapes = {"gp": [P, 64, 64], "neg": [P, 64, 64], "ctx": [P, 32, P], "wq": [P, P], "wk": [P, P], "wv": [P, P],
                  "bv": [P, P], "bo": [P, P], "jj": [P, 2], "jp": [P, 2], "sq": [P, 2], "bq": [P, 2], "bk": [P, 2],
                  "wo": [P, 2, P], "vb0": [P, 4, P], "vb1": [P, 4, P]}
        K = {k: ctx.enter_context(nc.sbuf_tensor("attn_" + k, s, F32)) for k, s in shapes.items()}
        attention_constants(nc, A, ident, K)
        attention(nc, A, resid, ident, K)

KEYS = {
    ("attention", "PE"): {1: range(-2, 4), 2: (2, 4), 4: (-3, -2, -1, 0, 1, 2, 3, 4, 5, 6, 8), 6: (12, 18)},
    ("attention", "ACT"): {1: range(-2, 4), 4: range(-3, 9)},
    ("attention", "DVE"): {1: range(-1, 4), 2: (6, 8), 4: range(-1, 9), 6: (14, 20)},
    ("attention", "Pool"): {2: (5, 7), 4: range(-2, 9), 6: (16, 18, 22, 24)},

    ("perceiver", "PE"): {1: range(-2, 4), 2: (0, 2, 4, 6, 8), 4: range(-4, 12)},
    ("perceiver", "ACT"): {1: (-2, -1, 0, 3, 4), 2: (4, 6), 4: range(-3, 13)},
    ("perceiver", "DVE"): {1: (-1, 0, 2, 3, 4), 2: (6, 8), 4: (*range(-2, 13), 14, 16, 18, 20),
                           12: (38, 40, 42, 44, 46, 50, 52, 54, 56, 58)},
    ("perceiver", "Pool"): {1: (1, 2), 2: range(2, 8), 4: (*range(-2, 8), 13, 15, 17, 19),
                            12: (36, 40, 46, 48, 52, 58)},
}


def store(nc, resid, out):
    with nc.semaphore("s_out") as s_out, nc.Block() as block:
        @block.sync
        def _(sp):
            sp.dma_start(out.rearrange("(t b) s d -> (b s) t d", b=2),
                         resid[:].rearrange("p (t d) -> p t d", d=P)).then_inc(s_out, 16)
            sp.wait_ge(s_out, 16)


def build(nc, A, out):
    NT = A["x"].shape[0] // 2
    with ExitStack() as ctx:
        def sb(name, shape, dt=F32):
            return ctx.enter_context(nc.sbuf_tensor(name, shape, dt))
        resid = sb("resid", [P, NT * P])
        ident = sb("ident", [P, P])
        with ExitStack() as c2:
            def sb2(name, shape, dt=F32):
                return c2.enter_context(nc.sbuf_tensor(name, shape, dt))
            kvraw = sb2("kvraw", [P, 2 * NT * P])
            wts = {k: sb2("fold_" + k, [P, 2048]) for k in ("A", "V")}
            wts["gain"] = sb2("ln_gain", [P, P])
            wts["shift"] = sb2("ln_shift", [P, P])
            fold_weights(nc, A, resid, kvraw, ident, wts)
            perceiver(nc, A, resid, kvraw, ident, wts)
        mixture(nc, A, "f0_", resid, ident, A["cw"], 8, choose_tokens,
                [A["w1"].rearrange("e d f -> d e f")], A["w2"].rearrange("e (c f) d -> f (e c) d", c=2), None)
        second_attention(nc, A, resid, ident)
        mixture(nc, A, "f1_", resid, ident, A["Wr"], 16, choose_experts,
                [A["Wg"].rearrange("e d f -> d e f"), A["Wu"].rearrange("e d f -> d e f")],
                A["Wd"].rearrange("(p h) f d -> (h f) p d", h=2), (A["Sg"], A["Su"], A["Sd"]))
        store(nc, resid, out)


_NAMES = {"x": "x", "ctx": "ctx_1024", "gp": "fside_BxSxS2_0", "mask": "mask_BxSxS2_ik1",
          "ln_m_g": "L0_xattn_ln_m_g", "ln_m_b": "L0_xattn_ln_m_b", "ln_l_g": "L0_xattn_ln_l_g",
          "ln_l_b": "L0_xattn_ln_l_b", "wq": "L0_xattn_Wq", "wkv": "L0_xattn_Wkv", "wout": "L0_xattn_Wout",
          "cw": "L0_ffn_choice_w", "w1": "L0_ffn_w1", "w2": "L0_ffn_w2",
          "aq_w": "L1_xattn_wq_k", "aq_b": "L1_xattn_wq_b", "ak_w": "L1_xattn_wk_k", "ak_b": "L1_xattn_wk_b",
          "av_w": "L1_xattn_wv_k", "av_b": "L1_xattn_wv_b", "ao_w": "L1_xattn_wo_k", "ao_b": "L1_xattn_wo_b",
          "Wr": "L1_ffn_Wr", "Wg": "L1_ffn_Wg", "Wu": "L1_ffn_Wu", "Wd": "L1_ffn_Wd",
          "Sg": "L1_ffn_Sg", "Su": "L1_ffn_Su", "Sd": "L1_ffn_Sd"}


def kernel(**inputs):
    import numpy as _np
    import concourse.bacc as _bacc
    from concourse.bass_utils import run_bass_kernel_spmd as _run

    nc = _bacc.Bacc("TRN2", target_bir_lowering=False, num_devices=1)
    arrays, A = {}, {}
    for short, name in _NAMES.items():
        a = _np.ascontiguousarray(inputs[name])
        arrays["in_" + short] = a
        A[short] = nc.dram_tensor("in_" + short, a.shape, mybir.dt.from_np(a.dtype), kind="ExternalInput").ap()
    out = nc.dram_tensor("out", A["x"].shape, F32, kind="ExternalOutput").ap()
    build(nc, A, out)
    r = _run(nc, [arrays], core_ids=[0])
    return r.results[0]["out"]
```

```python
from contextlib import ExitStack

import concourse.bass as bass
from concourse import mybir

F32 = mybir.dt.float32
FR = mybir.dt.float32r
I32 = mybir.dt.int32
U32 = mybir.dt.uint32
ALU = mybir.AluOpType
ACT = mybir.ActivationFunctionType
AX = mybir.AxisListType.X

P = 128
EPS = 1e-5


class Clock:

    def __init__(self, eng, step=1, keys=()):
        self.eng, self.step, self.keys, self.regs = eng, step, dict(keys), {}

    def enter(self, u):
        self.u, self.regs = u, {}
        for mul, add in ((per * self.step, add) for per, adds in self.keys.items() for add in adds):
            self.regs[mul, add] = self.eng.to_reg(u * mul + add if add else u * mul)

    def leave(self):
        self.regs = {}

    def ge(self, sem, per, tile, k, alone=False):
        u, c = tile
        if u is None:
            if per * c + k > 0:
                self.eng.wait_ge(sem, per * c + k)
            return
        key = (per * self.step, per * c + k)
        self.eng.wait_ge(sem, self.regs[key])
        if alone:
            self.eng.nop(nofuse=True)


def at(tile, d):
    return (tile[0], tile[1] + d)


def live(tile, lo, hi):
    return tile[0] is not None or lo <= tile[1] < hi


def build_identity(nc, eng, ident, made):
    eng.memset(ident[:], 0.0).then_inc(made, 1)
    eng.wait_ge(made, 1)
    eng.affine_select(out=ident[:], in_=ident[:], compare_op=ALU.not_equal, fill=1.0, base=0,
                      pattern=[[-1, P]], channel_multiplier=1).then_inc(made, 1)


def fold_weights(nc, A, resid, kvraw, ident, wts):
    D, INNER = A["wq"].shape
    DH = 64
    H = INNER // DH
    NB, S, _ = A["x"].shape
    with ExitStack() as ctx:
        def sb(name, shape, dt=F32):
            return ctx.enter_context(nc.sbuf_tensor(name, shape, dt))

        def sem(name):
            return ctx.enter_context(nc.semaphore(name))

        wq = sb("wq_raw", [D, INNER])
        wkv = sb("wkv_raw", [D, 2 * INNER])
        wo = sb("wo_raw", [P, INNER // P, D])
        wqT = sb("wqT", [P, H // 2, D])
        wkT = sb("wkT", [P, H // 2, D])
        wvT = sb("wvT", [P, H // 2, D])
        bank = [ctx.enter_context(nc.psum_tensor(f"fold_ps{i}", [P, 512], F32)) for i in range(2)]
        s_wq, s_wkv, s_wo, s_in = sem("s_wq"), sem("s_wkv"), sem("s_wo"), sem("s_in")
        s_ident = sem("s_ident")
        s_wT = sem("s_wT")
        s_wTc = sem("s_wTc")
        s_prod = sem("s_prod")
        s_fold = sem("s_fold")
        NT = 3 * H // 8
        NP = 2 * H // 4
        block = ctx.enter_context(nc.Block())

        @block.sync
        def _(sp):
            sp.dma_start(wq[:], A["wq"]).then_inc(s_wq, 16)
            sp.dma_start(wkv[:], A["wkv"]).then_inc(s_wkv, 16)
            sp.dma_start(wo[:], A["wout"].rearrange("(t p) n -> p t n", p=P)).then_inc(s_wo, 16)
            kv = kvraw[:].rearrange("p (b d) -> p b d", d=D)
            sp.dma_start(kv[0:S], A["ctx"].rearrange("b s d -> s b d")).then_inc(s_in, 16)
            sp.dma_start(kv[S:2 * S], A["x"].rearrange("b s d -> s b d")).then_inc(s_in, 16)
            sp.dma_start(resid[:].rearrange("p (t d) -> p t d", d=D),
                         A["x"].rearrange("(t b) s d -> (b s) t d", b=2)).then_inc(s_in, 16)
            sp.dma_start(wts["gain"][0:S], A["ln_m_g"].partition_broadcast(S)).then_inc(s_in, 16)
            sp.dma_start(wts["gain"][S:2 * S], A["ln_l_g"].partition_broadcast(S)).then_inc(s_in, 16)
            sp.dma_start(wts["shift"][0:S], A["ln_m_b"].partition_broadcast(S)).then_inc(s_in, 16)
            sp.dma_start(wts["shift"][S:2 * S], A["ln_l_b"].partition_broadcast(S)).then_inc(s_in, 16)
            sp.wait_ge(s_in, 7 * 16)

        @block.gpsimd
        def _(pool):
            build_identity(nc, nc.gpsimd, ident, s_ident)

        def source(n):
            kind, half = n // (H // 8), n % (H // 8)
            src, off = [(wq, 0), (wkv, 0), (wkv, INNER)][kind]
            return src, off + half * 512, [wqT, wkT, wvT][kind][:, half * 4:half * 4 + 4, :]

        @block.tensor
        def _(pe):
            pe.wait_ge(s_ident, 2)
            for n in range(NT):
                src, off, _ = source(n)
                pe.wait_ge(s_wq if n < H // 8 else s_wkv, 16)
                if n >= 2:
                    pe.wait_ge(s_wTc, n - 1)
                for k in range(4):
                    mm = nc.tensor.transpose(bank[n % 2][:, k * P:(k + 1) * P],
                                             src[:, off + k * P:off + (k + 1) * P], ident[:])
                mm.then_inc(s_wT, 1)
            pe.wait_ge(s_wTc, NT)
            pe.wait_ge(s_wo, 16)
            for n in range(NP):
                if n >= 2:
                    pe.wait_ge(s_fold, n - 1)
                for k in range(4):
                    q = n % (NP // 2)
                    h = 8 * (q // 2) + 2 * k + q % 2
                    r = slice((h % 2) * DH, (h % 2) * DH + DH)
                    if n < NP // 2:
                        mm = nc.tensor.matmul(bank[n % 2][:, k * P:(k + 1) * P], wqT[r, h // 2, :],
                                              wkT[r, h // 2, :], start=True, stop=True)
                    else:
                        mm = nc.tensor.matmul(bank[n % 2][:, k * P:(k + 1) * P], wvT[r, h // 2, :],
                                              wo[r, h // 2, :], start=True, stop=True)
                mm.then_inc(s_prod, 1)

        def folded(n):
            q = n % (NP // 2)
            name, scale = ("A", -float(DH) ** -0.5) if n < NP // 2 else ("V", 1.0)
            dst = wts[name][:].rearrange("p (g k e d) -> p g k e d", g=2, k=4, e=2)[:, q // 2, :, q % 2, :]
            return dst, scale

        @block.scalar
        def _(act):
            for n in range(NT):
                act.wait_ge(s_wT, n + 1)
                nc.scalar.activation(source(n)[2], bank[n % 2][:].rearrange("p (a b) -> p a b", a=4),
                                     ACT.Copy).then_inc(s_wTc, 1)
            for n in range(NP):
                act.wait_ge(s_prod, n + 1)
                dst, scale = folded(n)
                nc.scalar.activation(dst, bank[n % 2][:].rearrange("p (k d) -> p k d", k=4), ACT.Copy,
                                     scale=scale).then_inc(s_fold, 1)


def perceiver(nc, A, resid, kvraw, ident, wts):
    D, S, H = P, 64, 16
    NT = A["x"].shape[0] // 2
    with ExitStack() as ctx:
        def sb(name, shape, dt=F32):
            return ctx.enter_context(nc.sbuf_tensor(name, shape, dt))

        def sem(name):
            return ctx.enter_context(nc.semaphore(name))

        st = sb("ln_stats", [P, 2, 6])
        mv = sb("ln_meanvar", [P, 2, 2])
        ve = sb("ln_vareps", [P, 2])
        rstd = sb("ln_rstd", [P, 2])
        mhalf = sb("minus_half", [P, 2])
        kn = sb("kv_normed", [P, 2, D])
        kg = sb("kv_gained", [P, 2, D])
        kvf = sb("kv_full", [P, 2, 2, D])
        kvh = [sb(f"kv_hi{i}", [P, 2, D], FR) for i in range(2)]
        kvl = [sb(f"kv_lo{i}", [P, 2, D], FR) for i in range(2)]
        kvT = [sb(f"kvT{i}", [P, 2, P]) for i in range(2)]
        q = [sb(f"q{i}", [P, 2, H, S]) for i in range(2)]
        nmax = [sb(f"neg_max{i}", [P, 4]) for i in range(2)]
        zsum = [sb(f"exp_sum{i}", [P, 4]) for i in range(2)]
        rz = [sb(f"exp_rsum{i}", [P, 4]) for i in range(2)]
        pe_ = [sb(f"exp{i}", [P, 4, P]) for i in range(2)]
        pn = [sb(f"probs{i}", [P, 4, P]) for i in range(2)]
        pth = [sb(f"probsT_hi{i}", [P, 512], FR) for i in range(2)]
        ptl = [sb(f"probsT_lo{i}", [P, 512], FR) for i in range(2)]
        uT = [sb(f"uT{i}", [P, H, 2, S]) for i in range(2)]

        def pb(name):
            return ctx.enter_context(nc.psum_tensor(name, [P, 512], F32))
        sbank, tbank, ubank = ([pb(f"{n}{i}") for i in range(2)] for n in ("ps_s", "ps_t", "ps_u"))
        qbank, mbank = pb("ps_q"), pb("ps_m")

        s_half = sem("s_half")
        s_ln = sem("s_ln")
        s_rs = sem("s_rs")
        s_kv = sem("s_kv")
        s_kvt = sem("s_kvt")
        s_ktc = sem("s_ktc")
        s_kvl = sem("s_kvl")
        s_q = sem("s_q")
        s_qc = sem("s_qc")
        s_s = sem("s_s")
        s_mx = sem("s_mx")
        s_e = sem("s_e")
        s_rz = sem("s_rz")
        s_pn = sem("s_pn")
        s_t = sem("s_t")
        s_th = sem("s_th")
        s_tl = sem("s_tl")
        s_u = sem("s_u")
        s_uc = sem("s_uc")
        s_y = sem("s_y")
        s_x = sem("s_x")

        def chunk(i, j):
            return at(i, j // 4), j % 4

        def parts(k):
            return k % 2, k // 2

        def tile_cols(tile, width):
            u, c = tile
            return slice(c * width, (c + 1) * width) if u is None else bass.ds(u * (2 * width) + c * width, width)

        LO, HI = 0, NT

        def on(tile):
            return live(tile, LO, HI)

        def schedule(clock, body):
            for i in range(-3, 4):
                body((None, i))
            with clock.eng.Fori(2, NT // 2 - 2) as u:
                clock.enter(u)
                body((u, 0))
                body((u, 1))
                clock.leave()
            for i in range(NT - 4, NT + 2):
                body((None, i))

        block = ctx.enter_context(nc.Block())

        @block.tensor
        def _(pe):
            c = Clock(pe, 2, KEYS["perceiver", "PE"])

            def body(i):
                for j in range(4):
                    tt, kt = chunk(i, j - 2)
                    if on(tt):
                        c.ge(s_pn, 4, tt, kt + 1)
                        c.ge(s_tl, 4, tt, kt - 1)
                        for b in range(4):
                            mm = nc.tensor.transpose(tbank[kt % 2][:, b * P:(b + 1) * P], pn[kt % 2][:, b, :], ident[:])
                        mm.then_inc(s_t, 1)
                    if on(i):
                        b, g = parts(j)
                        r = i[1] % 2
                        c.ge(s_qc, 4, i, 2 * g + 2)
                        c.ge(s_e, 4, i, j - 1)
                        for k in range(4):
                            h = 8 * g + 2 * k
                            out = sbank[j % 2][:, k * P:(k + 1) * P]
                            mm = nc.tensor.matmul(out, q[r][:, b, h:h + 2, :], kvT[r][:, b, :], start=True, stop=True)
                        mm.then_inc(s_s, 1)
                    tu, ku = chunk(i, j - 3)
                    if on(tu):
                        b, g = parts(ku)
                        r = tu[1] % 2
                        c.ge(s_kvl, 2, tu, 2)
                        c.ge(s_tl, 4, tu, ku + 1)
                        c.ge(s_uc, 4, tu, ku - 1)
                        out = ubank[ku % 2][:]
                        nc.tensor.matmul(out, kvh[r][:, b, :], pth[ku % 2][:], start=True, stop=False)
                        nc.tensor.matmul(out, kvh[r][:, b, :], ptl[ku % 2][:], start=False, stop=False)
                        nc.tensor.matmul(out, kvl[r][:, b, :], pth[ku % 2][:], start=False, stop=True).then_inc(s_u, 1)
                    tq = at(i, 1)
                    if on(tq):
                        r = tq[1] % 2
                        c.ge(s_ktc, 1, tq, 1)
                        c.ge(s_qc, 4, tq, j)
                        for k in range(4):
                            h = 4 * j + k
                            out = qbank[:, k * P:(k + 1) * P]
                            mm = nc.tensor.matmul(out, wts["A"][:, h * P:(h + 1) * P], kvT[r][:, :, S:2 * S],
                                                  start=True, stop=True)
                        mm.then_inc(s_q, 1)
                    ty = at(i, -2)
                    if j < 2 and on(ty):
                        r = ty[1] % 2
                        if j == 0:
                            c.ge(s_uc, 4, ty, 4)
                            c.ge(s_x, 1, ty, 0)
                            if live(i, -3, NT - 1):
                                c.ge(s_ktc, 1, ty, 4)
                        for h in range(j * H // 2, (j + 1) * H // 2):
                            out = mbank[:, 0:D]
                            mm = nc.tensor.matmul(out, uT[r][:, h, :, :], wts["V"][:, h * P:(h + 1) * P],
                                                  start=(h == 0), stop=(h == H - 1))
                        if j == 1:
                            mm.then_inc(s_y, 1)
                    tk = at(i, 2)
                    if j == 2 and on(tk):
                        c.ge(s_kv, 2, tk, 2)
                        c.ge(s_x, 1, tk, -3)
                        for b in range(2):
                            mm = nc.tensor.transpose(mbank[:, b * P:(b + 1) * P], kvf[:, tk[1] % 2, b, :], ident[:])
                        mm.then_inc(s_kvt, 1)
            schedule(c, body)

        @block.scalar
        def _(act):
            c = Clock(act, 2, KEYS["perceiver", "ACT"])

            def body(i):
                for j in range(4):
                    tk = at(i, 2)
                    if j == 3 and on(tk):
                        c.ge(s_kvt, 1, tk, 1)
                        c.ge(s_s, 4, tk, -4)
                        nc.scalar.activation(kvT[tk[1] % 2][:], mbank[:, 0:2 * P].rearrange("p (b k) -> p b k", b=2),
                                             ACT.Copy).then_inc(s_ktc, 1)
                    tt, kt = chunk(i, j - 2)
                    if on(tt):
                        c.ge(s_t, 4, tt, kt + 1)
                        c.ge(s_u, 4, tt, kt - 1)
                        nc.scalar.activation(pth[kt % 2][:], tbank[kt % 2][:], ACT.Copy).then_inc(s_th, 1)
                    if on(i):
                        c.ge(s_mx, 4, i, j + 1)
                        c.ge(s_pn, 4, i, j - 1)
                        for k in range(4):
                            e = nc.scalar.activation(pe_[j % 2][:, k, :], sbank[j % 2][:, k * P:(k + 1) * P], ACT.Exp,
                                                     bias=nmax[j % 2][:, k:k + 1], scale=-1.0,
                                                     accum_out=zsum[j % 2][:, k:k + 1])
                        e.then_inc(s_e, 1)
                    tu, ku = chunk(i, j - 3)
                    if on(tu):
                        b, g = parts(ku)
                        c.ge(s_u, 4, tu, ku + 1)
                        c.ge(s_y, 1, tu, -1)
                        nc.scalar.activation(uT[tu[1] % 2][:, 8 * g:8 * g + 8, b, :],
                                             ubank[ku % 2][:].rearrange("p (h s) -> p h s", s=S),
                                             ACT.Copy).then_inc(s_uc, 1)
            schedule(c, body)

        @block.vector
        def _(dve):
            c = Clock(dve, 2, KEYS["perceiver", "DVE"])

            def body(i):
                for j in range(4):
                    if on(i):
                        c.ge(s_s, 4, i, j + 1)
                        c.ge(s_e, 4, i, j - 1)
                        nc.vector.tensor_reduce(nmax[j % 2][:], sbank[j % 2][:].rearrange("p (a b) -> p a b", a=4),
                                                AX, ALU.min).then_inc(s_mx, 1)
                    tk = at(i, 2)
                    tr, kr = chunk(i, j - 1)
                    if on(tr):
                        c.ge(s_e, 4, tr, kr + 1)
                        c.ge(s_pn, 4, tr, kr - 1)
                        nc.vector.reciprocal(rz[kr % 2][:], zsum[kr % 2][:]).then_inc(s_rz, 1)
                    tt, kt = chunk(i, j - 2)
                    if on(tt):
                        c.ge(s_th, 4, tt, kt + 1)
                        nc.vector.tensor_tensor(ptl[kt % 2][:], tbank[kt % 2][:], pth[kt % 2][:].bitcast(F32),
                                                ALU.subtract).then_inc(s_tl, 1)
                    tq = at(i, 1)
                    if on(tq):
                        c.ge(s_q, 4, tq, j + 1)
                        nc.vector.tensor_copy(q[tq[1] % 2][:, :, 4 * j:4 * j + 4, :],
                                              qbank[:].rearrange("p (h b s) -> p b h s", h=4, b=2)).then_inc(s_qc, 1)
                    ty = at(i, -2)
                    if j == 2 and on(ty):
                        cols = tile_cols(ty, D)
                        c.ge(s_y, 1, ty, 1)
                        nc.vector.tensor_tensor(resid[:, cols], mbank[:, 0:D], resid[:, cols], ALU.add).then_inc(s_x, 1)
                    tl = at(i, 3)
                    if on(tl) and j == 0:
                        cols = tile_cols(tl, 2 * D)
                        raw = kvraw[:, cols].rearrange("p (b d) -> p b d", b=2)
                        for b in range(2):
                            nc.vector.bn_stats(st[:, b, :], raw[:, b, :]).then_inc(s_ln, 1)
                        c.ge(s_ln, 12, tl, 2, alone=True)
                        for b in range(2):
                            nc.vector.bn_aggr(mv[:, b, :], st[:, b, :]).then_inc(s_ln, 1)
                    if on(tl) and j == 2:
                        cols = tile_cols(tl, 2 * D)
                        raw = kvraw[:, cols].rearrange("p (b d) -> p b d", b=2)
                        c.ge(s_ln, 12, tl, 4)
                        c.ge(s_rs, 4, tl, 2)
                        c.ge(s_kv, 2, tl, 0)
                        for b in range(2):
                            nc.vector.tensor_scalar(kn[:, b, :], raw[:, b, :], mv[:, b, 0:1], rstd[:, b:b + 1],
                                                    ALU.subtract, ALU.mult).then_inc(s_ln, 1)
                        c.ge(s_ln, 12, tl, 6)
                        for b in range(2):
                            nc.vector.bn_stats(st[S:P, b, :], kn[S:P, b, :]).then_inc(s_ln, 1)
                        c.ge(s_ln, 12, tl, 8, alone=True)
                        for b in range(2):
                            nc.vector.bn_aggr(mv[S:P, b, :], st[S:P, b, :]).then_inc(s_ln, 1)
                    if on(tl) and j == 3:
                        c.ge(s_ln, 12, tl, 10)
                        c.ge(s_rs, 4, tl, 4)
                        for b in range(2):
                            nc.vector.tensor_scalar(kn[S:P, b, :], kn[S:P, b, :], mv[S:P, b, 0:1], rstd[S:P, b:b + 1],
                                                    ALU.subtract, ALU.mult).then_inc(s_ln, 1)
            schedule(c, body)

        @block.gpsimd
        def _(pool):
            c = Clock(pool, 2, KEYS["perceiver", "Pool"])
            nc.gpsimd.memset(mhalf[:], -0.5).then_inc(s_half, 1)
            pool.wait_ge(s_half, 1)

            def body(i):
                for j in range(4):
                    tn, kn_ = chunk(i, j - 1)
                    if on(tn):
                        c.ge(s_rz, 4, tn, kn_ + 1)
                        c.ge(s_t, 4, tn, kn_ - 1)
                        nc.gpsimd.tensor_tensor(pn[kn_ % 2][:], pe_[kn_ % 2][:],
                                                rz[kn_ % 2][:].unsqueeze(2).to_broadcast((P, 4, P)),
                                                ALU.mult).then_inc(s_pn, 1)
                    tl = at(i, 3)
                    if on(tl) and j == 0:
                        c.ge(s_ln, 12, tl, 4, alone=True)
                        nc.gpsimd.tensor_scalar(ve[:], mv[:, :, 1], EPS, None, ALU.add).then_inc(s_rs, 1)
                        c.ge(s_rs, 4, tl, 1)
                        nc.gpsimd.tensor_tensor(rstd[:], ve[:], mhalf[:], ALU.pow).then_inc(s_rs, 1)
                    if on(tl) and j == 2:
                        c.ge(s_ln, 12, tl, 10, alone=True)
                        nc.gpsimd.tensor_scalar(ve[:], mv[:, :, 1], EPS, None, ALU.add).then_inc(s_rs, 1)
                        c.ge(s_rs, 4, tl, 3)
                        nc.gpsimd.tensor_tensor(rstd[:], ve[:], mhalf[:], ALU.pow).then_inc(s_rs, 1)
                    tk = at(i, 2)
                    if on(tk) and j == 0:
                        c.ge(s_ln, 12, tk, 12)
                        nc.gpsimd.tensor_tensor(kg[:], kn[:], wts["gain"][:].unsqueeze(1).to_broadcast((P, 2, D)),
                                                ALU.mult).then_inc(s_kv, 1)
                        c.ge(s_kv, 2, tk, 1)
                        c.ge(s_kvl, 2, tk, -2)
                        c.ge(s_kvt, 1, tk, -1)
                        nc.gpsimd.tensor_tensor(kvf[:, tk[1] % 2], kg[:], wts["shift"][:].unsqueeze(1).to_broadcast((P, 2, D)),
                                                ALU.add).then_inc(s_kv, 1)
                    tq = at(i, 1)
                    if j == 3 and on(tq):
                        r = tq[1] % 2
                        c.ge(s_kv, 2, tq, 2)
                        c.ge(s_u, 4, tq, -4, alone=True)
                        nc.gpsimd.tensor_copy(kvh[r][:], kvf[:, r]).then_inc(s_kvl, 1)
                        c.ge(s_kvl, 2, tq, 1)
                        nc.gpsimd.tensor_tensor(kvl[r][:], kvf[:, r], kvh[r][:].bitcast(F32),
                                                ALU.subtract).then_inc(s_kvl, 1)
            schedule(c, body)


def norm_and_score(nc, tag, resid, ident, score_src, E, z, logits, split=None, after=None):
    D = P
    NG = resid.shape[1] // (4 * D)
    with ExitStack() as ctx:
        def sb(name, shape, dt=F32):
            return ctx.enter_context(nc.sbuf_tensor(tag + name, shape, dt))

        def sem(name):
            return ctx.enter_context(nc.semaphore(tag + name))

        w = sb("w_score", [P, E])
        st = [sb(f"st{i}", [P, 4, 6]) for i in range(2)]
        mv = [sb(f"mv{i}", [P, 4, 2]) for i in range(2)]
        ve = [sb(f"ve{i}", [P, 4]) for i in range(2)]
        rstd = [sb(f"rstd{i}", [P, 4]) for i in range(2)]
        mhalf = sb("mhalf", [P, 4])
        zT = [sb(f"zT{i}", [P, 512]) for i in range(2)]
        tb = [ctx.enter_context(nc.psum_tensor(tag + f"tb{i}", [P, 512], F32)) for i in range(2)]
        lb = [ctx.enter_context(nc.psum_tensor(tag + f"lb{i}", [P, 512], F32)) for i in range(2)]
        s_w = sem("s_w")
        s_half = sem("s_half")
        s_ln = sem("s_ln")
        s_rs = sem("s_rs")
        s_t = sem("s_t")
        s_tc = sem("s_tc")
        s_lo = sem("s_lo")
        s_l = sem("s_l")
        s_lc = sem("s_lc")
        x3 = resid[:].rearrange("p (t d) -> p t d", d=D)
        z3 = z[:].rearrange("p (t d) -> p t d", d=D)
        block = ctx.enter_context(nc.Block())

        @block.sync
        def _(sp):
            if score_src.shape[1] == E:
                sp.dma_start(w[:], score_src).then_inc(s_w, 16)
            else:
                with nc.allow_non_contiguous_dma(reason="the small scoring matrix, transposed once"):
                    sp.dma_start(w[:], score_src.rearrange("e d -> d e")).then_inc(s_w, 16)

        @block.gpsimd
        def _(pool):
            nc.gpsimd.memset(mhalf[:], -0.5).then_inc(s_half, 1)
            pool.wait_ge(s_half, 1)
            for g in range(NG):
                pool.wait_ge(s_ln, 12 * g + 4 if g else 8)
                nc.gpsimd.tensor_scalar(ve[g % 2][:], mv[g % 2][:, :, 1], EPS, None, ALU.add).then_inc(s_rs, 1)
                pool.wait_ge(s_rs, 2 * g + 1)
                nc.gpsimd.tensor_tensor(rstd[g % 2][:], ve[g % 2][:], mhalf[:], ALU.pow).then_inc(s_rs, 1)

        @block.vector
        def _(dve):
            def stats(g):
                base = 0 if g == 0 else 12 * g - 4
                for k in range(4):
                    nc.vector.bn_stats(st[g % 2][:, k, :], x3[:, 4 * g + k, :]).then_inc(s_ln, 1)
                dve.wait_ge(s_ln, base + 4)
                for k in range(4):
                    nc.vector.bn_aggr(mv[g % 2][:, k, :], st[g % 2][:, k, :]).then_inc(s_ln, 1)

            def lo(g):
                dve.wait_ge(s_tc, 2 * g + 2)
                hi, low = (s[:, g * 512:(g + 1) * 512] for s in split)
                nc.vector.tensor_tensor(low, tb[g % 2][:], hi.bitcast(F32), ALU.subtract).then_inc(s_lo, 1)

            stats(0)
            for g in range(NG):
                if g + 1 < NG:
                    stats(g + 1)
                dve.wait_ge(s_rs, 2 * g + 2)
                for k in range(4):
                    nc.vector.tensor_scalar(z3[:, 4 * g + k, :], x3[:, 4 * g + k, :], mv[g % 2][:, k, 0:1],
                                            rstd[g % 2][:, k:k + 1], ALU.subtract, ALU.mult).then_inc(s_ln, 1)
                if split and g >= 1:
                    lo(g - 1)
            if split:
                lo(NG - 1)

        def normed(g):
            return 12 * (g + 2) - 4 if g + 1 < NG else 12 * NG

        @block.tensor
        def _(pe):
            def score(g):
                if g == 0:
                    pe.wait_ge(s_w, 16)
                pe.wait_ge(s_tc, (2 if split else 1) * g + 1)
                if g >= 2:
                    pe.wait_ge(s_lc, g - 1)
                for k in range(4):
                    mm = nc.tensor.matmul(lb[g % 2][:, k * E:(k + 1) * E], zT[g % 2][:, k * P:(k + 1) * P], w[:],
                                          start=True, stop=True)
                mm.then_inc(s_l, 1)

            for g in range(NG):
                pe.wait_ge(s_ln, normed(g))
                if g >= 2:
                    pe.wait_ge(s_lo if split else s_tc, g - 1)
                for k in range(4):
                    mm = nc.tensor.transpose(tb[g % 2][:, k * P:(k + 1) * P], z3[:, 4 * g + k, :], ident[:])
                mm.then_inc(s_t, 1)
                if g >= 1:
                    score(g - 1)
            score(NG - 1)

        @block.scalar
        def _(act):
            def out(g):
                act.wait_ge(s_l, g + 1)
                nc.scalar.activation(logits[:, g * 4 * E:(g + 1) * 4 * E], lb[g % 2][:, 0:4 * E],
                                     ACT.Copy).then_inc(s_lc, 1)

            for g in range(NG):
                act.wait_ge(s_t, g + 1)
                if g >= 2:
                    act.wait_ge(s_l, g - 1)
                nc.scalar.activation(zT[g % 2][:], tb[g % 2][:], ACT.Copy).then_inc(s_tc, 1)
                if split:
                    nc.scalar.activation(split[0][:, g * 512:(g + 1) * 512], tb[g % 2][:], ACT.Copy).then_inc(s_tc, 1)
                if g >= 1:
                    out(g - 1)
            out(NG - 1)


def softmax_rows(nc, tag, logits, E, NTL):
    with ExitStack() as ctx:
        mx = ctx.enter_context(nc.sbuf_tensor(tag + "mx", [P, NTL], F32))
        sm = ctx.enter_context(nc.sbuf_tensor(tag + "sm", [P, NTL], F32))
        rs = ctx.enter_context(nc.sbuf_tensor(tag + "rs", [P, NTL], F32))
        s_v = ctx.enter_context(nc.semaphore(tag + "s_v"))
        s_a = ctx.enter_context(nc.semaphore(tag + "s_a"))
        lg = logits[:].rearrange("p (t e) -> p t e", e=E)
        block = ctx.enter_context(nc.Block())

        @block.vector
        def _(dve):
            nc.vector.tensor_reduce(mx[:], lg, AX, ALU.max).then_inc(s_v, 1)
            dve.wait_ge(s_v, 1)
            nc.vector.tensor_tensor(lg, lg, mx[:].unsqueeze(2).to_broadcast((P, NTL, E)), ALU.subtract).then_inc(s_v, 1)
            dve.wait_ge(s_a, 1)
            nc.vector.tensor_reduce(sm[:], lg, AX, ALU.add).then_inc(s_v, 1)
            dve.wait_ge(s_v, 3)
            nc.vector.reciprocal(rs[:], sm[:]).then_inc(s_v, 1)
            dve.wait_ge(s_v, 4)
            nc.vector.tensor_tensor(lg, lg, rs[:].unsqueeze(2).to_broadcast((P, NTL, E)), ALU.mult).then_inc(s_v, 1)

        @block.scalar
        def _(act):
            act.wait_ge(s_v, 2)
            nc.scalar.activation(logits[:], logits[:], ACT.Exp).then_inc(s_a, 1)



def choose_tokens(nc, tag, ident, probs, pos):
    S, K = 64, 16
    with ExitStack() as ctx:
        def sb(name, shape, dt=F32):
            return ctx.enter_context(nc.sbuf_tensor(tag + name, shape, dt))

        def sem(name):
            return ctx.enter_context(nc.semaphore(tag + name))
        pT = sb("pT", [P, 4, S])
        w = [sb(f"left{i}", [P, 4, S]) for i in range(2)]
        m8 = [sb(f"best{i}", [P, 4, 8]) for i in range(2)]
        ones = sb("ones", [P, S])
        cum = sb("cum", [P, 4, S])
        tb = [ctx.enter_context(nc.psum_tensor(tag + f"tb{i}", [P, 512], F32)) for i in range(2)]
        s_pt = sem("s_pt")
        s_ptc = sem("s_ptc")
        s_one = sem("s_one")
        s_v = sem("s_v")
        s_ct = sem("s_ct")
        block = ctx.enter_context(nc.Block())

        @block.tensor
        def _(pe):
            for g in range(2):
                mm = nc.tensor.transpose(tb[0][:, g * P:(g + 1) * P], probs[:, g * P:(g + 1) * P], ident[:])
            mm.then_inc(s_pt, 1)
            pe.wait_ge(s_v, 22)
            for g in range(2):
                mm = nc.tensor.transpose(tb[1][:, g * P:(g + 1) * P], w[0][:, 2 * g:2 * g + 2, :], ident[:])
            mm.then_inc(s_ct, 1)

        @block.scalar
        def _(act):
            act.wait_ge(s_pt, 1)
            nc.scalar.activation(pT[:], tb[0][:, 0:2 * P].rearrange("p (c s) -> p c s", c=4), ACT.Copy).then_inc(s_ptc, 1)
            act.wait_ge(s_ct, 1)
            nc.scalar.activation(pos[:], tb[1][:, 0:2 * P], ACT.Copy)

        @block.gpsimd
        def _(pool):
            nc.gpsimd.memset(ones[:], 1.0).then_inc(s_one, 1)

        @block.vector
        def _(dve):
            dve.wait_ge(s_ptc, 1)
            src = pT
            for r in range(K // 8):
                for c in range(4):
                    nc.vector.max(m8[r][:, c, :], src[:, c, :]).then_inc(s_v, 1)
                dve.wait_ge(s_v, 8 * r + 4)
                for c in range(4):
                    nc.vector.match_replace(w[r][:, c, :], m8[r][:, c, :], src[:, c, :], -1.0).then_inc(s_v, 1)
                dve.wait_ge(s_v, 8 * r + 8)
                src = w[r]
            nc.vector.tensor_scalar(w[1][:], w[1][:], -1.0, None, ALU.is_equal).then_inc(s_v, 1)
            dve.wait_ge(s_v, 17)
            dve.wait_ge(s_one, 1)
            for c in range(4):
                nc.vector.tensor_tensor_scan(cum[:, c, :], ones[:], w[1][:, c, :], 0.0, ALU.mult,
                                             ALU.add).then_inc(s_v, 1)
            dve.wait_ge(s_v, 21)
            nc.vector.tensor_tensor(w[0][:], cum[:], w[1][:], ALU.mult).then_inc(s_v, 1)


def gather_tokens(nc, A, tag, z, pos, oh, xg, wts):
    E, K, S, D = 8, 16, 64, P
    NT = z.shape[1] // D
    CH = 8
    with ExitStack() as ctx:
        def sb(name, shape, dt=F32):
            return ctx.enter_context(nc.sbuf_tensor(tag + name, shape, dt))

        def sem(name):
            return ctx.enter_context(nc.semaphore(tag + name))
        zh, zl = sb("z_hi", [P, NT * D], FR), sb("z_lo", [P, NT * D], FR)
        iota = sb("iota", [P, K])
        raw = sb("w_raw", [P, 2048])
        bank = [[ctx.enter_context(nc.psum_tensor(tag + f"ps{i}{b}", [P, 512], F32)) for b in range(2)] for i in range(2)]
        s_w = sem("s_w")
        s_wh = sem("s_wh")
        s_wl = sem("s_wl")
        s_io = sem("s_io")
        s_zh = sem("s_zh")
        s_zl = sem("s_zl")
        s_oh = sem("s_oh")
        s_g = sem("s_g")
        s_ga = sem("s_ga")
        s_gv = sem("s_gv")
        block = ctx.enter_context(nc.Block())

        @block.sync
        def _(sp):
            sp.dma_start(raw[:].rearrange("p (e f) -> p e f", e=E), A["w1"].rearrange("e d f -> d e f")).then_inc(s_w, 16)
            sp.wait_ge(s_wl, 1)
            sp.dma_start(raw[:].rearrange("p (e d) -> p e d", d=D),
                         A["w2"].rearrange("e (c f) d -> f (e c) d", c=2)).then_inc(s_w, 16)

        @block.gpsimd
        def _(pool):
            nc.gpsimd.iota(iota[:], pattern=[[1, K]], base=1, channel_multiplier=0,
                           allow_small_or_imprecise_dtypes=True).then_inc(s_io, 1)
            for c in range(CH):
                cols = slice(c * 512, (c + 1) * 512)
                pool.wait_ge(s_zh, c + 1)
                nc.gpsimd.tensor_tensor(zl[:, cols], z[:, cols], zh[:, cols].bitcast(F32), ALU.subtract).then_inc(s_zl, 1)

        @block.tensor
        def _(pe):
            for t in range(NT):
                if t % 4 == 0:
                    pe.wait_ge(s_zl, t // 4 + 1)
                pe.wait_ge(s_oh, t + 1)
                if t >= 2:
                    pe.wait_ge(s_ga, t - 1)
                    pe.wait_ge(s_gv, t - 1)
                for b in range(2):
                    rows = slice(b * S, (b + 1) * S)
                    for k, part in enumerate((zh, zl)):
                        mm = nc.tensor.matmul(bank[t % 2][b][:, k * P:(k + 1) * P], part[rows, t * D:(t + 1) * D],
                                              oh[rows, t, :, :], start=True, stop=True)
                mm.then_inc(s_g, 1)

        @block.scalar
        def _(act):
            def high(c):
                cols = slice(c * 512, (c + 1) * 512)
                nc.scalar.activation(zh[:, cols], z[:, cols], ACT.Copy).then_inc(s_zh, 1)
            high(0)
            high(1)
            for t in range(NT):
                if t % 4 == 0 and t // 4 + 2 < CH:
                    high(t // 4 + 2)
                if t in (NT // 3, 2 * NT // 3):
                    k = 0 if t == NT // 3 else 1
                    act.wait_ge(s_w, 16 * (k + 1))
                    nc.scalar.activation(wts[k][0][:], raw[:], ACT.Copy).then_inc(s_wh, 1)
                act.wait_ge(s_g, t + 1)
                for k in range(2):
                    mm = nc.scalar.activation(xg[k][:, :, 2 * t, :],
                                              bank[t % 2][0][:, k * P:(k + 1) * P].rearrange("p (e j) -> p e j", e=E),
                                              ACT.Copy)
                mm.then_inc(s_ga, 1)

        @block.vector
        def _(dve):
            def one_hot(t):
                nc.vector.tensor_tensor(oh[:, t], pos[:, t * E:(t + 1) * E].unsqueeze(2).to_broadcast((P, E, K)),
                                        iota[:].unsqueeze(1).to_broadcast((P, E, K)), ALU.is_equal).then_inc(s_oh, 1)
            dve.wait_ge(s_io, 1)
            for t in range(3):
                one_hot(t)
            for t in range(NT):
                if t + 3 < NT:
                    one_hot(t + 3)
                if t in (NT // 3 + 2, 2 * NT // 3 + 2):
                    k = 0 if t == NT // 3 + 2 else 1
                    dve.wait_ge(s_wh, k + 1)
                    nc.vector.tensor_tensor(wts[k][1][:], raw[:], wts[k][0][:].bitcast(F32), ALU.subtract).then_inc(s_wl, 1)
                dve.wait_ge(s_g, t + 1)
                for k in range(2):
                    mm = nc.vector.tensor_copy(xg[k][:, :, 2 * t + 1, :],
                                               bank[t % 2][1][:, k * P:(k + 1) * P].rearrange("p (e j) -> p e j", e=E))
                mm.then_inc(s_gv, 1)


def run_experts(nc, tag, xg, wts, yT):
    E, K, NB = 8, 16, xg[0].shape[2]
    GB = 512 // K
    NS = (NB // GB) * E * 2
    LAG = 2
    with ExitStack() as ctx:
        def sb(name, shape, dt=F32):
            return ctx.enter_context(nc.sbuf_tensor(tag + name, shape, dt))

        def sem(name):
            return ctx.enter_context(nc.semaphore(tag + name))
        h32 = [sb(f"hid{i}", [P, 512]) for i in range(2)]
        hh = [sb(f"hid_hi{i}", [P, 512], FR) for i in range(3)]
        hl = [sb(f"hid_lo{i}", [P, 512], FR) for i in range(3)]
        hb = [ctx.enter_context(nc.psum_tensor(tag + f"ps_h{i}", [P, 512], F32)) for i in range(3)]
        yb = [ctx.enter_context(nc.psum_tensor(tag + f"ps_y{i}", [P, 512], F32)) for i in range(2)]
        s_h = sem("s_h")
        s_si = sem("s_si")
        s_hi = sem("s_hi")
        s_lo = sem("s_lo")
        s_d = sem("s_d")
        s_yc = sem("s_yc")
        (w1h, w1l), (w2h, w2l) = wts
        block = ctx.enter_context(nc.Block())

        def place(n):
            return n // (2 * E), (n // 2) % E, n % 2

        @block.tensor
        def _(pe):
            for n in range(NS + LAG):
                if n < NS:
                    g, e, f = place(n)
                    if n >= 3:
                        pe.wait_ge(s_si, n - 2)
                    w = slice((2 * e + f) * P, (2 * e + f + 1) * P)
                    for k, (wp, xp) in enumerate(((w1h, 0), (w1h, 1), (w1l, 0))):
                        mm = nc.tensor.matmul(hb[n % 3][:], wp[:, w], xg[xp][:, e, g * GB:(g + 1) * GB, :],
                                              start=(k == 0), stop=(k == 2))
                    mm.then_inc(s_h, 1)
                m = n - LAG
                if m >= 0:
                    g, e, f = place(m)
                    w = slice((2 * e + f) * P, (2 * e + f + 1) * P)
                    pe.wait_ge(s_lo, m + 1)
                    if f == 0 and m >= 4:
                        pe.wait_ge(s_yc, m // 2 - 1)
                    for k, (wp, h) in enumerate(((w2h, hh), (w2h, hl), (w2l, hh))):
                        mm = nc.tensor.matmul(yb[(m // 2) % 2][:], wp[:, w], h[m % 3][:],
                                              start=(f == 0 and k == 0), stop=(f == 1 and k == 2))
                    mm.then_inc(s_d, 1)

        @block.scalar
        def _(act):
            for n in range(NS + LAG):
                if n < NS:
                    act.wait_ge(s_h, n + 1)
                    if n >= 2:
                        act.wait_ge(s_lo, n - 1)
                    nc.scalar.activation(h32[n % 2][:], hb[n % 3][:], ACT.Silu).then_inc(s_si, 1)
                    act.wait_ge(s_si, n + 1)
                    if n >= 3:
                        act.wait_ge(s_d, n - 2)
                    nc.scalar.activation(hh[n % 3][:], h32[n % 2][:], ACT.Copy).then_inc(s_hi, 1)
                m = n - LAG
                if m >= 0 and m % 2:
                    g, e, _f = place(m)
                    act.wait_ge(s_d, m + 1)
                    nc.scalar.activation(yT[:, g * GB:(g + 1) * GB, e, :],
                                         yb[(m // 2) % 2][:].rearrange("p (b j) -> p b j", j=K), ACT.Copy).then_inc(s_yc, 1)

        @block.vector
        def _(dve):
            for n in range(NS):
                dve.wait_ge(s_hi, n + 1)
                if n >= 3:
                    dve.wait_ge(s_d, n - 2)
                nc.vector.tensor_tensor(hl[n % 3][:], h32[n % 2][:], hh[n % 3][:].bitcast(F32),
                                        ALU.subtract).then_inc(s_lo, 1)


def scatter_outputs(nc, tag, resid, ident, oh, probs, yT):
    E, K, S, D = 8, 16, 64, P
    NT = resid.shape[1] // D
    with ExitStack() as ctx:
        def sb(name, shape, dt=F32):
            return ctx.enter_context(nc.sbuf_tensor(tag + name, shape, dt))

        def sem(name):
            return ctx.enter_context(nc.semaphore(tag + name))
        ohw = [sb(f"one_hot_w{i}", [P, E, K]) for i in range(2)]
        ys = [sb(f"slots{i}", [P, 3 * P]) for i in range(2)]
        tb = [ctx.enter_context(nc.psum_tensor(tag + f"ps_t{i}", [P, 512], F32)) for i in range(2)]
        ob = [ctx.enter_context(nc.psum_tensor(tag + f"ps_o{i}", [P, 512], F32)) for i in range(2)]
        s_w = sem("s_w")
        s_t = sem("s_t")
        s_c = sem("s_c")
        s_o = sem("s_o")
        s_x = sem("s_x")
        pr = probs[:].rearrange("p (t e) -> p t e", e=E)
        block = ctx.enter_context(nc.Block())

        @block.gpsimd
        def _(pool):
            for t in range(NT):
                if t >= 2:
                    pool.wait_ge(s_t, t - 1)
                nc.gpsimd.tensor_tensor(ohw[t % 2][:], oh[:, t].bitcast(F32),
                                        pr[:, t, :].unsqueeze(2).to_broadcast((P, E, K)), ALU.mult).then_inc(s_w, 1)

        @block.tensor
        def _(pe):
            for n in range(NT + 1):
                if n < NT:
                    pe.wait_ge(s_w, n + 1)
                    if n >= 2:
                        pe.wait_ge(s_c, n - 1)
                    nc.tensor.transpose(tb[n % 2][:, 0:P], ohw[n % 2][:], ident[:])
                    for b in range(2):
                        mm = nc.tensor.transpose(tb[n % 2][:, (b + 1) * P:(b + 2) * P], yT[:, 2 * n + b], ident[:])
                    mm.then_inc(s_t, 1)
                t = n - 1
                if t >= 0:
                    pe.wait_ge(s_c, t + 1)
                    if t >= 2:
                        pe.wait_ge(s_x, t - 1)
                    for b in range(2):
                        mm = nc.tensor.matmul(ob[t % 2][b * S:(b + 1) * S, 0:D], ys[t % 2][:, b * S:(b + 1) * S],
                                              ys[t % 2][:, (b + 1) * P:(b + 2) * P], start=True, stop=True)
                    mm.then_inc(s_o, 1)

        @block.scalar
        def _(act):
            for t in range(NT):
                act.wait_ge(s_t, t + 1)
                if t >= 2:
                    act.wait_ge(s_o, t - 1)
                nc.scalar.activation(ys[t % 2][:], tb[t % 2][:, 0:3 * P], ACT.Copy).then_inc(s_c, 1)

        @block.vector
        def _(dve):
            for t in range(NT):
                dve.wait_ge(s_o, t + 1)
                cols = slice(t * D, (t + 1) * D)
                nc.vector.tensor_tensor(resid[:, cols], ob[t % 2][:, 0:D], resid[:, cols], ALU.add).then_inc(s_x, 1)


def expert_choice(nc, A, resid, ident):
    NT, E, K = resid.shape[1] // P, 8, 16
    with ExitStack() as ctx:
        def sb(name, shape, dt=F32, stack=ctx):
            return stack.enter_context(nc.sbuf_tensor("ec_" + name, shape, dt))
        probs = sb("probs", [P, NT * E])
        pos = sb("pos", [P, NT * E])
        oh = sb("one_hot", [P, NT, E, K], FR)
        with ExitStack() as c2:
            xg = [sb(f"xg{i}", [P, E, 2 * NT, K], FR, c2) for i in range(2)]
            wts = [[sb(f"w{k}_{n}", [P, 2048], FR, c2) for n in ("hi", "lo")] for k in (1, 2)]
            with ExitStack() as c3:
                z = sb("z", [P, NT * P], F32, c3)
                norm_and_score(nc, "ec_ns_", resid, ident, A["cw"], E, z, probs)
                softmax_rows(nc, "ec_sm_", probs, E, NT)
                choose_tokens(nc, "ec_ch_", ident, probs, pos)
                gather_tokens(nc, A, "ec_ga_", z, pos, oh, xg, wts)
            yT = sb("yT", [P, 2 * NT, E, K], F32, c2)
            run_experts(nc, "ec_ex_", xg, wts, yT)
            scatter_outputs(nc, "ec_sc_", resid, ident, oh, probs, yT)


def choose_experts(nc, tag, ident, probs, cw):
    E, K = 16, 2
    NT = probs.shape[1] // E
    with ExitStack() as ctx:
        m8 = ctx.enter_context(nc.sbuf_tensor(tag + "best", [P, NT, 8], F32))
        left = ctx.enter_context(nc.sbuf_tensor(tag + "left", [P, NT, E], F32))
        s_v = ctx.enter_context(nc.semaphore(tag + "s_v"))
        pr = probs[:].rearrange("p (t e) -> p t e", e=E)
        block = ctx.enter_context(nc.Block())

        @block.vector
        def _(dve):
            for t in range(NT):
                nc.vector.max(m8[:, t, :], pr[:, t, :]).then_inc(s_v, 1)
            dve.wait_ge(s_v, NT)
            nc.vector.memset(m8[:, :, K:8], -5.0).then_inc(s_v, 1)
            dve.wait_ge(s_v, NT + 1)
            for t in range(NT):
                nc.vector.match_replace(left[:, t, :], m8[:, t, :], pr[:, t, :], -1.0).then_inc(s_v, 1)
            dve.wait_ge(s_v, 2 * NT + 1)
            nc.vector.tensor_scalar(left[:], left[:], -1.0, None, ALU.is_equal).then_inc(s_v, 1)
            dve.wait_ge(s_v, 2 * NT + 2)
            nc.vector.tensor_tensor(cw[:].rearrange("p (t e) -> p t e", e=E), left[:], pr, ALU.mult)


def transpose_weights(nc, tag, ident, cw, E, cwT):
    NT = cwT.shape[1] // P
    NG = NT // 4
    with ExitStack() as ctx:
        parts = ctx.enter_context(nc.sbuf_tensor(tag + "parts", [P, NT, 2 * E], F32))
        high = ctx.enter_context(nc.sbuf_tensor(tag + "high", [P, NT, E], FR))
        tb = [ctx.enter_context(nc.psum_tensor(tag + f"wt{i}", [P, 512], F32)) for i in range(2)]
        s_h = ctx.enter_context(nc.semaphore(tag + "s_h"))
        s_p = ctx.enter_context(nc.semaphore(tag + "s_p"))
        s_t = ctx.enter_context(nc.semaphore(tag + "s_wt"))
        s_c = ctx.enter_context(nc.semaphore(tag + "s_c"))
        cw3 = cw[:].rearrange("p (t e) -> p t e", e=E)
        block = ctx.enter_context(nc.Block())

        @block.vector
        def _(dve):
            dve.wait_ge(s_h, 1)
            nc.vector.tensor_copy(parts[:, :, 0:E], high[:].bitcast(F32)).then_inc(s_p, 1)
            nc.vector.tensor_tensor(parts[:, :, E:], cw3, high[:].bitcast(F32), ALU.subtract).then_inc(s_p, 1)

        @block.tensor
        def _(pe):
            pe.wait_ge(s_p, 2)
            for g in range(NG):
                if g >= 2:
                    pe.wait_ge(s_c, g - 1)
                for k in range(4):
                    mm = nc.tensor.transpose(tb[g % 2][0:2 * E, k * P:(k + 1) * P], parts[:, 4 * g + k, :], ident[:])
                mm.then_inc(s_t, 1)

        @block.scalar
        def _(act):
            nc.scalar.activation(high[:], cw3, ACT.Copy).then_inc(s_h, 1)
            for g in range(NG):
                act.wait_ge(s_t, g + 1)
                nc.scalar.activation(cwT[:, g * 512:(g + 1) * 512], tb[g % 2][0:2 * E, :], ACT.Copy).then_inc(s_c, 1)


def experts(nc, tag, resid, ident, zT, cwT, E, up_src, down_src, shared):
    D, NG = P, zT[0].shape[1] // 512
    F = up_src[0].shape[2]
    gated = len(up_src) == 2
    steps = E * F // P + (1 if shared else 0)
    G = 2 if steps % 2 else 1
    SU = G * steps
    NU = NG // G
    LAG, RING = (2, 2) if gated else (3, 4)
    with ExitStack() as ctx:
        def sb(name, shape, dt=F32):
            return ctx.enter_context(nc.sbuf_tensor(tag + name, shape, dt))

        def sem(name):
            return ctx.enter_context(nc.semaphore(tag + name))

        def pb(name):
            return ctx.enter_context(nc.psum_tensor(tag + name, [P, 512], F32))

        sel = sb("sel", [2 * E, E * F], FR)
        ups = [[sb(f"up{i}_hi", [P, steps * P], FR), sb(f"up{i}_lo", [P, steps * P], FR)] for i in range(len(up_src))]
        down = [sb("down_hi", [P, steps * P], FR), sb("down_lo", [P, steps * P], FR)]
        with ExitStack() as c2:
            raw = [c2.enter_context(nc.sbuf_tensor(tag + f"raw{i}", [P, steps * P], F32)) for i in range(len(up_src) + 1)]
            self_ = c2.enter_context(nc.sbuf_tensor(tag + "sel32", [2 * E, E, F], F32))
            s_w = c2.enter_context(nc.semaphore(tag + "s_w"))
            s_hi = c2.enter_context(nc.semaphore(tag + "s_hi"))
            s_sel = c2.enter_context(nc.semaphore(tag + "s_sel"))
            block = c2.enter_context(nc.Block())

            @block.sync
            def _(sp):
                for r, src in zip(raw[:-1], up_src):
                    sp.dma_start(r[:, 0:E * F].rearrange("p (e f) -> p e f", f=F), src).then_inc(s_w, 16)
                sp.dma_start(raw[-1][:, 0:E * F].rearrange("p (s d) -> p s d", d=P), down_src).then_inc(s_w, 16)
                for r, src in zip(raw, shared or ()):
                    sp.dma_start(r[:, E * F:], src).then_inc(s_w, 16)

            @block.scalar
            def _(act):
                act.wait_ge(s_w, 16 * (len(raw) * (2 if shared else 1)))
                for r, (hi, _) in zip(raw, ups + [down]):
                    nc.scalar.activation(hi[:], r[:], ACT.Copy).then_inc(s_hi, 1)
                act.wait_ge(s_sel, 3)
                nc.scalar.activation(sel[:].rearrange("p (e f) -> p e f", f=F), self_[:], ACT.Copy)

            @block.vector
            def _(dve):
                for n, (r, (hi, lo)) in enumerate(zip(raw, ups + [down])):
                    dve.wait_ge(s_hi, n + 1)
                    nc.vector.tensor_tensor(lo[:], r[:], hi[:].bitcast(F32), ALU.subtract)

            @block.gpsimd
            def _(pool):
                nc.gpsimd.memset(self_[:], 0.0).then_inc(s_sel, 1)
                pool.wait_ge(s_sel, 1)
                nc.gpsimd.affine_select(out=self_[:], in_=self_[:], compare_op=ALU.not_equal, fill=1.0, base=0,
                                        pattern=[[-1, E], [0, F]], channel_multiplier=1).then_inc(s_sel, 1)
                pool.wait_ge(s_sel, 2)
                nc.gpsimd.affine_select(out=self_[:], in_=self_[:], compare_op=ALU.not_equal, fill=1.0, base=-E,
                                        pattern=[[-1, E], [0, F]], channel_multiplier=1).then_inc(s_sel, 1)

        act_out = [sb(f"silu{i}", [P, 512]) for i in range(2)]
        prod = [sb(f"prod{i}", [P, 512]) for i in range(2)]
        hid = [sb(f"hid{i}", [P, 512]) for i in range(2)]
        hh = [sb(f"hid_hi{i}", [P, 512], FR) for i in range(RING)]
        hl = [sb(f"hid_lo{i}", [P, 512], FR) for i in range(RING)]
        yT = sb("yT", [P, 512])
        gb = [pb(f"gate{i}") for i in range(2)]
        ub = [pb(f"up{i}") for i in range(2)] if gated else None
        cb = [pb(f"weight{i}") for i in range(2)]
        yb, tb = pb("y"), pb("t")
        s_g = sem("s_g")
        s_ucp = sem("s_up")
        s_si = sem("s_si")
        s_pr = sem("s_pr")
        s_hd = sem("s_hd")
        s_hi = sem("s_hi2")
        s_lo = sem("s_lo2")
        s_d = sem("s_d")
        s_yc = sem("s_yc")
        s_t = sem("s_yt")
        s_x = sem("s_x")

        def group_of(tile, s):
            u, c = tile
            k = s // steps
            return slice((c * G + k) * 512, (c * G + k + 1) * 512) if u is None else \
                bass.ds(u * (G * 512) + (c * G + k) * 512, 512)

        def norm(tile, s):
            return at(tile, s // SU), s % SU

        def on(tile):
            return live(tile, 0, NU)

        def schedule(clock, body):
            body((None, 0))
            with clock.eng.Fori(1, NU) as u:
                clock.enter(u)
                body((u, 0))
                clock.leave()
            body((None, NU))

        TLAG = 2
        AFTER = LAG + TLAG
        block = ctx.enter_context(nc.Block())

        @block.tensor
        def _(pe):
            c = Clock(pe, 1, {SU: range(-8, SU + 3), G: range(-3, G + 2)})

            def body(i):
                for s in range(SU):
                    if on(i):
                        cols = group_of(i, s)
                        m = s % steps
                        r = s % 2
                        w = slice(m * P, (m + 1) * P)
                        weighted = not (shared and m == steps - 1)
                        c.ge(s_si, SU, i, s - 1)
                        for b, (wp, zp) in enumerate(((0, 0), (0, 1), (1, 0))):
                            mm = nc.tensor.matmul(gb[r][:], ups[0][wp][:, w], zT[zp][:, cols], start=(b == 0), stop=(b == 2))
                        mm.then_inc(s_g, 1)
                        c.ge(s_hd, SU, i, s - 1, alone=not gated)
                        if gated:
                            for b, (wp, zp) in enumerate(((0, 0), (0, 1), (1, 0))):
                                mm = nc.tensor.matmul(ub[r][:], ups[1][wp][:, w], zT[zp][:, cols], start=(b == 0), stop=(b == 2))
                        if weighted:
                            mm = nc.tensor.matmul(cb[r][:], sel[:, w], cwT[:, cols], start=True, stop=True)
                        mm.then_inc(s_ucp, 1)
                    td, kd = norm(i, s - LAG)
                    if on(td):
                        m = kd % steps
                        w = slice(m * P, (m + 1) * P)
                        c.ge(s_lo, SU, td, kd + 1)
                        if m == 0:
                            c.ge(s_yc, G, td, kd // steps)
                        for b, (wp, h) in enumerate(((0, hh), (0, hl), (1, hh))):
                            mm = nc.tensor.matmul(yb[:], down[wp][:, w], h[kd % RING][:], start=(m == 0 and b == 0),
                                                  stop=(m == steps - 1 and b == 2))
                        mm.then_inc(s_d, 1)
                    ty, ky = norm(i, s - AFTER)
                    if on(ty) and ky % steps == steps - 1:
                        k = ky // steps
                        c.ge(s_yc, G, ty, k + 1)
                        c.ge(s_x, G, ty, k)
                        for b in range(4):
                            mm = nc.tensor.transpose(tb[:, b * P:(b + 1) * P], yT[:, b * P:(b + 1) * P], ident[:])
                        mm.then_inc(s_t, 1)
                    if not on(i) and i[1] == NU and s >= AFTER:
                        break
            schedule(c, body)

        @block.scalar
        def _(act):
            c = Clock(act, 1, {SU: range(-8, SU + 3), G: range(-3, G + 2)})

            def body(i):
                for s in range(SU):
                    if on(i):
                        c.ge(s_g, SU, i, s + 1)
                        c.ge(s_hd, SU, i, s - 1)
                        nc.scalar.activation(act_out[s % 2][:], gb[s % 2][:], ACT.Silu).then_inc(s_si, 1)
                    th, kh = norm(i, s - 1)
                    if on(th):
                        c.ge(s_hd, SU, th, kh + 1)
                        c.ge(s_d, SU, th, kh + 1 - RING)
                        nc.scalar.activation(hh[kh % RING][:], hid[kh % 2][:], ACT.Copy).then_inc(s_hi, 1)
                    ty, ky = norm(i, s - LAG)
                    if on(ty) and ky % steps == steps - 1:
                        c.ge(s_d, SU, ty, ky + 1)
                        c.ge(s_t, G, ty, ky // steps)
                        nc.scalar.activation(yT[:], yb[:], ACT.Copy).then_inc(s_yc, 1)
            schedule(c, body)

        @block.vector
        def _(dve):
            c = Clock(dve, 1, {SU: range(-8, SU + 3), G: range(-3, G + 2)})

            def body(i):
                for s in range(SU):
                    if on(i):
                        r = s % 2
                        weighted = not (shared and s % steps == steps - 1)
                        c.ge(s_si, SU, i, s + 1)
                        c.ge(s_ucp, SU, i, s + 1)
                        c.ge(s_lo, SU, i, s - 1)
                        first = hid[r] if not weighted else prod[r]
                        if gated:
                            mm = nc.vector.tensor_tensor(first[:], ub[r][:], act_out[r][:], ALU.mult)
                            if weighted:
                                mm.then_inc(s_pr, 1)
                                c.ge(s_pr, G * (steps - 1), i, s + 1 - s // steps)
                        if weighted:
                            src = prod[r] if gated else act_out[r]
                            mm = nc.vector.tensor_tensor(hid[r][:], cb[r][:], src[:], ALU.mult)
                        mm.then_inc(s_hd, 1)
                    ty, ky = norm(i, s - AFTER)
                    if on(ty) and ky % steps == steps - 1:
                        c.ge(s_t, G, ty, ky // steps + 1)
                        cols = group_of(ty, ky)
                        nc.vector.tensor_tensor(resid[:, cols], tb[:], resid[:, cols], ALU.add).then_inc(s_x, 1)
            if gated and shared:
                c.keys[G * (steps - 1)] = range(1, G * (steps - 1) + 1)
            schedule(c, body)

        @block.gpsimd
        def _(pool):
            c = Clock(pool, 1, {SU: range(-8, SU + 3)})

            def body(i):
                for s in range(SU):
                    th, kh = norm(i, s - 1)
                    if on(th):
                        c.ge(s_hi, SU, th, kh + 1)
                        nc.gpsimd.tensor_tensor(hl[kh % RING][:], hid[kh % 2][:], hh[kh % RING][:].bitcast(F32),
                                                ALU.subtract).then_inc(s_lo, 1)
            schedule(c, body)


def mixture(nc, A, tag, resid, ident, score_src, E, choose, up_src, down_src, shared):
    NT = resid.shape[1] // P
    with ExitStack() as ctx:
        def sb(name, shape, dt=F32):
            return ctx.enter_context(nc.sbuf_tensor(tag + name, shape, dt))
        zT = [sb(f"zT_{n}", [P, NT * P], FR) for n in ("hi", "lo")]
        cwT = sb("cwT", [2 * E, NT * P], FR)
        with ExitStack() as c2:
            def sb2(name, shape):
                return c2.enter_context(nc.sbuf_tensor(tag + name, shape, F32))
            z = sb2("z", [P, NT * P])
            logits = sb2("logits", [P, NT * E])
            cw = sb2("cw", [P, NT * E])
            norm_and_score(nc, tag + "ns_", resid, ident, score_src, E, z, logits, split=zT)
            softmax_rows(nc, tag + "sm_", logits, E, NT)
            choose(nc, tag + "ch_", ident, logits, cw)
            transpose_weights(nc, tag + "tw_", ident, cw, E, cwT)
        experts(nc, tag + "ex_", resid, ident, zT, cwT, E, up_src, down_src, shared)


def attention_constants(nc, A, ident, K):
    H, S = 16, 64
    DH = P // H
    with ExitStack() as ctx:
        def sb(name, shape, dt=F32):
            return ctx.enter_context(nc.sbuf_tensor("ac_" + name, shape, dt))

        def sem(name):
            return ctx.enter_context(nc.semaphore("ac_" + name))
        mask = sb("mask", [P, 64, S], I32)
        heads = sb("heads", [P, H])
        pairs = sb("pairs", [P, H // 2])
        bq, bk, wo = sb("bq", [P, 1]), sb("bk", [P, 1]), sb("wo", [P, P])
        s_mask = sem("s_mask")
        s_small = sem("s_small")
        s_in = sem("s_in")
        s_v = sem("s_v")
        block = ctx.enter_context(nc.Block())

        @block.sync
        def _(sp):
            with nc.allow_non_contiguous_dma(reason="one bias a partition"):
                sp.dma_start(bq[:], A["aq_b"].unsqueeze(1)).then_inc(s_small, 16)
                sp.dma_start(bk[:], A["ak_b"].unsqueeze(1)).then_inc(s_small, 16)
            sp.dma_start(wo[:], A["ao_w"]).then_inc(s_small, 16)
            for j in range(2):
                sp.dma_start(mask[j * S:(j + 1) * S], A["mask"].rearrange("b q k -> q b k")).then_inc(s_mask, 16)
            for j in range(2):
                sp.dma_start(K["gp"][j * S:(j + 1) * S], A["gp"].rearrange("b q k -> q b k")).then_inc(s_in, 16)
            sp.dma_start(K["ctx"][:], A["ctx"].rearrange("(t b) s d -> (b s) t d", b=2)).then_inc(s_in, 16)
            sp.dma_start(K["wq"][:], A["aq_w"]).then_inc(s_in, 16)
            sp.dma_start(K["wk"][:], A["ak_w"]).then_inc(s_in, 16)
            sp.dma_start(K["wv"][:], A["av_w"]).then_inc(s_in, 16)
            sp.dma_start(K["bv"][:], A["av_b"].partition_broadcast(P)).then_inc(s_in, 16)
            sp.dma_start(K["bo"][:], A["ao_b"].partition_broadcast(P)).then_inc(s_in, 16)
            sp.wait_ge(s_in, 8 * 16)

        @block.vector
        def _(dve):
            nc.vector.tensor_reduce(heads[:], ident[:].rearrange("p (h d) -> p h d", h=H), AX, ALU.add).then_inc(s_v, 1)
            dve.wait_ge(s_v, 1)
            nc.vector.tensor_reduce(K["jj"][:], heads[:].rearrange("p (a j) -> p j a", j=2), AX, ALU.add).then_inc(s_v, 1)
            nc.vector.tensor_reduce(pairs[:], heads[:].rearrange("p (a j) -> p a j", j=2), AX, ALU.add).then_inc(s_v, 1)
            dve.wait_ge(s_v, 3)
            nc.vector.tensor_reduce(K["jp"][:], pairs[:].rearrange("p (r j) -> p j r", j=2), AX, ALU.add).then_inc(s_v, 1)
            dve.wait_ge(s_small, 3 * 16)
            for j in range(2):
                nc.vector.tensor_scalar(K["wo"][:, j, :], wo[:], K["jj"][:, j:j + 1], None, ALU.mult)
            nc.vector.tensor_scalar(K["sq"][:], K["jj"][:], float(DH) ** -0.5, None, ALU.mult).then_inc(s_v, 1)
            dve.wait_ge(s_v, 5)
            nc.vector.tensor_scalar(K["bq"][:], K["sq"][:], bq[:], None, ALU.mult)
            nc.vector.tensor_scalar(K["bk"][:], K["jp"][:], bk[:], None, ALU.mult)
            for r in range(2):
                nc.vector.memset(K[f"vb{r}"][:], 0.0)
            dve.wait_ge(s_mask, 2 * 16)
            nc.vector.tensor_scalar(K["neg"][:], mask[:], -1.0, 1e9, ALU.add, ALU.mult)


def attention(nc, A, resid, ident, K):
    D, S, H = P, 64, 16
    NQ = resid.shape[1] // (2 * D)
    with ExitStack() as ctx:
        def sb(name, shape, dt=F32):
            return ctx.enter_context(nc.sbuf_tensor("at_" + name, shape, dt))

        def sem(name):
            return ctx.enter_context(nc.semaphore("at_" + name))

        def pb(name):
            return ctx.enter_context(nc.psum_tensor("at_" + name, [P, 512], F32))

        st, mv = sb("ln_stats", [P, 2, 6]), sb("ln_meanvar", [P, 2, 2])
        ve, rstd, mhalf = sb("ln_vareps", [P, 2]), sb("ln_rstd", [P, 2]), sb("minus_half", [P, 2])
        z = sb("z", [P, 2, D])
        cstage = sb("ctx_tiles", [P, 2, D])
        zT = sb("zT", [P, 256])
        ctxT = sb("ctxT", [P, 4, 2, S])
        qx = [sb(f"qx{i}", [P, 4, 2, S]) for i in range(2)]
        kx = [sb(f"kx{i}", [P, 4, 2, S]) for i in range(2)]
        vb = [K["vb0"], K["vb1"]]
        sm = [sb(f"scores{i}", [P, 4, 2, S]) for i in range(2)]
        mx = [sb(f"max{i}", [P, 4, 2]) for i in range(2)]
        ex = [sb(f"exp{i}", [P, 4, 2, S]) for i in range(2)]
        pg = [sb(f"probs{i}", [P, 4, 2, S]) for i in range(2)]
        pT = [sb(f"probsT{i}", [P, 512]) for i in range(2)]
        zs, rz = sb("exp_sum", [P, 4, 2]), sb("exp_rsum", [P, 4, 2])
        oT = sb("outT", [P, 2, 4, S])
        sbank, tbank = ([pb(f"{n}{i}") for i in range(2)] for n in ("ps_s", "ps_t"))
        obank, prep, qkbank, ybank = pb("ps_o"), pb("ps_prep"), pb("ps_qk"), pb("ps_y")

        s_half = sem("s_half")
        s_ln = sem("s_ln")
        s_rs = sem("s_rs")
        s_bo = sem("s_bo")
        s_cs = sem("s_cs")
        s_zt = sem("s_zt")
        s_ztc = sem("s_ztc")
        s_qk = sem("s_qk")
        s_qx = sem("s_qx")
        s_v = sem("s_v")
        s_vb = sem("s_vb")
        s_s = sem("s_s")
        s_ma = sem("s_ma")
        s_mx = sem("s_mx")
        s_sub = sem("s_sub")
        s_e = sem("s_e")
        s_sum = sem("s_sum")
        s_rz = sem("s_rz")
        s_gp = sem("s_gp")
        s_pn = sem("s_pn")
        s_t = sem("s_t")
        s_ptc = sem("s_ptc")
        s_pv = sem("s_pv")
        s_otc = sem("s_otc")
        s_y = sem("s_y")
        s_x = sem("s_x")

        def step(i, j):
            return at(i, j // 4), j % 4

        def quad_cols(q, width):
            u, c = q
            return slice(c * width, (c + 1) * width) if u is None else bass.ds(u * (2 * width) + c * width, width)

        def quad_batches(q):
            u, c = q
            return slice(4 * c, 4 * c + 4) if u is None else bass.ds(u * 8 + 4 * c, 4)

        def ctx_tiles(q):
            u, c = q
            return slice(2 * c, 2 * c + 2) if u is None else bass.ds(u * 4 + 2 * c, 2)

        def on_(q):
            return live(q, 0, NQ)

        def schedule(clock, body):
            for i in range(-2, 4):
                body((None, i))
            with clock.eng.Fori(2, NQ // 2 - 1) as u:
                clock.enter(u)
                body((u, 0))
                body((u, 1))
                clock.leave()
            for i in range(NQ - 2, NQ + 2):
                body((None, i))

        block = ctx.enter_context(nc.Block())

        @block.tensor
        def _(pe):
            c = Clock(pe, 2, KEYS["attention", "PE"])

            def body(i):
                for j in range(4):
                    if on_(i):
                        r = i[1] % 2
                        rows = slice(32 * j, 32 * j + 32)
                        if j == 0:
                            c.ge(s_qx, 4, i, 4)
                        c.ge(s_ma, 4, i, j - 1)
                        for b in range(4):
                            mm = nc.tensor.matmul(sbank[j % 2][:, b * P:(b + 1) * P], qx[r][rows, b], kx[r][rows, b],
                                                  start=True, stop=True)
                        mm.then_inc(s_s, 1)
                    tt, kt = step(i, j - 2)
                    if on_(tt):
                        c.ge(s_pn, 4, tt, kt + 1)
                        c.ge(s_ptc, 4, tt, kt - 1)
                        for b in range(4):
                            mm = nc.tensor.transpose(tbank[kt % 2][:, b * P:(b + 1) * P], pg[kt % 2][:, b], ident[:])
                        mm.then_inc(s_t, 1)
                    ti = at(i, 1)
                    if j == 0 and on_(ti):
                        c.ge(s_ln, 6, ti, 6)
                        c.ge(s_vb, 2, ti, 0)
                        c.ge(s_cs, 1, ti, 1)
                        for t in range(2):
                            nc.tensor.transpose(prep[:, t * P:(t + 1) * P], z[:, t], ident[:])
                        for t in range(2):
                            mm = nc.tensor.transpose(prep[:, (2 + t) * P:(3 + t) * P], cstage[:, t], ident[:])
                        mm.then_inc(s_zt, 1)
                    if j == 1 and on_(ti):
                        c.ge(s_ztc, 1, ti, 1)
                        c.ge(s_qx, 4, ti, 0)
                        nc.tensor.matmul(qkbank[:, 0:256], K["wq"][:], zT[:], start=True, stop=True)
                        nc.tensor.matmul(qkbank[:, 256:512], K["wk"][:], ctxT[:, :, 0, :], start=True, stop=True).then_inc(s_qk, 1)
                    if j == 2 and on_(ti):
                        for b in range(4):
                            mm = nc.tensor.matmul(prep[:, b * P:(b + 1) * P], ctxT[:, b], K["wv"][:], start=True, stop=True)
                        mm.then_inc(s_v, 1)
                    ty = at(i, -2)
                    if j == 0 and on_(ty):
                        c.ge(s_otc, 1, ty, 1)
                        c.ge(s_x, 1, ty, 0)
                        for t in range(2):
                            for jj in range(2):
                                mm = nc.tensor.matmul(ybank[:, t * P:(t + 1) * P], oT[:, jj, 2 * t:2 * t + 2, :],
                                                      K["wo"][:, jj, :], start=(jj == 0), stop=(jj == 1))
                        mm.then_inc(s_y, 1)
                    tv, kv = step(i, j - 3)
                    if on_(tv):
                        c.ge(s_ptc, 4, tv, kv + 1)
                        if kv == 0:
                            c.ge(s_vb, 2, tv, 2)
                            c.ge(s_otc, 1, tv, 0)
                        for b in range(4):
                            mm = nc.tensor.matmul(obank[32 * kv:32 * kv + 32, b * P:(b + 1) * P],
                                                  vb[tv[1] % 2][:, b, 32 * kv:32 * kv + 32],
                                                  pT[kv % 2][:, b * P:(b + 1) * P], start=True, stop=True)
                        mm.then_inc(s_pv, 1)
            schedule(c, body)

        @block.scalar
        def _(act):
            c = Clock(act, 2, KEYS["attention", "ACT"])

            def body(i):
                for j in range(4):
                    to = at(i, -1)
                    if j == 3 and on_(to):
                        c.ge(s_pv, 4, to, 4)
                        c.ge(s_y, 1, to, 0)
                        nc.scalar.activation(oT[:], obank[:].rearrange("p (b j s) -> p j b s", b=4, j=2),
                                             ACT.Copy).then_inc(s_otc, 1)
                    tt, kt = step(i, j - 2)
                    if on_(tt):
                        c.ge(s_t, 4, tt, kt + 1)
                        c.ge(s_pv, 4, tt, kt - 1)
                        nc.scalar.activation(pT[kt % 2][:], tbank[kt % 2][:], ACT.Copy).then_inc(s_ptc, 1)
                    ti = at(i, 1)
                    if j == 0 and on_(ti):
                        c.ge(s_zt, 1, ti, 1)
                        c.ge(s_v, 1, ti, 0)
                        nc.scalar.activation(zT[:], prep[:, 0:256], ACT.Copy)
                        nc.scalar.activation(ctxT[:], prep[:, 256:512].rearrange("p (b s) -> p b s", b=4).unsqueeze(2)
                                             .to_broadcast((P, 4, 2, S)), ACT.Copy).then_inc(s_ztc, 1)
                    if j == 1 and on_(ti):
                        c.ge(s_qk, 1, ti, 1)
                        r = ti[1] % 2
                        for k in range(2):
                            for dst, off, scale, bias in ((qx, 0, "sq", "bq"), (kx, 256, "jp", "bk")):
                                nc.scalar.activation(dst[r][:, :, k, :],
                                                     qkbank[:, off:off + 256].rearrange("p (b s) -> p b s", b=4),
                                                     ACT.Identity, bias=K[bias][:, k:k + 1],
                                                     scale=K[scale][:, k:k + 1]).then_inc(s_qx, 1)
                    if on_(i):
                        c.ge(s_sub, 4, i, j + 1)
                        c.ge(s_gp, 4, i, j - 1)
                        c.ge(s_sum, 4, i, j - 1)
                        nc.scalar.activation(ex[j % 2][:], sm[j % 2][:], ACT.Exp).then_inc(s_e, 1)
                    tc = at(i, 2)
                    if j == 3 and on_(tc):
                        c.ge(s_zt, 1, tc, 0)
                        nc.scalar.activation(cstage[:], K["ctx"][:, ctx_tiles(tc), :], ACT.Copy).then_inc(s_cs, 1)
            schedule(c, body)

        @block.vector
        def _(dve):
            c = Clock(dve, 2, KEYS["attention", "DVE"])

            def body(i):
                for j in range(4):
                    if on_(i):
                        c.ge(s_s, 4, i, j + 1)
                        c.ge(s_e, 4, i, j - 1)
                        neg = K["neg"][:, quad_batches(i), :].unsqueeze(2).to_broadcast((P, 4, 2, S))
                        nc.vector.tensor_tensor(sm[j % 2][:], sbank[j % 2][:].rearrange("p (b j s) -> p b j s", b=4, j=2),
                                                neg, ALU.add).then_inc(s_ma, 1)
                        c.ge(s_ma, 4, i, j + 1)
                        nc.vector.tensor_reduce(mx[j % 2][:], sm[j % 2][:], AX, ALU.max).then_inc(s_mx, 1)
                    ts, ks = step(i, j - 1)
                    if on_(ts):
                        c.ge(s_e, 4, ts, ks + 1)
                        nc.vector.tensor_reduce(zs[:], ex[ks % 2][:], AX, ALU.add).then_inc(s_sum, 1)
                        c.ge(s_sum, 4, ts, ks + 1)
                        nc.vector.reciprocal(rz[:], zs[:]).then_inc(s_rz, 1)
                        c.ge(s_rz, 4, ts, ks + 1)
                        c.ge(s_gp, 4, ts, ks + 1)
                        nc.vector.tensor_tensor(pg[ks % 2][:], pg[ks % 2][:],
                                                rz[:].unsqueeze(3).to_broadcast((P, 4, 2, S)), ALU.mult).then_inc(s_pn, 1)
                    tp = at(i, -1)
                    ti = at(i, 1)
                    if j == 3 and on_(ti):
                        c.ge(s_v, 1, ti, 1)
                        if live(tp, 0, NQ):
                            c.ge(s_pv, 4, tp, 4)
                        for jp in range(2):
                            rows = slice(jp * S, (jp + 1) * S)
                            src = prep[rows, :].rearrange("p (b r j e) -> p b r j e", b=4, r=4, j=2)[:, :, :, jp, :]
                            dst = vb[ti[1] % 2][rows].rearrange("p b (r j e) -> p b r j e", r=4, j=2)[:, :, :, jp, :]
                            bias = K["bv"][rows].rearrange("p (r j e) -> p r j e", r=4, j=2)[:, :, jp, :]
                            nc.vector.tensor_tensor(dst, src, bias.unsqueeze(1).to_broadcast((S, 4, 4, 16)),
                                                    ALU.add).then_inc(s_vb, 1)
                    ty = at(i, -2)
                    if j == 2 and on_(ty):
                        c.ge(s_y, 1, ty, 1)
                        c.ge(s_bo, 1, ty, 1)
                        cols = quad_cols(ty, 2 * D)
                        nc.vector.tensor_tensor(resid[:, cols], ybank[:, 0:256], resid[:, cols], ALU.add).then_inc(s_x, 1)
                    tl = at(i, 2)
                    if on_(tl) and j in (0, 2):
                        x = resid[:, quad_cols(tl, 2 * D)].rearrange("p (t d) -> p t d", t=2)
                        if j == 0:
                            for t in range(2):
                                nc.vector.bn_stats(st[:, t, :], x[:, t, :]).then_inc(s_ln, 1)
                            c.ge(s_ln, 6, tl, 2, alone=True)
                            for t in range(2):
                                nc.vector.bn_aggr(mv[:, t, :], st[:, t, :]).then_inc(s_ln, 1)
                        else:
                            c.ge(s_rs, 2, tl, 2)
                            c.ge(s_zt, 1, tl, 0)
                            for t in range(2):
                                nc.vector.tensor_scalar(z[:, t, :], x[:, t, :], mv[:, t, 0:1], rstd[:, t:t + 1],
                                                        ALU.subtract, ALU.mult).then_inc(s_ln, 1)
            schedule(c, body)

        @block.gpsimd
        def _(pool):
            c = Clock(pool, 2, KEYS["attention", "Pool"])
            nc.gpsimd.memset(mhalf[:], -0.5).then_inc(s_half, 1)
            pool.wait_ge(s_half, 1)

            def body(i):
                for j in range(4):
                    ts, ks = step(i, j - 1)
                    if on_(ts):
                        c.ge(s_e, 4, ts, ks + 1)
                        c.ge(s_t, 4, ts, ks - 1, alone=True)
                        gp = K["gp"][:, quad_batches(ts), :].unsqueeze(2).to_broadcast((P, 4, 2, S))
                        nc.gpsimd.tensor_tensor(pg[ks % 2][:], ex[ks % 2][:], gp, ALU.mult).then_inc(s_gp, 1)
                    if on_(i):
                        c.ge(s_mx, 4, i, j + 1)
                        nc.gpsimd.tensor_tensor(sm[j % 2][:], sm[j % 2][:],
                                                mx[j % 2][:].unsqueeze(3).to_broadcast((P, 4, 2, S)),
                                                ALU.subtract).then_inc(s_sub, 1)
                    tl = at(i, 2)
                    if on_(tl) and j == 1:
                        c.ge(s_ln, 6, tl, 4, alone=True)
                        nc.gpsimd.tensor_scalar(ve[:], mv[:, :, 1], EPS, None, ALU.add).then_inc(s_rs, 1)
                        c.ge(s_rs, 2, tl, 1)
                        nc.gpsimd.tensor_tensor(rstd[:], ve[:], mhalf[:], ALU.pow).then_inc(s_rs, 1)
                    if on_(tl) and j == 3:
                        c.ge(s_ln, 6, tl, 6, alone=True)
                        x = resid[:, quad_cols(tl, 2 * D)].rearrange("p (t d) -> p t d", t=2)
                        nc.gpsimd.tensor_tensor(x, x, K["bo"][:].unsqueeze(1).to_broadcast((P, 2, D)),
                                                ALU.add).then_inc(s_bo, 1)
            schedule(c, body)


def second_attention(nc, A, resid, ident):
    with ExitStack() as ctx:
        shapes = {"gp": [P, 64, 64], "neg": [P, 64, 64], "ctx": [P, 32, P], "wq": [P, P], "wk": [P, P], "wv": [P, P],
                  "bv": [P, P], "bo": [P, P], "jj": [P, 2], "jp": [P, 2], "sq": [P, 2], "bq": [P, 2], "bk": [P, 2],
                  "wo": [P, 2, P], "vb0": [P, 4, P], "vb1": [P, 4, P]}
        K = {k: ctx.enter_context(nc.sbuf_tensor("attn_" + k, s, F32)) for k, s in shapes.items()}
        attention_constants(nc, A, ident, K)
        attention(nc, A, resid, ident, K)

KEYS = {
    ("attention", "PE"): {1: range(-2, 4), 2: (2, 4), 4: (-3, -2, -1, 0, 1, 2, 3, 4, 5, 6, 8), 6: (12, 18)},
    ("attention", "ACT"): {1: range(-2, 4), 4: range(-3, 9)},
    ("attention", "DVE"): {1: range(-1, 4), 2: (6, 8), 4: range(-1, 9), 6: (14, 20)},
    ("attention", "Pool"): {2: (5, 7), 4: range(-2, 9), 6: (16, 18, 22, 24)},

    ("perceiver", "PE"): {1: range(-2, 4), 2: (0, 2, 4, 6, 8), 4: range(-4, 12)},
    ("perceiver", "ACT"): {1: (-2, -1, 0, 3, 4), 2: (4, 6), 4: range(-3, 13)},
    ("perceiver", "DVE"): {1: (-1, 0, 2, 3, 4), 2: (6, 8), 4: (*range(-2, 13), 14, 16, 18, 20),
                           12: (38, 40, 42, 44, 46, 50, 52, 54, 56, 58)},
    ("perceiver", "Pool"): {1: (1, 2), 2: range(2, 8), 4: (*range(-2, 8), 13, 15, 17, 19),
                            12: (36, 40, 46, 48, 52, 58)},
}


def store(nc, resid, out):
    with nc.semaphore("s_out") as s_out, nc.Block() as block:
        @block.sync
        def _(sp):
            sp.dma_start(out.rearrange("(t b) s d -> (b s) t d", b=2),
                         resid[:].rearrange("p (t d) -> p t d", d=P)).then_inc(s_out, 16)
            sp.wait_ge(s_out, 16)


def build(nc, A, out):
    NT = A["x"].shape[0] // 2
    with ExitStack() as ctx:
        def sb(name, shape, dt=F32):
            return ctx.enter_context(nc.sbuf_tensor(name, shape, dt))
        resid = sb("resid", [P, NT * P])
        ident = sb("ident", [P, P])
        with ExitStack() as c2:
            def sb2(name, shape, dt=F32):
                return c2.enter_context(nc.sbuf_tensor(name, shape, dt))
            kvraw = sb2("kvraw", [P, 2 * NT * P])
            wts = {k: sb2("fold_" + k, [P, 2048]) for k in ("A", "V")}
            wts["gain"] = sb2("ln_gain", [P, P])
            wts["shift"] = sb2("ln_shift", [P, P])
            fold_weights(nc, A, resid, kvraw, ident, wts)
            perceiver(nc, A, resid, kvraw, ident, wts)
        expert_choice(nc, A, resid, ident)
        second_attention(nc, A, resid, ident)
        mixture(nc, A, "f1_", resid, ident, A["Wr"], 16, choose_experts,
                [A["Wg"].rearrange("e d f -> d e f"), A["Wu"].rearrange("e d f -> d e f")],
                A["Wd"].rearrange("(p h) f d -> (h f) p d", h=2), (A["Sg"], A["Su"], A["Sd"]))
        store(nc, resid, out)


_NAMES = {"x": "x", "ctx": "ctx_1024", "gp": "fside_BxSxS2_0", "mask": "mask_BxSxS2_ik1",
          "ln_m_g": "L0_xattn_ln_m_g", "ln_m_b": "L0_xattn_ln_m_b", "ln_l_g": "L0_xattn_ln_l_g",
          "ln_l_b": "L0_xattn_ln_l_b", "wq": "L0_xattn_Wq", "wkv": "L0_xattn_Wkv", "wout": "L0_xattn_Wout",
          "cw": "L0_ffn_choice_w", "w1": "L0_ffn_w1", "w2": "L0_ffn_w2",
          "aq_w": "L1_xattn_wq_k", "aq_b": "L1_xattn_wq_b", "ak_w": "L1_xattn_wk_k", "ak_b": "L1_xattn_wk_b",
          "av_w": "L1_xattn_wv_k", "av_b": "L1_xattn_wv_b", "ao_w": "L1_xattn_wo_k", "ao_b": "L1_xattn_wo_b",
          "Wr": "L1_ffn_Wr", "Wg": "L1_ffn_Wg", "Wu": "L1_ffn_Wu", "Wd": "L1_ffn_Wd",
          "Sg": "L1_ffn_Sg", "Su": "L1_ffn_Su", "Sd": "L1_ffn_Sd"}


def kernel(**inputs):
    import numpy as _np
    import concourse.bacc as _bacc
    from concourse.bass_utils import run_bass_kernel_spmd as _run

    nc = _bacc.Bacc("TRN2", target_bir_lowering=False, num_devices=1)
    arrays, A = {}, {}
    for short, name in _NAMES.items():
        a = _np.ascontiguousarray(inputs[name])
        arrays["in_" + short] = a
        A[short] = nc.dram_tensor("in_" + short, a.shape, mybir.dt.from_np(a.dtype), kind="ExternalInput").ap()
    out = nc.dram_tensor("out", A["x"].shape, F32, kind="ExternalOutput").ap()
    build(nc, A, out)
    r = _run(nc, [arrays], core_ids=[0])
    return r.results[0]["out"]
```

```python
from contextlib import ExitStack

import concourse.bass as bass
from concourse import mybir

F32 = mybir.dt.float32
FR = mybir.dt.float32r
I32 = mybir.dt.int32
ALU = mybir.AluOpType
ACT = mybir.ActivationFunctionType
AX = mybir.AxisListType.X

P = 128
EPS = 1e-5


class Clock:

    def __init__(self, eng, step=1, keys=()):
        self.eng, self.step, self.keys, self.regs = eng, step, dict(keys), {}

    def enter(self, u):
        self.u, self.regs = u, {}
        for mul, add in ((per * self.step, add) for per, adds in self.keys.items() for add in adds):
            self.regs[mul, add] = self.eng.to_reg(u * mul + add if add else u * mul)

    def leave(self):
        self.regs = {}

    def ge(self, sem, per, tile, k, alone=False):
        u, c = tile
        if u is None:
            if per * c + k > 0:
                self.eng.wait_ge(sem, per * c + k)
            return
        key = (per * self.step, per * c + k)
        self.eng.wait_ge(sem, self.regs[key])
        if alone:
            self.eng.nop(nofuse=True)


def at(tile, d):
    return (tile[0], tile[1] + d)


def live(tile, lo, hi):
    return tile[0] is not None or lo <= tile[1] < hi


def is_tile(tile, n):
    return tile[0] is None and tile[1] == n


def build_identity(nc, eng, ident, made):
    eng.memset(ident[:], 0.0).then_inc(made, 1)
    eng.wait_ge(made, 1)
    eng.affine_select(out=ident[:], in_=ident[:], compare_op=ALU.not_equal, fill=1.0, base=0,
                      pattern=[[-1, P]], channel_multiplier=1).then_inc(made, 1)


def fold_weights(nc, ctx, A, ident, wts, bank):
    D, INNER = A["wq"].shape
    DH = 64
    H = INNER // DH

    def sb(name, shape, dt=F32):
        return ctx.enter_context(nc.sbuf_tensor(name, shape, dt))

    def sem(name):
        return ctx.enter_context(nc.semaphore(name))

    wq = sb("wq_raw", [D, INNER])
    wkv = sb("wkv_raw", [D, 2 * INNER])
    wo = sb("wo_raw", [P, INNER // P, D])
    wqT = sb("wqT", [P, H // 2, D])
    wkT = sb("wkT", [P, H // 2, D])
    wvT = sb("wvT", [P, H // 2, D])
    s_wq, s_wkv, s_wo = sem("s_wq"), sem("s_wkv"), sem("s_wo")
    s_wT = sem("s_wT")
    s_wTc = sem("s_wTc")
    s_prod = sem("s_prod")
    s_fold = sem("s_fold")
    NT = 3 * H // 8
    NP = 2 * H // 4

    def load(sp):
        sp.dma_start(wq[:], A["wq"]).then_inc(s_wq, 16)
        sp.dma_start(wkv[:], A["wkv"]).then_inc(s_wkv, 16)
        sp.dma_start(wo[:], A["wout"].rearrange("(t p) n -> p t n", p=P)).then_inc(s_wo, 16)

    def source(n):
        kind, half = n // (H // 8), n % (H // 8)
        src, off = [(wq, 0), (wkv, 0), (wkv, INNER)][kind]
        return src, off + half * 512, [wqT, wkT, wvT][kind][:, half * 4:half * 4 + 4, :]

    def multiply(pe):
        for n in range(NT):
            src, off, _ = source(n)
            pe.wait_ge(s_wq if n < H // 8 else s_wkv, 16)
            if n >= 2:
                pe.wait_ge(s_wTc, n - 1)
            for k in range(4):
                mm = nc.tensor.transpose(bank[n % 2][:, k * P:(k + 1) * P],
                                         src[:, off + k * P:off + (k + 1) * P], ident[:])
            mm.then_inc(s_wT, 1)
        pe.wait_ge(s_wTc, NT)
        pe.wait_ge(s_wo, 16)
        for n in range(NP):
            if n >= 2:
                pe.wait_ge(s_fold, n - 1)
            for k in range(4):
                q = n % (NP // 2)
                h = 8 * (q // 2) + 2 * k + q % 2
                r = slice((h % 2) * DH, (h % 2) * DH + DH)
                if n < NP // 2:
                    mm = nc.tensor.matmul(bank[n % 2][:, k * P:(k + 1) * P], wqT[r, h // 2, :],
                                          wkT[r, h // 2, :], start=True, stop=True)
                else:
                    mm = nc.tensor.matmul(bank[n % 2][:, k * P:(k + 1) * P], wvT[r, h // 2, :],
                                          wo[r, h // 2, :], start=True, stop=True)
            mm.then_inc(s_prod, 1)

    def folded(n):
        q = n % (NP // 2)
        name, scale = ("A", -float(DH) ** -0.5) if n < NP // 2 else ("V", 1.0)
        dst = wts[name][:].rearrange("p (g k e d) -> p g k e d", g=2, k=4, e=2)[:, q // 2, :, q % 2, :]
        return dst, scale

    def copy_out(act):
        for n in range(NT):
            act.wait_ge(s_wT, n + 1)
            nc.scalar.activation(source(n)[2], bank[n % 2][:].rearrange("p (a b) -> p a b", a=4),
                                 ACT.Copy).then_inc(s_wTc, 1)
        for n in range(NP):
            act.wait_ge(s_prod, n + 1)
            dst, scale = folded(n)
            nc.scalar.activation(dst, bank[n % 2][:].rearrange("p (k d) -> p k d", k=4), ACT.Copy,
                                 scale=scale).then_inc(s_fold, 1)

    return load, multiply, copy_out, (s_fold, NP)


def perceiver(nc, A, resid, kvraw, ident, wts):
    D, S, H = P, 64, 16
    NT = A["x"].shape[0] // 2
    with ExitStack() as ctx:
        def sb(name, shape, dt=F32):
            return ctx.enter_context(nc.sbuf_tensor(name, shape, dt))

        def sem(name):
            return ctx.enter_context(nc.semaphore(name))

        st = sb("ln_stats", [P, 2, 6])
        mv = sb("ln_meanvar", [P, 2, 2])
        ve = sb("ln_vareps", [P, 2])
        rstd = sb("ln_rstd", [P, 2])
        mhalf = sb("minus_half", [P, 2])
        kn = sb("kv_normed", [P, 2, D])
        kg = sb("kv_gained", [P, 2, D])
        kvf = sb("kv_full", [P, 2, 2, D])
        kvh = [sb(f"kv_hi{i}", [P, 2, D], FR) for i in range(2)]
        kvl = [sb(f"kv_lo{i}", [P, 2, D], FR) for i in range(2)]
        kvT = [sb(f"kvT{i}", [P, 2, P]) for i in range(2)]
        q = [sb(f"q{i}", [P, 2, H, S]) for i in range(2)]
        nmax = [sb(f"neg_max{i}", [P, 4]) for i in range(2)]
        zsum = [sb(f"exp_sum{i}", [P, 4]) for i in range(2)]
        rz = [sb(f"exp_rsum{i}", [P, 4]) for i in range(2)]
        pe_ = [sb(f"exp{i}", [P, 4, P]) for i in range(2)]
        pn = [sb(f"probs{i}", [P, 4, P]) for i in range(2)]
        pth = [sb(f"probsT_hi{i}", [P, 512], FR) for i in range(2)]
        ptl = [sb(f"probsT_lo{i}", [P, 512], FR) for i in range(2)]
        uT = [sb(f"uT{i}", [P, H, 2, S]) for i in range(2)]

        def pb(name):
            return ctx.enter_context(nc.psum_tensor(name, [P, 512], F32))
        sbank, tbank, ubank = ([pb(f"{n}{i}") for i in range(2)] for n in ("ps_s", "ps_t", "ps_u"))
        qbank, mbank = pb("ps_q"), pb("ps_m")

        load_weights, fold, copy_folded, (s_fold, FOLDED) = fold_weights(nc, ctx, A, ident, wts, tbank)
        s_ident = sem("s_ident")
        s_kin = [sem(f"s_kin{i}") for i in range(2)]
        s_gain = sem("s_gain")
        s_xin = sem("s_xin")
        s_half = sem("s_half")
        s_ln = sem("s_ln")
        s_rs = sem("s_rs")
        s_kv = sem("s_kv")
        s_kvt = sem("s_kvt")
        s_ktc = sem("s_ktc")
        s_kvl = sem("s_kvl")
        s_q = sem("s_q")
        s_qc = sem("s_qc")
        s_s = sem("s_s")
        s_mx = sem("s_mx")
        s_e = sem("s_e")
        s_rz = sem("s_rz")
        s_pn = sem("s_pn")
        s_t = sem("s_t")
        s_th = sem("s_th")
        s_tl = sem("s_tl")
        s_u = sem("s_u")
        s_uc = sem("s_uc")
        s_y = sem("s_y")
        s_x = sem("s_x")

        def chunk(i, j):
            return at(i, j // 4), j % 4

        def parts(k):
            return k % 2, k // 2

        def tile_cols(tile, width):
            u, c = tile
            return slice(c * width, (c + 1) * width) if u is None else bass.ds(u * (2 * width) + c * width, width)

        def on(tile):
            return live(tile, 0, NT)

        def schedule(clock, body):
            for i in range(-3, 4):
                body((None, i))
            with clock.eng.Fori(2, NT // 2 - 2) as u:
                clock.enter(u)
                body((u, 0))
                body((u, 1))
                clock.leave()
            for i in range(NT - 4, NT + 2):
                body((None, i))

        block = ctx.enter_context(nc.Block())

        EARLY = 4

        @block.sync
        def _(sp):
            load_weights(sp)
            kv = kvraw[:].rearrange("p (b d) -> p b d", d=D)

            def load_kv(b, done):
                sp.dma_start(kv[0:S, b], A["ctx"].rearrange("b s d -> s b d")[:, b]).then_inc(done, 16)
                sp.dma_start(kv[S:2 * S, b], A["x"].rearrange("b s d -> s b d")[:, b]).then_inc(done, 16)
            load_kv(slice(0, 2 * EARLY), s_kin[0])
            sp.dma_start(wts["gain"][0:S], A["ln_m_g"].partition_broadcast(S)).then_inc(s_gain, 16)
            sp.dma_start(wts["gain"][S:2 * S], A["ln_l_g"].partition_broadcast(S)).then_inc(s_gain, 16)
            sp.dma_start(wts["shift"][0:S], A["ln_m_b"].partition_broadcast(S)).then_inc(s_gain, 16)
            sp.dma_start(wts["shift"][S:2 * S], A["ln_l_b"].partition_broadcast(S)).then_inc(s_gain, 16)
            load_kv(slice(2 * EARLY, 2 * NT), s_kin[1])
            sp.dma_start(resid[:].rearrange("p (t d) -> p t d", d=D),
                         A["x"].rearrange("(t b) s d -> (b s) t d", b=2)).then_inc(s_xin, 16)

        @block.tensor
        def _(pe):
            pe.wait_ge(s_ident, 2)
            fold(pe)
            c = Clock(pe, 2, KEYS["perceiver", "PE"])

            def body(i):
                for j in range(4):
                    tt, kt = chunk(i, j - 2)
                    if on(tt):
                        c.ge(s_pn, 4, tt, kt + 1)
                        c.ge(s_tl, 4, tt, kt - 1)
                        for b in range(4):
                            mm = nc.tensor.transpose(tbank[kt % 2][:, b * P:(b + 1) * P], pn[kt % 2][:, b, :], ident[:])
                        mm.then_inc(s_t, 1)
                    if on(i):
                        b, g = parts(j)
                        r = i[1] % 2
                        c.ge(s_qc, 4, i, 2 * g + 2)
                        c.ge(s_e, 4, i, j - 1)
                        for k in range(4):
                            h = 8 * g + 2 * k
                            out = sbank[j % 2][:, k * P:(k + 1) * P]
                            mm = nc.tensor.matmul(out, q[r][:, b, h:h + 2, :], kvT[r][:, b, :], start=True, stop=True)
                        mm.then_inc(s_s, 1)
                    tu, ku = chunk(i, j - 3)
                    if on(tu):
                        b, g = parts(ku)
                        r = tu[1] % 2
                        c.ge(s_kvl, 2, tu, 2)
                        c.ge(s_tl, 4, tu, ku + 1)
                        c.ge(s_uc, 4, tu, ku - 1)
                        out = ubank[ku % 2][:]
                        nc.tensor.matmul(out, kvh[r][:, b, :], pth[ku % 2][:], start=True, stop=False)
                        nc.tensor.matmul(out, kvh[r][:, b, :], ptl[ku % 2][:], start=False, stop=False)
                        nc.tensor.matmul(out, kvl[r][:, b, :], pth[ku % 2][:], start=False, stop=True).then_inc(s_u, 1)
                    tq = at(i, 1)
                    if on(tq):
                        r = tq[1] % 2
                        if is_tile(tq, 0) and j == 0:
                            pe.wait_ge(s_fold, FOLDED)
                        c.ge(s_ktc, 1, tq, 1)
                        c.ge(s_qc, 4, tq, j)
                        for k in range(4):
                            h = 4 * j + k
                            out = qbank[:, k * P:(k + 1) * P]
                            mm = nc.tensor.matmul(out, wts["A"][:, h * P:(h + 1) * P], kvT[r][:, :, S:2 * S],
                                                  start=True, stop=True)
                        mm.then_inc(s_q, 1)
                    ty = at(i, -2)
                    if j < 3 and on(ty):
                        r = ty[1] % 2
                        if j == 0:
                            c.ge(s_uc, 4, ty, 4)
                            c.ge(s_x, 1, ty, 0)
                            if live(i, -3, NT - 1):
                                c.ge(s_ktc, 1, ty, 4)
                        for h in range(j * H // 3, (j + 1) * H // 3):
                            out = mbank[:, 0:D]
                            mm = nc.tensor.matmul(out, uT[r][:, h, :, :], wts["V"][:, h * P:(h + 1) * P],
                                                  start=(h == 0), stop=(h == H - 1))
                        if j == 2:
                            mm.then_inc(s_y, 1)
                    tk = at(i, 2)
                    if j == 3 and on(tk):
                        c.ge(s_kv, 2, tk, 2)
                        c.ge(s_x, 1, tk, -3)
                        for b in range(2):
                            mm = nc.tensor.transpose(mbank[:, b * P:(b + 1) * P], kvf[:, tk[1] % 2, b, :], ident[:])
                        mm.then_inc(s_kvt, 1)
            schedule(c, body)

        @block.scalar
        def _(act):
            copy_folded(act)
            c = Clock(act, 2, KEYS["perceiver", "ACT"])

            def body(i):
                for j in range(4):
                    tk = at(i, 1)
                    if j == 0 and on(tk):
                        c.ge(s_kvt, 1, tk, 1)
                        c.ge(s_s, 4, tk, -4)
                        nc.scalar.activation(kvT[tk[1] % 2][:], mbank[:, 0:2 * P].rearrange("p (b k) -> p b k", b=2),
                                             ACT.Copy).then_inc(s_ktc, 1)
                    tt, kt = chunk(i, j - 2)
                    if on(tt):
                        c.ge(s_t, 4, tt, kt + 1)
                        c.ge(s_u, 4, tt, kt - 1)
                        nc.scalar.activation(pth[kt % 2][:], tbank[kt % 2][:], ACT.Copy).then_inc(s_th, 1)
                    if on(i):
                        c.ge(s_mx, 4, i, j + 1)
                        c.ge(s_pn, 4, i, j - 1)
                        for k in range(4):
                            e = nc.scalar.activation(pe_[j % 2][:, k, :], sbank[j % 2][:, k * P:(k + 1) * P], ACT.Exp,
                                                     bias=nmax[j % 2][:, k:k + 1], scale=-1.0,
                                                     accum_out=zsum[j % 2][:, k:k + 1])
                        e.then_inc(s_e, 1)
                    tu, ku = chunk(i, j - 3)
                    if on(tu):
                        b, g = parts(ku)
                        c.ge(s_u, 4, tu, ku + 1)
                        c.ge(s_y, 1, tu, -1)
                        nc.scalar.activation(uT[tu[1] % 2][:, 8 * g:8 * g + 8, b, :],
                                             ubank[ku % 2][:].rearrange("p (h s) -> p h s", s=S),
                                             ACT.Copy).then_inc(s_uc, 1)
            schedule(c, body)

        @block.vector
        def _(dve):
            c = Clock(dve, 2, KEYS["perceiver", "DVE"])

            def body(i):
                for j in range(4):
                    ty = at(i, -2)
                    if j == 3 and on(ty):
                        cols = tile_cols(ty, D)
                        if is_tile(ty, 0):
                            dve.wait_ge(s_xin, 16)
                        c.ge(s_y, 1, ty, 1)
                        nc.vector.tensor_tensor(resid[:, cols], mbank[:, 0:D], resid[:, cols], ALU.add).then_inc(s_x, 1)
                    if on(i):
                        c.ge(s_s, 4, i, j + 1)
                        c.ge(s_e, 4, i, j - 1)
                        nc.vector.tensor_reduce(nmax[j % 2][:], sbank[j % 2][:].rearrange("p (a b) -> p a b", a=4),
                                                AX, ALU.min).then_inc(s_mx, 1)
                    tk = at(i, 2)
                    tr, kr = chunk(i, j - 1)
                    if on(tr):
                        c.ge(s_e, 4, tr, kr + 1)
                        c.ge(s_pn, 4, tr, kr - 1)
                        nc.vector.reciprocal(rz[kr % 2][:], zsum[kr % 2][:]).then_inc(s_rz, 1)
                    tt, kt = chunk(i, j - 2)
                    if on(tt):
                        c.ge(s_th, 4, tt, kt + 1)
                        nc.vector.tensor_tensor(ptl[kt % 2][:], tbank[kt % 2][:], pth[kt % 2][:].bitcast(F32),
                                                ALU.subtract).then_inc(s_tl, 1)
                    tq = at(i, 1)
                    if on(tq):
                        c.ge(s_q, 4, tq, j + 1)
                        nc.vector.tensor_copy(q[tq[1] % 2][:, :, 4 * j:4 * j + 4, :],
                                              qbank[:].rearrange("p (h b s) -> p b h s", h=4, b=2)).then_inc(s_qc, 1)
                    tl = at(i, 3)
                    if on(tl) and j == 0:
                        cols = tile_cols(tl, 2 * D)
                        raw = kvraw[:, cols].rearrange("p (b d) -> p b d", b=2)
                        if is_tile(tl, 0) or is_tile(tl, EARLY):
                            dve.wait_ge(s_kin[tl[1] // EARLY], 2 * 16)
                        for b in range(2):
                            nc.vector.bn_stats(st[:, b, :], raw[:, b, :]).then_inc(s_ln, 1)
                        c.ge(s_ln, 12, tl, 2, alone=True)
                        for b in range(2):
                            nc.vector.bn_aggr(mv[:, b, :], st[:, b, :]).then_inc(s_ln, 1)
                    if on(tl) and j == 2:
                        cols = tile_cols(tl, 2 * D)
                        raw = kvraw[:, cols].rearrange("p (b d) -> p b d", b=2)
                        c.ge(s_ln, 12, tl, 4)
                        c.ge(s_rs, 4, tl, 2)
                        c.ge(s_kv, 2, tl, 0)
                        for b in range(2):
                            nc.vector.tensor_scalar(kn[:, b, :], raw[:, b, :], mv[:, b, 0:1], rstd[:, b:b + 1],
                                                    ALU.subtract, ALU.mult).then_inc(s_ln, 1)
                        c.ge(s_ln, 12, tl, 6)
                        for b in range(2):
                            nc.vector.bn_stats(st[S:P, b, :], kn[S:P, b, :]).then_inc(s_ln, 1)
                        c.ge(s_ln, 12, tl, 8, alone=True)
                        for b in range(2):
                            nc.vector.bn_aggr(mv[S:P, b, :], st[S:P, b, :]).then_inc(s_ln, 1)
                    if on(tl) and j == 3:
                        c.ge(s_ln, 12, tl, 10)
                        c.ge(s_rs, 4, tl, 4)
                        for b in range(2):
                            nc.vector.tensor_scalar(kn[S:P, b, :], kn[S:P, b, :], mv[S:P, b, 0:1], rstd[S:P, b:b + 1],
                                                    ALU.subtract, ALU.mult).then_inc(s_ln, 1)
            schedule(c, body)

        @block.gpsimd
        def _(pool):
            c = Clock(pool, 2, KEYS["perceiver", "Pool"])
            build_identity(nc, nc.gpsimd, ident, s_ident)
            nc.gpsimd.memset(mhalf[:], -0.5).then_inc(s_half, 1)
            pool.wait_ge(s_half, 1)
            pool.wait_ge(s_gain, 4 * 16)

            def body(i):
                for j in range(4):
                    tn, kn_ = chunk(i, j - 1)
                    if on(tn):
                        c.ge(s_rz, 4, tn, kn_ + 1)
                        c.ge(s_t, 4, tn, kn_ - 1)
                        nc.gpsimd.tensor_tensor(pn[kn_ % 2][:], pe_[kn_ % 2][:],
                                                rz[kn_ % 2][:].unsqueeze(2).to_broadcast((P, 4, P)),
                                                ALU.mult).then_inc(s_pn, 1)
                    tl = at(i, 3)
                    if on(tl) and j == 0:
                        c.ge(s_ln, 12, tl, 4, alone=True)
                        nc.gpsimd.tensor_scalar(ve[:], mv[:, :, 1], EPS, None, ALU.add).then_inc(s_rs, 1)
                        c.ge(s_rs, 4, tl, 1)
                        nc.gpsimd.tensor_tensor(rstd[:], ve[:], mhalf[:], ALU.pow).then_inc(s_rs, 1)
                    if on(tl) and j == 2:
                        c.ge(s_ln, 12, tl, 10, alone=True)
                        nc.gpsimd.tensor_scalar(ve[:], mv[:, :, 1], EPS, None, ALU.add).then_inc(s_rs, 1)
                        c.ge(s_rs, 4, tl, 3)
                        nc.gpsimd.tensor_tensor(rstd[:], ve[:], mhalf[:], ALU.pow).then_inc(s_rs, 1)
                    tk = at(i, 2)
                    if on(tk) and j == 0:
                        c.ge(s_ln, 12, tk, 12)
                        nc.gpsimd.tensor_tensor(kg[:], kn[:], wts["gain"][:].unsqueeze(1).to_broadcast((P, 2, D)),
                                                ALU.mult).then_inc(s_kv, 1)
                        c.ge(s_kv, 2, tk, 1)
                        c.ge(s_kvl, 2, tk, -2)
                        c.ge(s_kvt, 1, tk, -1)
                        nc.gpsimd.tensor_tensor(kvf[:, tk[1] % 2], kg[:], wts["shift"][:].unsqueeze(1).to_broadcast((P, 2, D)),
                                                ALU.add).then_inc(s_kv, 1)
                    tq = at(i, 1)
                    if j == 3 and on(tq):
                        r = tq[1] % 2
                        c.ge(s_kv, 2, tq, 2)
                        c.ge(s_u, 4, tq, -4, alone=True)
                        nc.gpsimd.tensor_copy(kvh[r][:], kvf[:, r]).then_inc(s_kvl, 1)
                        c.ge(s_kvl, 2, tq, 1)
                        nc.gpsimd.tensor_tensor(kvl[r][:], kvf[:, r], kvh[r][:].bitcast(F32),
                                                ALU.subtract).then_inc(s_kvl, 1)
            schedule(c, body)


def norm_and_score(nc, tag, resid, ident, score_src, E, z, logits, split=None, loads=None):
    D = P
    NG = resid.shape[1] // (4 * D)
    with ExitStack() as ctx:
        def sb(name, shape, dt=F32):
            return ctx.enter_context(nc.sbuf_tensor(tag + name, shape, dt))

        def sem(name):
            return ctx.enter_context(nc.semaphore(tag + name))

        w = sb("w_score", [P, E])
        st = [sb(f"st{i}", [P, 4, 6]) for i in range(2)]
        mv = [sb(f"mv{i}", [P, 4, 2]) for i in range(2)]
        ve = [sb(f"ve{i}", [P, 4]) for i in range(2)]
        rstd = [sb(f"rstd{i}", [P, 4]) for i in range(2)]
        mhalf = sb("mhalf", [P, 4])
        zT = [sb(f"zT{i}", [P, 512]) for i in range(2)]
        tb = [ctx.enter_context(nc.psum_tensor(tag + f"tb{i}", [P, 512], F32)) for i in range(2)]
        lb = [ctx.enter_context(nc.psum_tensor(tag + f"lb{i}", [P, 512], F32)) for i in range(2)]
        s_w = sem("s_w")
        s_half = sem("s_half")
        s_ln = sem("s_ln")
        s_rs = sem("s_rs")
        s_t = sem("s_t")
        s_tc = sem("s_tc")
        s_lo = sem("s_lo")
        s_l = sem("s_l")
        s_lc = sem("s_lc")
        x3 = resid[:].rearrange("p (t d) -> p t d", d=D)
        z3 = z[:].rearrange("p (t d) -> p t d", d=D)
        block = ctx.enter_context(nc.Block())

        @block.sync
        def _(sp):
            if score_src.shape[1] == E:
                sp.dma_start(w[:], score_src).then_inc(s_w, 16)
            else:
                with nc.allow_non_contiguous_dma(reason="the small scoring matrix, transposed once"):
                    sp.dma_start(w[:], score_src.rearrange("e d -> d e")).then_inc(s_w, 16)

            if loads:
                loads(sp)

        @block.gpsimd
        def _(pool):
            nc.gpsimd.memset(mhalf[:], -0.5).then_inc(s_half, 1)
            pool.wait_ge(s_half, 1)
            for g in range(NG):
                pool.wait_ge(s_ln, 12 * g + 4 if g else 8)
                nc.gpsimd.tensor_scalar(ve[g % 2][:], mv[g % 2][:, :, 1], EPS, None, ALU.add).then_inc(s_rs, 1)
                pool.wait_ge(s_rs, 2 * g + 1)
                nc.gpsimd.tensor_tensor(rstd[g % 2][:], ve[g % 2][:], mhalf[:], ALU.pow).then_inc(s_rs, 1)

        @block.vector
        def _(dve):
            def stats(g):
                base = 0 if g == 0 else 12 * g - 4
                for k in range(4):
                    nc.vector.bn_stats(st[g % 2][:, k, :], x3[:, 4 * g + k, :]).then_inc(s_ln, 1)
                dve.wait_ge(s_ln, base + 4)
                for k in range(4):
                    nc.vector.bn_aggr(mv[g % 2][:, k, :], st[g % 2][:, k, :]).then_inc(s_ln, 1)

            def lo(g):
                dve.wait_ge(s_tc, 2 * g + 2)
                hi, low = (s[:, g * 512:(g + 1) * 512] for s in split)
                nc.vector.tensor_tensor(low, tb[g % 2][:], hi.bitcast(F32), ALU.subtract).then_inc(s_lo, 1)

            stats(0)
            for g in range(NG):
                if g + 1 < NG:
                    stats(g + 1)
                dve.wait_ge(s_rs, 2 * g + 2)
                for k in range(4):
                    nc.vector.tensor_scalar(z3[:, 4 * g + k, :], x3[:, 4 * g + k, :], mv[g % 2][:, k, 0:1],
                                            rstd[g % 2][:, k:k + 1], ALU.subtract, ALU.mult).then_inc(s_ln, 1)
                if split and g >= 1:
                    lo(g - 1)
            if split:
                lo(NG - 1)

        def normed(g):
            return 12 * (g + 2) - 4 if g + 1 < NG else 12 * NG

        @block.tensor
        def _(pe):
            def score(g):
                if g == 0:
                    pe.wait_ge(s_w, 16)
                pe.wait_ge(s_tc, (2 if split else 1) * g + 1)
                if g >= 2:
                    pe.wait_ge(s_lc, g - 1)
                for k in range(4):
                    mm = nc.tensor.matmul(lb[g % 2][:, k * E:(k + 1) * E], zT[g % 2][:, k * P:(k + 1) * P], w[:],
                                          start=True, stop=True)
                mm.then_inc(s_l, 1)

            for g in range(NG):
                pe.wait_ge(s_ln, normed(g))
                if g >= 2:
                    pe.wait_ge(s_lo if split else s_tc, g - 1)
                for k in range(4):
                    mm = nc.tensor.transpose(tb[g % 2][:, k * P:(k + 1) * P], z3[:, 4 * g + k, :], ident[:])
                mm.then_inc(s_t, 1)
                if g >= 1:
                    score(g - 1)
            score(NG - 1)

        @block.scalar
        def _(act):
            def out(g):
                act.wait_ge(s_l, g + 1)
                nc.scalar.activation(logits[:, g * 4 * E:(g + 1) * 4 * E], lb[g % 2][:, 0:4 * E],
                                     ACT.Copy).then_inc(s_lc, 1)

            for g in range(NG):
                act.wait_ge(s_t, g + 1)
                if g >= 2:
                    act.wait_ge(s_l, g - 1)
                nc.scalar.activation(zT[g % 2][:], tb[g % 2][:], ACT.Copy).then_inc(s_tc, 1)
                if split:
                    nc.scalar.activation(split[0][:, g * 512:(g + 1) * 512], tb[g % 2][:], ACT.Copy).then_inc(s_tc, 1)
                if g >= 1:
                    out(g - 1)
            out(NG - 1)


def softmax_rows(nc, tag, logits, E, NTL):
    with ExitStack() as ctx:
        mx = ctx.enter_context(nc.sbuf_tensor(tag + "mx", [P, NTL], F32))
        sm = ctx.enter_context(nc.sbuf_tensor(tag + "sm", [P, NTL], F32))
        rs = ctx.enter_context(nc.sbuf_tensor(tag + "rs", [P, NTL], F32))
        s_v = ctx.enter_context(nc.semaphore(tag + "s_v"))
        s_a = ctx.enter_context(nc.semaphore(tag + "s_a"))
        lg = logits[:].rearrange("p (t e) -> p t e", e=E)
        block = ctx.enter_context(nc.Block())

        @block.vector
        def _(dve):
            nc.vector.tensor_reduce(mx[:], lg, AX, ALU.max).then_inc(s_v, 1)
            dve.wait_ge(s_v, 1)
            nc.vector.tensor_tensor(lg, lg, mx[:].unsqueeze(2).to_broadcast((P, NTL, E)), ALU.subtract).then_inc(s_v, 1)
            dve.wait_ge(s_a, 1)
            nc.vector.tensor_reduce(sm[:], lg, AX, ALU.add).then_inc(s_v, 1)
            dve.wait_ge(s_v, 3)
            nc.vector.reciprocal(rs[:], sm[:]).then_inc(s_v, 1)
            dve.wait_ge(s_v, 4)
            nc.vector.tensor_tensor(lg, lg, rs[:].unsqueeze(2).to_broadcast((P, NTL, E)), ALU.mult).then_inc(s_v, 1)

        @block.scalar
        def _(act):
            act.wait_ge(s_v, 2)
            nc.scalar.activation(logits[:], logits[:], ACT.Exp).then_inc(s_a, 1)




def choose_tokens(nc, tag, ident, probs, pos):
    S, K = 64, 16
    with ExitStack() as ctx:
        def sb(name, shape, dt=F32):
            return ctx.enter_context(nc.sbuf_tensor(tag + name, shape, dt))

        def sem(name):
            return ctx.enter_context(nc.semaphore(tag + name))
        pT = sb("pT", [P, 4, S])
        w = [sb(f"left{i}", [P, 4, S]) for i in range(2)]
        m8 = [sb(f"best{i}", [P, 4, 8]) for i in range(2)]
        ones = sb("ones", [P, S])
        cum = sb("cum", [P, 4, S])
        tb = [ctx.enter_context(nc.psum_tensor(tag + f"tb{i}", [P, 512], F32)) for i in range(2)]
        s_pt = sem("s_pt")
        s_ptc = sem("s_ptc")
        s_one = sem("s_one")
        s_v = sem("s_v")
        s_ct = sem("s_ct")
        block = ctx.enter_context(nc.Block())

        @block.tensor
        def _(pe):
            for g in range(2):
                mm = nc.tensor.transpose(tb[0][:, g * P:(g + 1) * P], probs[:, g * P:(g + 1) * P], ident[:])
            mm.then_inc(s_pt, 1)
            pe.wait_ge(s_v, 22)
            for g in range(2):
                mm = nc.tensor.transpose(tb[1][:, g * P:(g + 1) * P], w[0][:, 2 * g:2 * g + 2, :], ident[:])
            mm.then_inc(s_ct, 1)

        @block.scalar
        def _(act):
            act.wait_ge(s_pt, 1)
            nc.scalar.activation(pT[:], tb[0][:, 0:2 * P].rearrange("p (c s) -> p c s", c=4), ACT.Copy).then_inc(s_ptc, 1)
            act.wait_ge(s_ct, 1)
            nc.scalar.activation(pos[:], tb[1][:, 0:2 * P], ACT.Copy)

        @block.gpsimd
        def _(pool):
            nc.gpsimd.memset(ones[:], 1.0).then_inc(s_one, 1)

        @block.vector
        def _(dve):
            dve.wait_ge(s_ptc, 1)
            src = pT
            for r in range(K // 8):
                for c in range(4):
                    nc.vector.max(m8[r][:, c, :], src[:, c, :]).then_inc(s_v, 1)
                dve.wait_ge(s_v, 8 * r + 4)
                for c in range(4):
                    nc.vector.match_replace(w[r][:, c, :], m8[r][:, c, :], src[:, c, :], -1.0).then_inc(s_v, 1)
                dve.wait_ge(s_v, 8 * r + 8)
                src = w[r]
            nc.vector.tensor_scalar(w[1][:], w[1][:], -1.0, None, ALU.is_equal).then_inc(s_v, 1)
            dve.wait_ge(s_v, 17)
            dve.wait_ge(s_one, 1)
            for c in range(4):
                nc.vector.tensor_tensor_scan(cum[:, c, :], ones[:], w[1][:, c, :], 0.0, ALU.mult,
                                             ALU.add).then_inc(s_v, 1)
            dve.wait_ge(s_v, 21)
            nc.vector.tensor_tensor(w[0][:], cum[:], w[1][:], ALU.mult).then_inc(s_v, 1)


def gather_tokens(nc, A, tag, z, pos, oh, xg, wts):
    E, K, S, D = 8, 16, 64, P
    NT = z.shape[1] // D
    CH = 8
    with ExitStack() as ctx:
        def sb(name, shape, dt=F32):
            return ctx.enter_context(nc.sbuf_tensor(tag + name, shape, dt))

        def sem(name):
            return ctx.enter_context(nc.semaphore(tag + name))
        zh, zl = sb("z_hi", [P, NT * D], FR), sb("z_lo", [P, NT * D], FR)
        iota = sb("iota", [P, K])
        raw = sb("w_raw", [P, 2048])
        bank = [[ctx.enter_context(nc.psum_tensor(tag + f"ps{i}{b}", [P, 512], F32)) for b in range(2)] for i in range(2)]
        s_w = sem("s_w")
        s_wh = sem("s_wh")
        s_wl = sem("s_wl")
        s_io = sem("s_io")
        s_zh = sem("s_zh")
        s_zl = sem("s_zl")
        s_oh = sem("s_oh")
        s_g = sem("s_g")
        s_ga = sem("s_ga")
        s_gv = sem("s_gv")
        block = ctx.enter_context(nc.Block())

        @block.sync
        def _(sp):
            sp.dma_start(raw[:].rearrange("p (e f) -> p e f", e=E), A["w1"].rearrange("e d f -> d e f")).then_inc(s_w, 16)
            sp.wait_ge(s_wl, 1)
            sp.dma_start(raw[:].rearrange("p (e d) -> p e d", d=D),
                         A["w2"].rearrange("e (c f) d -> f (e c) d", c=2)).then_inc(s_w, 16)

        @block.gpsimd
        def _(pool):
            nc.gpsimd.iota(iota[:], pattern=[[1, K]], base=1, channel_multiplier=0,
                           allow_small_or_imprecise_dtypes=True).then_inc(s_io, 1)
            for c in range(CH):
                cols = slice(c * 512, (c + 1) * 512)
                pool.wait_ge(s_zh, c + 1)
                nc.gpsimd.tensor_tensor(zl[:, cols], z[:, cols], zh[:, cols].bitcast(F32), ALU.subtract).then_inc(s_zl, 1)
                if c in (CH // 2, CH - 1):
                    k = c // (CH - 1)
                    pool.wait_ge(s_wh, k + 1)
                    nc.gpsimd.tensor_tensor(wts[k][1][:], raw[:], wts[k][0][:].bitcast(F32), ALU.subtract).then_inc(s_wl, 1)

        @block.tensor
        def _(pe):
            for t in range(NT):
                if t % 4 == 0:
                    pe.wait_ge(s_zl, t // 4 + 1)
                    pe.wait_ge(s_oh, t // 4 + 1)
                if t >= 2:
                    pe.wait_ge(s_ga, t - 1)
                    pe.wait_ge(s_gv, t - 1)
                for b in range(2):
                    rows = slice(b * S, (b + 1) * S)
                    for k, part in enumerate((zh, zl)):
                        mm = nc.tensor.matmul(bank[t % 2][b][:, k * P:(k + 1) * P], part[rows, t * D:(t + 1) * D],
                                              oh[rows, t, :, :], start=True, stop=True)
                mm.then_inc(s_g, 1)

        @block.scalar
        def _(act):
            def high(c):
                cols = slice(c * 512, (c + 1) * 512)
                nc.scalar.activation(zh[:, cols], z[:, cols], ACT.Copy).then_inc(s_zh, 1)
            high(0)
            high(1)
            for t in range(NT):
                if t % 4 == 0 and t // 4 + 2 < CH:
                    high(t // 4 + 2)
                if t in (NT // 3, 2 * NT // 3):
                    k = 0 if t == NT // 3 else 1
                    act.wait_ge(s_w, 16 * (k + 1))
                    nc.scalar.activation(wts[k][0][:], raw[:], ACT.Copy).then_inc(s_wh, 1)
                act.wait_ge(s_g, t + 1)
                nc.scalar.activation(xg[:, :, 2 * t, :], bank[t % 2][0][:, 0:2 * P].rearrange("p (e j) -> p e j", j=K),
                                     ACT.Copy).then_inc(s_ga, 1)

        @block.vector
        def _(dve):
            def one_hot(c):
                rows = slice(4 * c, 4 * c + 4)
                nc.vector.tensor_tensor(oh[:, rows].rearrange("p t e j -> p (t e) j"),
                                        pos[:, 4 * c * E:(4 * c + 4) * E].unsqueeze(2).to_broadcast((P, 4 * E, K)),
                                        iota[:].unsqueeze(1).to_broadcast((P, 4 * E, K)), ALU.is_equal).then_inc(s_oh, 1)
            dve.wait_ge(s_io, 1)
            one_hot(0)
            for t in range(NT):
                if t % 4 == 0 and t // 4 + 1 < CH:
                    one_hot(t // 4 + 1)
                dve.wait_ge(s_g, t + 1)
                nc.vector.tensor_copy(xg[:, :, 2 * t + 1, :],
                                      bank[t % 2][1][:, 0:2 * P].rearrange("p (e j) -> p e j", j=K)).then_inc(s_gv, 1)


def run_experts(nc, tag, xg, wts, yT):
    E, K, NB = 8, 16, xg.shape[2]
    GB = 512 // K
    NS = (NB // GB) * E * 2
    LAG = 2
    with ExitStack() as ctx:
        def sb(name, shape, dt=F32):
            return ctx.enter_context(nc.sbuf_tensor(tag + name, shape, dt))

        def sem(name):
            return ctx.enter_context(nc.semaphore(tag + name))
        h32 = [sb(f"hid{i}", [P, 512]) for i in range(2)]
        hh = [sb(f"hid_hi{i}", [P, 512], FR) for i in range(3)]
        hl = [sb(f"hid_lo{i}", [P, 512], FR) for i in range(3)]
        hb = [ctx.enter_context(nc.psum_tensor(tag + f"ps_h{i}", [P, 512], F32)) for i in range(3)]
        yb = [ctx.enter_context(nc.psum_tensor(tag + f"ps_y{i}", [P, 512], F32)) for i in range(2)]
        s_h = sem("s_h")
        s_si = sem("s_si")
        s_hi = sem("s_hi")
        s_lo = sem("s_lo")
        s_d = sem("s_d")
        s_yc = sem("s_yc")
        (w1h, w1l), (w2h, w2l) = wts
        block = ctx.enter_context(nc.Block())

        def place(n):
            return n // (2 * E), (n // 2) % E, n % 2

        @block.tensor
        def _(pe):
            for n in range(NS + LAG):
                if n < NS:
                    g, e, f = place(n)
                    if n >= 3:
                        pe.wait_ge(s_si, n - 2)
                    w = slice((2 * e + f) * P, (2 * e + f + 1) * P)
                    for k, (wp, xp) in enumerate(((w1h, 0), (w1h, 1), (w1l, 0))):
                        mm = nc.tensor.matmul(hb[n % 3][:], wp[:, w], xg[:, xp * E + e, g * GB:(g + 1) * GB, :],
                                              start=(k == 0), stop=(k == 2))
                    mm.then_inc(s_h, 1)
                m = n - LAG
                if m >= 0:
                    g, e, f = place(m)
                    w = slice((2 * e + f) * P, (2 * e + f + 1) * P)
                    pe.wait_ge(s_lo, m + 1)
                    if f == 0 and m >= 4:
                        pe.wait_ge(s_yc, m // 2 - 1)
                    for k, (wp, h) in enumerate(((w2h, hh), (w2h, hl), (w2l, hh))):
                        mm = nc.tensor.matmul(yb[(m // 2) % 2][:], wp[:, w], h[m % 3][:],
                                              start=(f == 0 and k == 0), stop=(f == 1 and k == 2))
                    mm.then_inc(s_d, 1)

        @block.scalar
        def _(act):
            for n in range(NS + LAG):
                if n < NS:
                    act.wait_ge(s_h, n + 1)
                    if n >= 2:
                        act.wait_ge(s_lo, n - 1)
                    nc.scalar.activation(h32[n % 2][:], hb[n % 3][:], ACT.Silu).then_inc(s_si, 1)
                    act.wait_ge(s_si, n + 1)
                    if n >= 3:
                        act.wait_ge(s_d, n - 2)
                    nc.scalar.activation(hh[n % 3][:], h32[n % 2][:], ACT.Copy).then_inc(s_hi, 1)
                m = n - LAG
                if m >= 0 and m % 2:
                    g, e, _f = place(m)
                    act.wait_ge(s_d, m + 1)
                    nc.scalar.activation(yT[:, g * GB:(g + 1) * GB, e, :],
                                         yb[(m // 2) % 2][:].rearrange("p (b j) -> p b j", j=K), ACT.Copy).then_inc(s_yc, 1)

        @block.vector
        def _(dve):
            for n in range(NS):
                dve.wait_ge(s_hi, n + 1)
                if n >= 3:
                    dve.wait_ge(s_d, n - 2)
                nc.vector.tensor_tensor(hl[n % 3][:], h32[n % 2][:], hh[n % 3][:].bitcast(F32),
                                        ALU.subtract).then_inc(s_lo, 1)


def scatter_outputs(nc, tag, resid, ident, oh, probs, yT, K2):
    E, K, S, D = 8, 16, 64, P
    NT = resid.shape[1] // D
    with ExitStack() as ctx:
        def sb(name, shape, dt=F32):
            return ctx.enter_context(nc.sbuf_tensor(tag + name, shape, dt))

        def sem(name):
            return ctx.enter_context(nc.semaphore(tag + name))
        ohw = [sb(f"one_hot_w{i}", [P, E, K]) for i in range(2)]
        ys = [sb(f"slots{i}", [P, 3 * P]) for i in range(2)]
        tb = [ctx.enter_context(nc.psum_tensor(tag + f"ps_t{i}", [P, 512], F32)) for i in range(2)]
        ob = [ctx.enter_context(nc.psum_tensor(tag + f"ps_o{i}", [P, 512], F32)) for i in range(2)]
        s_w = sem("s_w")
        s_t = sem("s_t")
        s_c = sem("s_c")
        s_o = sem("s_o")
        s_x = sem("s_x")
        pr = probs[:].rearrange("p (t e) -> p t e", e=E)
        block = ctx.enter_context(nc.Block())

        @block.gpsimd
        def _(pool):
            for t in range(NT):
                if t >= 2:
                    pool.wait_ge(s_t, t - 1)
                nc.gpsimd.tensor_tensor(ohw[t % 2][:], oh[:, t].bitcast(F32),
                                        pr[:, t, :].unsqueeze(2).to_broadcast((P, E, K)), ALU.mult).then_inc(s_w, 1)

        @block.tensor
        def _(pe):
            for n in range(NT + 1):
                if n < NT:
                    pe.wait_ge(s_w, n + 1)
                    if n >= 2:
                        pe.wait_ge(s_c, n - 1)
                    nc.tensor.transpose(tb[n % 2][:, 0:P], ohw[n % 2][:], ident[:])
                    for b in range(2):
                        mm = nc.tensor.transpose(tb[n % 2][:, (b + 1) * P:(b + 2) * P], yT[:, 2 * n + b], ident[:])
                    mm.then_inc(s_t, 1)
                t = n - 1
                if t >= 0:
                    pe.wait_ge(s_c, t + 1)
                    if t >= 2:
                        pe.wait_ge(s_x, t - 1)
                    for b in range(2):
                        mm = nc.tensor.matmul(ob[t % 2][b * S:(b + 1) * S, 0:D], ys[t % 2][:, b * S:(b + 1) * S],
                                              ys[t % 2][:, (b + 1) * P:(b + 2) * P], start=True, stop=True)
                    mm.then_inc(s_o, 1)

        @block.scalar
        def _(act):
            for t in range(NT):
                act.wait_ge(s_t, t + 1)
                if t >= 2:
                    act.wait_ge(s_o, t - 1)
                nc.scalar.activation(ys[t % 2][:], tb[t % 2][:, 0:3 * P], ACT.Copy).then_inc(s_c, 1)

        @block.vector
        def _(dve):
            attention_constants(nc, dve, ident, K2)
            for t in range(NT):
                dve.wait_ge(s_o, t + 1)
                cols = slice(t * D, (t + 1) * D)
                nc.vector.tensor_tensor(resid[:, cols], ob[t % 2][:, 0:D], resid[:, cols], ALU.add).then_inc(s_x, 1)


def expert_choice(nc, A, resid, ident, K2):
    NT, E, K = resid.shape[1] // P, 8, 16
    with ExitStack() as ctx:
        def sb(name, shape, dt=F32, stack=ctx):
            return stack.enter_context(nc.sbuf_tensor("ec_" + name, shape, dt))
        probs = sb("probs", [P, NT * E])
        pos = sb("pos", [P, NT * E])
        oh = sb("one_hot", [P, NT, E, K], FR)
        with ExitStack() as c2:
            xg = sb("xg", [P, 2 * E, 2 * NT, K], FR, c2)
            wts = [[sb(f"w{k}_{n}", [P, 2048], FR, c2) for n in ("hi", "lo")] for k in (1, 2)]
            with ExitStack() as c3:
                z = sb("z", [P, NT * P], F32, c3)
                norm_and_score(nc, "ec_ns_", resid, ident, A["cw"], E, z, probs, loads=lambda sp: load_attention_constants(nc, sp, A, K2))
                softmax_rows(nc, "ec_sm_", probs, E, NT)
                choose_tokens(nc, "ec_ch_", ident, probs, pos)
                gather_tokens(nc, A, "ec_ga_", z, pos, oh, xg, wts)
            yT = sb("yT", [P, 2 * NT, E, K], F32, c2)
            run_experts(nc, "ec_ex_", xg, wts, yT)
            scatter_outputs(nc, "ec_sc_", resid, ident, oh, probs, yT, K2)


def load_expert_weights(sp, A, W):
    EF = W["raw"][0].shape[1] - P
    for r, name in zip(W["raw"], ("Wg", "Wu")):
        sp.dma_start(r[:, 0:EF].rearrange("p (e f) -> p e f", e=A[name].shape[0]),
                     A[name].rearrange("e d f -> d e f")).then_inc(W["loaded"], 16)
    sp.dma_start(W["raw"][2][:, 0:EF].rearrange("p (s d) -> p s d", d=P),
                 A["Wd"].rearrange("(p h) f d -> (h f) p d", h=2)).then_inc(W["loaded"], 16)
    for r, name in zip(W["raw"], ("Sg", "Su", "Sd")):
        sp.dma_start(r[:, EF:], A[name]).then_inc(W["loaded"], 16)


def choose_experts(nc, tag, logits, cw, W):
    E, K = 16, 2
    NT = logits.shape[1] // E
    with ExitStack() as ctx:
        peak, total, rtotal = (ctx.enter_context(nc.sbuf_tensor(tag + n, [P, NT], F32)) for n in ("max", "sum", "rsum"))
        m8 = ctx.enter_context(nc.sbuf_tensor(tag + "best", [P, NT, 8], F32))
        left = ctx.enter_context(nc.sbuf_tensor(tag + "left", [P, NT, E], F32))
        s_v = ctx.enter_context(nc.semaphore(tag + "s_v"))
        s_e = ctx.enter_context(nc.semaphore(tag + "s_e"))
        s_sm = ctx.enter_context(nc.semaphore(tag + "s_sm"))
        s_hi = ctx.enter_context(nc.semaphore(tag + "s_hi"))
        s_sel = ctx.enter_context(nc.semaphore(tag + "s_sel"))
        pr = logits[:].rearrange("p (t e) -> p t e", e=E)
        block = ctx.enter_context(nc.Block())

        @block.scalar
        def _(act):
            act.wait_ge(W["loaded"], 6 * 16)
            for n, (raw, (hi, _lo)) in enumerate(zip(W["raw"], W["hi_lo"])):
                nc.scalar.activation(hi[:], raw[:], ACT.Copy).then_inc(s_hi, 1)
                if n == 0:
                    act.wait_ge(s_sm, 2)
                    nc.scalar.activation(logits[:], logits[:], ACT.Exp).then_inc(s_e, 1)
            act.wait_ge(s_sel, 3)
            nc.scalar.activation(W["sel"][:], W["sel32"][:].rearrange("p e f -> p (e f)"), ACT.Copy)

        @block.gpsimd
        def _(pool):
            sel = W["sel32"]
            nc.gpsimd.memset(sel[:], 0.0).then_inc(s_sel, 1)
            for k in range(2):
                pool.wait_ge(s_sel, k + 1)
                nc.gpsimd.affine_select(out=sel[:], in_=sel[:], compare_op=ALU.not_equal, fill=1.0, base=-k * E,
                                        pattern=[[-1, E], [0, sel.shape[2]]], channel_multiplier=1).then_inc(s_sel, 1)
            for n, (raw, (hi, lo)) in enumerate(zip(W["raw"], W["hi_lo"])):
                pool.wait_ge(s_hi, n + 1)
                nc.gpsimd.tensor_tensor(lo[:], raw[:], hi[:].bitcast(F32), ALU.subtract)

        @block.vector
        def _(dve):
            def spread(v):
                return v[:].unsqueeze(2).to_broadcast((P, NT, E))
            nc.vector.tensor_reduce(peak[:], pr, AX, ALU.max).then_inc(s_sm, 1)
            dve.wait_ge(s_sm, 1)
            nc.vector.tensor_tensor(pr, pr, spread(peak), ALU.subtract).then_inc(s_sm, 1)
            dve.wait_ge(s_e, 1)
            nc.vector.tensor_reduce(total[:], pr, AX, ALU.add).then_inc(s_sm, 1)
            dve.wait_ge(s_sm, 3)
            nc.vector.reciprocal(rtotal[:], total[:]).then_inc(s_sm, 1)
            dve.wait_ge(s_sm, 4)
            nc.vector.tensor_tensor(pr, pr, spread(rtotal), ALU.mult).then_inc(s_sm, 1)
            dve.wait_ge(s_sm, 5)
            for t in range(NT):
                nc.vector.max(m8[:, t, :], pr[:, t, :]).then_inc(s_v, 1)
            dve.wait_ge(s_v, NT)
            nc.vector.memset(m8[:, :, K:8], -5.0).then_inc(s_v, 1)
            dve.wait_ge(s_v, NT + 1)
            for t in range(NT):
                nc.vector.match_replace(left[:, t, :], m8[:, t, :], pr[:, t, :], -1.0).then_inc(s_v, 1)
            dve.wait_ge(s_v, 2 * NT + 1)
            nc.vector.tensor_scalar(left[:], left[:], -1.0, None, ALU.is_equal).then_inc(s_v, 1)
            dve.wait_ge(s_v, 2 * NT + 2)
            nc.vector.tensor_tensor(cw[:].rearrange("p (t e) -> p t e", e=E), left[:], pr, ALU.mult)


def transpose_weights(nc, tag, ident, cw, E, cwT):
    NT = cwT.shape[1] // P
    NG = NT // 4
    with ExitStack() as ctx:
        parts = ctx.enter_context(nc.sbuf_tensor(tag + "parts", [P, NT, 2 * E], F32))
        high = ctx.enter_context(nc.sbuf_tensor(tag + "high", [P, NT, E], FR))
        tb = [ctx.enter_context(nc.psum_tensor(tag + f"wt{i}", [P, 512], F32)) for i in range(2)]
        s_h = ctx.enter_context(nc.semaphore(tag + "s_h"))
        s_p = ctx.enter_context(nc.semaphore(tag + "s_p"))
        s_t = ctx.enter_context(nc.semaphore(tag + "s_wt"))
        s_c = ctx.enter_context(nc.semaphore(tag + "s_c"))
        cw3 = cw[:].rearrange("p (t e) -> p t e", e=E)
        block = ctx.enter_context(nc.Block())

        @block.vector
        def _(dve):
            dve.wait_ge(s_h, 1)
            nc.vector.tensor_copy(parts[:, :, 0:E], high[:].bitcast(F32)).then_inc(s_p, 1)
            nc.vector.tensor_tensor(parts[:, :, E:], cw3, high[:].bitcast(F32), ALU.subtract).then_inc(s_p, 1)

        @block.tensor
        def _(pe):
            pe.wait_ge(s_p, 2)
            for g in range(NG):
                if g >= 2:
                    pe.wait_ge(s_c, g - 1)
                for k in range(4):
                    mm = nc.tensor.transpose(tb[g % 2][0:2 * E, k * P:(k + 1) * P], parts[:, 4 * g + k, :], ident[:])
                mm.then_inc(s_t, 1)

        @block.scalar
        def _(act):
            nc.scalar.activation(high[:], cw3, ACT.Copy).then_inc(s_h, 1)
            for g in range(NG):
                act.wait_ge(s_t, g + 1)
                nc.scalar.activation(cwT[:, g * 512:(g + 1) * 512], tb[g % 2][0:2 * E, :], ACT.Copy).then_inc(s_c, 1)


def experts(nc, tag, resid, ident, zT, cwT, E, F, W, out):
    D, NG = P, zT[0].shape[1] // 512
    sel, ups, down = W["sel"], W["hi_lo"][:-1], W["hi_lo"][-1]
    steps = E * F // P + 1
    G = 2 if steps % 2 else 1
    SU = G * steps
    NU = NG // G
    LAG = 2
    with ExitStack() as ctx:
        def sb(name, shape, dt=F32):
            return ctx.enter_context(nc.sbuf_tensor(tag + name, shape, dt))

        def sem(name):
            return ctx.enter_context(nc.semaphore(tag + name))

        def pb(name):
            return ctx.enter_context(nc.psum_tensor(tag + name, [P, 512], F32))

        act_out = [sb(f"silu{i}", [P, 512]) for i in range(2)]
        prod = [sb(f"prod{i}", [P, 512]) for i in range(2)]
        hid = [sb(f"hid{i}", [P, 512]) for i in range(2)]
        hh = [sb(f"hid_hi{i}", [P, 512], FR) for i in range(2)]
        hl = [sb(f"hid_lo{i}", [P, 512], FR) for i in range(2)]
        yT = sb("yT", [P, 512])
        gb = [pb(f"gate{i}") for i in range(2)]
        ub = [pb(f"up{i}") for i in range(2)]
        cb = [pb(f"weight{i}") for i in range(2)]
        yb, tb = pb("y"), pb("t")
        s_g = sem("s_g")
        s_ucp = sem("s_up")
        s_si = sem("s_si")
        s_pr = sem("s_pr")
        s_hd = sem("s_hd")
        s_hi = sem("s_hi2")
        s_lo = sem("s_lo2")
        s_d = sem("s_d")
        s_yc = sem("s_yc")
        s_t = sem("s_yt")
        s_x = sem("s_x")

        def group_of(tile, s):
            u, c = tile
            k = s // steps
            return slice((c * G + k) * 512, (c * G + k + 1) * 512) if u is None else \
                bass.ds(u * (G * 512) + (c * G + k) * 512, 512)

        def norm(tile, s):
            return at(tile, s // SU), s % SU

        def on(tile):
            return live(tile, 0, NU)

        def schedule(clock, body):
            body((None, 0))
            with clock.eng.Fori(1, NU) as u:
                clock.enter(u)
                body((u, 0))
                clock.leave()
            body((None, NU))

        s_out = sem("s_out")

        TLAG = 2
        AFTER = LAG + TLAG
        block = ctx.enter_context(nc.Block())

        @block.sync
        def _(sp):
            c = Clock(sp, 1, {G: range(1, G + 1)})
            tiles = out.rearrange("(t b) s d -> (b s) t d", b=2)

            def body(i):
                u, v = i
                for k in range(G):
                    c.ge(s_x, G, i, k + 1, alone=True)
                    t = slice((v * G + k) * 4, (v * G + k + 1) * 4) if u is None else bass.ds(u * (G * 4) + k * 4, 4)
                    sp.dma_start(tiles[:, t, :], resid[:, group_of(i, k * steps)].rearrange("p (t d) -> p t d", d=D)
                                 ).then_inc(s_out, 16)
            body((None, 0))
            with sp.Fori(1, NU) as u:
                c.enter(u)
                body((u, 0))
                c.leave()
            sp.wait_ge(s_out, 16 * NG)

        @block.tensor
        def _(pe):
            c = Clock(pe, 1, {SU: range(-1, SU - 1), G: (-1, 0, 1)})

            def body(i):
                for s in range(SU):
                    if on(i):
                        cols = group_of(i, s)
                        m = s % steps
                        r = s % 2
                        w = slice(m * P, (m + 1) * P)
                        weighted = m < steps - 1
                        c.ge(s_si, SU, i, s - 1)
                        for b, (wp, zp) in enumerate(((0, 0), (0, 1), (1, 0))):
                            mm = nc.tensor.matmul(gb[r][:], ups[0][wp][:, w], zT[zp][:, cols], start=(b == 0), stop=(b == 2))
                        mm.then_inc(s_g, 1)
                        c.ge(s_hd, SU, i, s - 1)
                        for b, (wp, zp) in enumerate(((0, 0), (0, 1), (1, 0))):
                            mm = nc.tensor.matmul(ub[r][:], ups[1][wp][:, w], zT[zp][:, cols], start=(b == 0), stop=(b == 2))
                        if weighted:
                            mm = nc.tensor.matmul(cb[r][:], sel[:, w], cwT[:, cols], start=True, stop=True)
                        mm.then_inc(s_ucp, 1)
                    td, kd = norm(i, s - LAG)
                    if on(td):
                        m = kd % steps
                        w = slice(m * P, (m + 1) * P)
                        c.ge(s_lo, SU, td, kd + 1)
                        if m == 0:
                            c.ge(s_yc, G, td, kd // steps)
                        for b, (wp, h) in enumerate(((0, hh), (0, hl), (1, hh))):
                            mm = nc.tensor.matmul(yb[:], down[wp][:, w], h[kd % 2][:], start=(m == 0 and b == 0),
                                                  stop=(m == steps - 1 and b == 2))
                        mm.then_inc(s_d, 1)
                    ty, ky = norm(i, s - AFTER)
                    if on(ty) and ky % steps == steps - 1:
                        k = ky // steps
                        c.ge(s_yc, G, ty, k + 1)
                        c.ge(s_x, G, ty, k)
                        for b in range(4):
                            mm = nc.tensor.transpose(tb[:, b * P:(b + 1) * P], yT[:, b * P:(b + 1) * P], ident[:])
                        mm.then_inc(s_t, 1)
                    if not on(i) and i[1] == NU and s >= AFTER:
                        break
            schedule(c, body)

        @block.scalar
        def _(act):
            c = Clock(act, 1, {SU: range(-2, SU + 1), G: (-1, 0)})

            def body(i):
                for s in range(SU):
                    if on(i):
                        c.ge(s_g, SU, i, s + 1)
                        c.ge(s_hd, SU, i, s - 1)
                        nc.scalar.activation(act_out[s % 2][:], gb[s % 2][:], ACT.Silu).then_inc(s_si, 1)
                    th, kh = norm(i, s - 1)
                    if on(th):
                        c.ge(s_hd, SU, th, kh + 1)
                        c.ge(s_d, SU, th, kh + 1 - 2)
                        nc.scalar.activation(hh[kh % 2][:], hid[kh % 2][:], ACT.Copy).then_inc(s_hi, 1)
                    ty, ky = norm(i, s - LAG)
                    if on(ty) and ky % steps == steps - 1:
                        c.ge(s_d, SU, ty, ky + 1)
                        c.ge(s_t, G, ty, ky // steps)
                        nc.scalar.activation(yT[:], yb[:], ACT.Copy).then_inc(s_yc, 1)
            schedule(c, body)

        @block.vector
        def _(dve):
            c = Clock(dve, 1, {SU: range(-1, SU + 1), G: (0, 1), G * (steps - 1): range(1, G * (steps - 1) + 1)})

            def body(i):
                for s in range(SU):
                    if on(i):
                        r = s % 2
                        weighted = s % steps < steps - 1
                        c.ge(s_si, SU, i, s + 1)
                        c.ge(s_ucp, SU, i, s + 1)
                        c.ge(s_lo, SU, i, s - 1)
                        if weighted:
                            nc.vector.tensor_tensor(prod[r][:], ub[r][:], act_out[r][:], ALU.mult).then_inc(s_pr, 1)
                            c.ge(s_pr, G * (steps - 1), i, s + 1 - s // steps)
                            mm = nc.vector.tensor_tensor(hid[r][:], cb[r][:], prod[r][:], ALU.mult)
                        else:
                            mm = nc.vector.tensor_tensor(hid[r][:], ub[r][:], act_out[r][:], ALU.mult)
                        mm.then_inc(s_hd, 1)
                    ty, ky = norm(i, s - AFTER)
                    if on(ty) and ky % steps == steps - 1:
                        c.ge(s_t, G, ty, ky // steps + 1)
                        cols = group_of(ty, ky)
                        nc.vector.tensor_tensor(resid[:, cols], tb[:], resid[:, cols], ALU.add).then_inc(s_x, 1)
            schedule(c, body)

        @block.gpsimd
        def _(pool):
            c = Clock(pool, 1, {SU: range(SU)})

            def body(i):
                for s in range(SU):
                    th, kh = norm(i, s - 1)
                    if on(th):
                        c.ge(s_hi, SU, th, kh + 1)
                        nc.gpsimd.tensor_tensor(hl[kh % 2][:], hid[kh % 2][:], hh[kh % 2][:].bitcast(F32),
                                                ALU.subtract).then_inc(s_lo, 1)
            schedule(c, body)


def mixture(nc, A, resid, ident, out):
    NT, E, F, tag = resid.shape[1] // P, 16, 64, "mx_"
    with ExitStack() as ctx:
        def sb(name, shape, dt=F32, stack=ctx):
            return stack.enter_context(nc.sbuf_tensor(tag + name, shape, dt))
        cols = E * F + P
        zT = [sb(f"zT_{n}", [P, NT * P], FR) for n in ("hi", "lo")]
        cwT = sb("cwT", [2 * E, NT * P], FR)
        W = {"hi_lo": [[sb(f"{w}_{n}", [P, cols], FR) for n in ("hi", "lo")] for w in ("gate", "up", "down")],
             "sel": sb("sel", [2 * E, E * F], FR),
             "loaded": ctx.enter_context(nc.semaphore(tag + "s_loaded"))}
        with ExitStack() as c2:
            W["raw"] = [sb(f"{w}_raw", [P, cols], F32, c2) for w in ("gate", "up", "down")]
            W["sel32"] = sb("sel32", [2 * E, E, F], F32, c2)
            z = sb("z", [P, NT * P], F32, c2)
            logits = sb("logits", [P, NT * E], F32, c2)
            cw = sb("cw", [P, NT * E], F32, c2)
            norm_and_score(nc, tag + "ns_", resid, ident, A["Wr"], E, z, logits, split=zT,
                           loads=lambda sp: load_expert_weights(sp, A, W))
            choose_experts(nc, tag + "ch_", logits, cw, W)
            transpose_weights(nc, tag + "tw_", ident, cw, E, cwT)
        experts(nc, tag + "ex_", resid, ident, zT, cwT, E, F, W, out)


BIG_HI, BIG_LO = float(3814 << 18), float(1000000000 - (3814 << 18))


def load_attention_constants(nc, sp, A, K):
    s = K["loaded"]
    with nc.allow_non_contiguous_dma(reason="one bias a partition"):
        sp.dma_start(K["bq1"][:], A["aq_b"].unsqueeze(1)).then_inc(s, 16)
        sp.dma_start(K["bk1"][:], A["ak_b"].unsqueeze(1)).then_inc(s, 16)
    sp.dma_start(K["wo1"][:], A["ao_w"]).then_inc(s, 16)
    sp.dma_start(K["wq"][:], A["aq_w"]).then_inc(s, 16)
    sp.dma_start(K["wk"][:], A["ak_w"]).then_inc(s, 16)
    sp.dma_start(K["wv"][:], A["av_w"]).then_inc(s, 16)
    sp.dma_start(K["bv"][:], A["av_b"].partition_broadcast(P)).then_inc(s, 16)
    sp.dma_start(K["bo"][:], A["ao_b"].partition_broadcast(P)).then_inc(s, 16)


def attention_constants(nc, dve, ident, K):
    S = 64
    nc.vector.tensor_reduce(K["heads"][:], ident[:].rearrange("p (h d) -> p h d", h=16), AX, ALU.add).then_inc(K["steps"], 1)
    dve.wait_ge(K["steps"], 1)
    nc.vector.tensor_reduce(K["jj"][:], K["heads"][:].rearrange("p (a j) -> p j a", j=2), AX, ALU.add).then_inc(K["steps"], 1)
    nc.vector.tensor_reduce(K["pairs"][:], K["heads"][:].rearrange("p (a j) -> p a j", j=2), AX, ALU.add).then_inc(K["steps"], 1)
    dve.wait_ge(K["steps"], 3)
    nc.vector.tensor_reduce(K["jp"][:], K["pairs"][:].rearrange("p (r j) -> p j r", j=2), AX, ALU.add).then_inc(K["steps"], 1)
    nc.vector.memset(K["big"][0:S], BIG_HI)
    nc.vector.memset(K["big"][S:], BIG_LO)
    for half in range(2):
        cols = slice(half * S, (half + 1) * S)
        nc.vector.tensor_tensor(K["twice"][:, cols], ident[:, 0:S], ident[:, S:P], ALU.add)
    dve.wait_ge(K["loaded"], 8 * 16)
    for j in range(2):
        nc.vector.tensor_scalar(K["wo"][:, j, :], K["wo1"][:], K["jj"][:, j:j + 1], None, ALU.mult)
    nc.vector.tensor_scalar(K["sq"][:], K["jj"][:], float(8) ** -0.5, None, ALU.mult).then_inc(K["steps"], 1)
    dve.wait_ge(K["steps"], 5)
    nc.vector.tensor_scalar(K["bq"][:], K["sq"][:], K["bq1"][:], None, ALU.mult)
    nc.vector.tensor_scalar(K["bk"][:], K["jp"][:], K["bk1"][:], None, ALU.mult)
    for r in range(2):
        nc.vector.memset(K[f"vb{r}"][:], 0.0)


def attention(nc, A, resid, ident, K):
    D, S, H = P, 64, 16
    NQ = resid.shape[1] // (2 * D)
    with ExitStack() as ctx:
        def sb(name, shape, dt=F32):
            return ctx.enter_context(nc.sbuf_tensor("at_" + name, shape, dt))

        def sem(name):
            return ctx.enter_context(nc.semaphore("at_" + name))

        def pb(name):
            return ctx.enter_context(nc.psum_tensor("at_" + name, [P, 512], F32))

        st, mv = sb("ln_stats", [P, 2, 6]), sb("ln_meanvar", [P, 2, 2])
        ve, rstd, mhalf = sb("ln_vareps", [P, 2]), sb("ln_rstd", [P, 2]), sb("minus_half", [P, 2])
        z = sb("z", [P, 2, D])
        ctx_in = [sb(f"ctx_in{i}", [P, 2, D]) for i in range(2)]
        gp_in = [sb(f"gp_in{i}", [P, 4, S]) for i in range(2)]
        mask_in = [sb(f"mask_in{i}", [P, 4, S], I32) for i in range(2)]
        neg = [sb(f"neg{i}", [P, 4, S], FR) for i in range(2)]
        zT = sb("zT", [P, 256])
        ctxT = sb("ctxT", [P, 4, 2, S])
        qx = [sb(f"qx{i}", [P, 4, 2, S]) for i in range(2)]
        kx = [sb(f"kx{i}", [P, 4, 2, S]) for i in range(2)]
        vb = [K["vb0"], K["vb1"]]
        sm = [sb(f"scores{i}", [P, 4, 2, S]) for i in range(2)]
        mx = [sb(f"max{i}", [P, 4, 2]) for i in range(2)]
        ex = [sb(f"exp{i}", [P, 4, 2, S]) for i in range(2)]
        pg = [sb(f"probs{i}", [P, 4, 2, S]) for i in range(4)]
        pT = [sb(f"probsT{i}", [P, 512]) for i in range(2)]
        zs, rz = [sb(f"exp_sum{i}", [P, 4, 2]) for i in range(2)], [sb(f"exp_rsum{i}", [P, 4, 2]) for i in range(2)]
        oT = sb("outT", [P, 2, 4, S])
        sbank, tbank = ([pb(f"{n}{i}") for i in range(2)] for n in ("ps_s", "ps_t"))
        obank, prep, qkbank, ybank = pb("ps_o"), pb("ps_prep"), pb("ps_qk"), pb("ps_y")

        s_half = sem("s_half")
        s_ln = sem("s_ln")
        s_rs = sem("s_rs")
        s_cin = [sem(f"s_cin{i}") for i in range(2)]
        s_gin = [sem(f"s_gin{i}") for i in range(2)]
        s_neg = sem("s_neg")
        s_zt = sem("s_zt")
        s_ztc = sem("s_ztc")
        s_qk = sem("s_qk")
        s_qx = sem("s_qx")
        s_v = sem("s_v")
        s_vb = sem("s_vb")
        s_s = sem("s_s")
        s_mx = sem("s_mx")
        s_sub = sem("s_sub")
        s_e = sem("s_e")
        s_sum = sem("s_sum")
        s_rz = sem("s_rz")
        s_gp = sem("s_gp")
        s_pn = sem("s_pn")
        s_t = sem("s_t")
        s_ptc = sem("s_ptc")
        s_pv = sem("s_pv")
        s_otc = sem("s_otc")
        s_y = sem("s_y")
        s_x = sem("s_x")

        def step(i, j):
            return at(i, j // 4), j % 4

        def quad_cols(q, width):
            u, c = q
            return slice(c * width, (c + 1) * width) if u is None else bass.ds(u * (2 * width) + c * width, width)

        def quad_batches(q, n):
            u, c = q
            return slice(n * c, n * (c + 1)) if u is None else bass.ds(u * (2 * n) + n * c, n)

        def loaded(clock, sems, per, q):
            u, c = q
            clock.ge(sems[c % 2], per // 2 if u is not None else per, q if u is not None else (None, c // 2),
                     per * (c // 2 + 1) - (per // 2) * c if u is not None else per)

        def on_(q):
            return live(q, 0, NQ)

        def schedule(clock, body):
            for i in range(-3, 4):
                body((None, i))
            with clock.eng.Fori(2, NQ // 2 - 2) as u:
                clock.enter(u)
                body((u, 0))
                body((u, 1))
                clock.leave()
            for i in range(NQ - 4, NQ + 2):
                body((None, i))

        block = ctx.enter_context(nc.Block())

        @block.sync
        def _(sp):
            c = Clock(sp, 2, KEYS["attention", "SP"])

            def body(i):
                tc = at(i, 3)
                if on_(tc):
                    c.ge(s_zt, 1, tc, -1, alone=True)
                    sp.dma_start(ctx_in[tc[1] % 2][:], A["ctx"].rearrange("(t b) s d -> (b s) t d", b=2)
                                 [:, quad_batches(tc, 2), :]).then_inc(s_cin[tc[1] % 2], 16)
                tg = at(i, 2)
                if on_(tg):
                    c.ge(s_gp, 4, tg, -4)
                    c.ge(s_neg, 1, tg, -1, alone=True)
                    for dst, src in ((gp_in, "gp"), (mask_in, "mask")):
                        for jj in range(2):
                            sp.dma_start(dst[tg[1] % 2][jj * S:(jj + 1) * S], A[src].rearrange("b q k -> q b k")
                                         [:, quad_batches(tg, 4), :]).then_inc(s_gin[tg[1] % 2], 16)
            schedule(c, body)

        @block.tensor
        def _(pe):
            c = Clock(pe, 2, KEYS["attention", "PE"])

            def body(i):
                for j in range(4):
                    if on_(i):
                        r = i[1] % 2
                        rows = slice(32 * j, 32 * j + 32)
                        if j == 0:
                            c.ge(s_qx, 4, i, 4)
                            c.ge(s_neg, 1, i, 1)
                        c.ge(s_sub, 4, i, j - 1)
                        for b in range(4):
                            nc.tensor.matmul(sbank[j % 2][:, b * P:(b + 1) * P], qx[r][rows, b], kx[r][rows, b],
                                             start=(b == 0), stop=False)
                        nc.tensor.matmul(sbank[j % 2][:], K["twice"][:],
                                         neg[r][:].unsqueeze(2).to_broadcast((P, 4, 2, S)), start=False,
                                         stop=True).then_inc(s_s, 1)
                    tt, kt = step(i, j - 3)
                    if on_(tt):
                        c.ge(s_pn, 4, tt, kt + 1)
                        c.ge(s_ptc, 4, tt, kt - 1)
                        for b in range(4):
                            mm = nc.tensor.transpose(tbank[kt % 2][:, b * P:(b + 1) * P], pg[kt][:, b], ident[:])
                        mm.then_inc(s_t, 1)
                    ti = at(i, 1)
                    if j == 0 and on_(ti):
                        c.ge(s_ln, 6, ti, 6)
                        c.ge(s_ztc, 1, ti, 0)
                        loaded(c, s_cin, 16, ti)
                        for t in range(2):
                            nc.tensor.transpose(prep[:, t * P:(t + 1) * P], z[:, t], ident[:])
                        for t in range(2):
                            mm = nc.tensor.transpose(prep[:, (2 + t) * P:(3 + t) * P], ctx_in[ti[1] % 2][:, t], ident[:])
                        mm.then_inc(s_zt, 1)
                    if j == 1 and on_(ti):
                        c.ge(s_ztc, 1, ti, 1)
                        c.ge(s_vb, 2, ti, 0)
                        nc.tensor.matmul(qkbank[:, 0:256], K["wq"][:], zT[:], start=True, stop=True)
                        nc.tensor.matmul(qkbank[:, 256:512], K["wk"][:], ctxT[:, :, 0, :], start=True, stop=True).then_inc(s_qk, 1)
                    ty = at(i, -2)
                    if j == 1 and on_(ty):
                        c.ge(s_otc, 1, ty, 1)
                        c.ge(s_x, 1, ty, 0)
                        for t in range(2):
                            for jj in range(2):
                                nc.tensor.matmul(ybank[:, t * P:(t + 1) * P], oT[:, jj, 2 * t:2 * t + 2, :],
                                                 K["wo"][:, jj, :], start=(jj == 0), stop=False)
                            mm = nc.tensor.matmul(ybank[:, t * P:(t + 1) * P], ident[:], K["bo"][:], start=False, stop=True)
                        mm.then_inc(s_y, 1)
                    tv, kv = step(i, j - 4)
                    if on_(tv):
                        c.ge(s_ptc, 4, tv, kv + 1)
                        if kv == 0:
                            c.ge(s_vb, 2, tv, 2)
                            c.ge(s_otc, 1, tv, 0)
                        for b in range(4):
                            mm = nc.tensor.matmul(obank[32 * kv:32 * kv + 32, b * P:(b + 1) * P],
                                                  vb[tv[1] % 2][:, b, 32 * kv:32 * kv + 32],
                                                  pT[kv % 2][:, b * P:(b + 1) * P], start=True, stop=True)
                        mm.then_inc(s_pv, 1)
                    if j == 2 and on_(ti):
                        c.ge(s_qx, 4, ti, 4)
                        for b in range(4):
                            mm = nc.tensor.matmul(qkbank[:, b * P:(b + 1) * P], ctxT[:, b], K["wv"][:], start=True,
                                                  stop=True)
                        mm.then_inc(s_v, 1)
            schedule(c, body)

        @block.scalar
        def _(act):
            c = Clock(act, 2, KEYS["attention", "ACT"])

            def body(i):
                for j in range(4):
                    tt, kt = step(i, j - 3)
                    if on_(tt):
                        c.ge(s_t, 4, tt, kt + 1)
                        c.ge(s_pv, 4, tt, kt - 1)
                        nc.scalar.activation(pT[kt % 2][:], tbank[kt % 2][:], ACT.Copy).then_inc(s_ptc, 1)
                    ti = at(i, 1)
                    if j == 0 and on_(ti):
                        c.ge(s_zt, 1, ti, 1)
                        c.ge(s_v, 1, ti, 0)
                        nc.scalar.activation(zT[:], prep[:, 0:256], ACT.Copy)
                        nc.scalar.activation(ctxT[:], prep[:, 256:512].rearrange("p (b s) -> p b s", b=4).unsqueeze(2)
                                             .to_broadcast((P, 4, 2, S)), ACT.Copy).then_inc(s_ztc, 1)
                    if j == 1 and on_(ti):
                        c.ge(s_qk, 1, ti, 1)
                        r = ti[1] % 2
                        for k in range(2):
                            for dst, off, scale, bias in ((qx, 0, "sq", "bq"), (kx, 256, "jp", "bk")):
                                nc.scalar.activation(dst[r][:, :, k, :],
                                                     qkbank[:, off:off + 256].rearrange("p (b s) -> p b s", b=4),
                                                     ACT.Identity, bias=K[bias][:, k:k + 1],
                                                     scale=K[scale][:, k:k + 1]).then_inc(s_qx, 1)
                    to = at(i, -1)
                    if j == 3 and on_(to):
                        c.ge(s_pv, 4, to, 4)
                        c.ge(s_y, 1, to, 0)
                        nc.scalar.activation(oT[:], obank[:].rearrange("p (b j s) -> p j b s", b=4, j=2),
                                             ACT.Copy).then_inc(s_otc, 1)
                    if on_(i):
                        c.ge(s_sub, 4, i, j + 1)
                        c.ge(s_gp, 4, i, j - 1)
                        c.ge(s_sum, 4, i, j - 1)
                        nc.scalar.activation(ex[j % 2][:], sm[j % 2][:], ACT.Exp).then_inc(s_e, 1)
            schedule(c, body)

        @block.vector
        def _(dve):
            c = Clock(dve, 2, KEYS["attention", "DVE"])

            def body(i):
                for j in range(4):
                    if on_(i):
                        c.ge(s_s, 4, i, j + 1)
                        nc.vector.tensor_reduce(mx[j % 2][:], sbank[j % 2][:].rearrange("p (b j s) -> p b j s", b=4, j=2), AX,
                                                ALU.max).then_inc(s_mx, 1)
                        c.ge(s_mx, 4, i, j + 1)
                        c.ge(s_e, 4, i, j - 1)
                        nc.vector.tensor_tensor(sm[j % 2][:], sbank[j % 2][:].rearrange("p (b j s) -> p b j s", b=4, j=2),
                                                mx[j % 2][:].unsqueeze(3).to_broadcast((P, 4, 2, S)),
                                                ALU.subtract).then_inc(s_sub, 1)
                    ts, ks = step(i, j - 1)
                    if on_(ts):
                        c.ge(s_e, 4, ts, ks + 1)
                        c.ge(s_pn, 4, ts, ks - 1)
                        nc.vector.tensor_reduce(zs[ks % 2][:], ex[ks % 2][:], AX, ALU.add).then_inc(s_sum, 1)
                        c.ge(s_sum, 4, ts, ks + 1)
                        nc.vector.reciprocal(rz[ks % 2][:], zs[ks % 2][:]).then_inc(s_rz, 1)
                    tp = at(i, -1)
                    ti = at(i, 1)
                    if j == 3 and on_(ti):
                        c.ge(s_v, 1, ti, 1)
                        if live(tp, 0, NQ):
                            c.ge(s_pv, 4, tp, 4)
                        for jp in range(2):
                            rows = slice(jp * S, (jp + 1) * S)
                            src = qkbank[rows, :].rearrange("p (b r j e) -> p b r j e", b=4, r=4, j=2)[:, :, :, jp, :]
                            dst = vb[ti[1] % 2][rows].rearrange("p b (r j e) -> p b r j e", r=4, j=2)[:, :, :, jp, :]
                            bias = K["bv"][rows].rearrange("p (r j e) -> p r j e", r=4, j=2)[:, :, jp, :]
                            nc.vector.tensor_tensor(dst, src, bias.unsqueeze(1).to_broadcast((S, 4, 4, 16)),
                                                    ALU.add).then_inc(s_vb, 1)
                    ty = at(i, -2)
                    if j == 2 and on_(ty):
                        c.ge(s_y, 1, ty, 1)
                        cols = quad_cols(ty, 2 * D)
                        nc.vector.tensor_tensor(resid[:, cols], ybank[:, 0:256], resid[:, cols], ALU.add).then_inc(s_x, 1)
                    tl = at(i, 2)
                    if on_(tl) and j in (0, 2):
                        x = resid[:, quad_cols(tl, 2 * D)].rearrange("p (t d) -> p t d", t=2)
                        if j == 0:
                            for t in range(2):
                                nc.vector.bn_stats(st[:, t, :], x[:, t, :]).then_inc(s_ln, 1)
                            c.ge(s_ln, 6, tl, 2, alone=True)
                            for t in range(2):
                                nc.vector.bn_aggr(mv[:, t, :], st[:, t, :]).then_inc(s_ln, 1)
                        else:
                            c.ge(s_rs, 2, tl, 2)
                            c.ge(s_zt, 1, tl, 0)
                            for t in range(2):
                                nc.vector.tensor_scalar(z[:, t, :], x[:, t, :], mv[:, t, 0:1], rstd[:, t:t + 1],
                                                        ALU.subtract, ALU.mult).then_inc(s_ln, 1)
            schedule(c, body)

        @block.gpsimd
        def _(pool):
            c = Clock(pool, 2, KEYS["attention", "Pool"])
            nc.gpsimd.memset(mhalf[:], -0.5).then_inc(s_half, 1)
            pool.wait_ge(s_half, 1)

            def body(i):
                for j in range(4):
                    tm = at(i, 1)
                    if j == 2 and on_(tm):
                        loaded(c, s_gin, 64, tm)
                        c.ge(s_s, 4, tm, -4, alone=True)
                        nc.gpsimd.tensor_scalar(neg[tm[1] % 2][:], mask_in[tm[1] % 2][:], -1.0, K["big"][:], ALU.add,
                                                ALU.mult).then_inc(s_neg, 1)
                    ts, ks = step(i, j - 1)
                    if on_(ts):
                        c.ge(s_e, 4, ts, ks + 1)
                        c.ge(s_t, 4, ts, ks - 3, alone=True)
                        gp = gp_in[ts[1] % 2][:].unsqueeze(2).to_broadcast((P, 4, 2, S))
                        nc.gpsimd.tensor_tensor(pg[ks][:], ex[ks % 2][:], gp, ALU.mult).then_inc(s_gp, 1)
                        c.ge(s_rz, 4, ts, ks + 1)
                        c.ge(s_gp, 4, ts, ks + 1)
                        nc.gpsimd.tensor_tensor(pg[ks][:], pg[ks][:],
                                                rz[ks % 2][:].unsqueeze(3).to_broadcast((P, 4, 2, S)),
                                                ALU.mult).then_inc(s_pn, 1)
                    tl = at(i, 2)
                    if on_(tl) and j == 1:
                        c.ge(s_ln, 6, tl, 4, alone=True)
                        nc.gpsimd.tensor_scalar(ve[:], mv[:, :, 1], EPS, None, ALU.add).then_inc(s_rs, 1)
                        c.ge(s_rs, 2, tl, 1)
                        nc.gpsimd.tensor_tensor(rstd[:], ve[:], mhalf[:], ALU.pow).then_inc(s_rs, 1)
            schedule(c, body)


def attention_buffers(nc, ctx):
    shapes = {"big": [P, 1], "wq": [P, P], "wk": [P, P], "wv": [P, P], "wo1": [P, P], "bv": [P, P], "bo": [P, P],
              "jj": [P, 2], "jp": [P, 2], "sq": [P, 2], "bq1": [P, 1], "bk1": [P, 1], "bq": [P, 2], "bk": [P, 2],
              "wo": [P, 2, P], "heads": [P, 16], "pairs": [P, 8], "vb0": [P, 4, P], "vb1": [P, 4, P]}
    K = {k: ctx.enter_context(nc.sbuf_tensor("attn_" + k, s, F32)) for k, s in shapes.items()}
    K["twice"] = ctx.enter_context(nc.sbuf_tensor("attn_twice", [P, P], FR))
    K["loaded"] = ctx.enter_context(nc.semaphore("attn_loaded"))
    K["steps"] = ctx.enter_context(nc.semaphore("attn_steps"))
    return K

KEYS = {
    ("attention", "SP"): {1: (1, 2, 3), 4: (4, 8)},
    ("attention", "PE"): {1: range(-2, 4), 2: (0, 2, 4), 4: (*range(-4, 7), 8, 12), 6: (12, 18), 8: (16, 32)},
    ("attention", "ACT"): {1: range(-1, 4), 4: range(-4, 9)},
    ("attention", "DVE"): {1: (-1, 0, 2, 3), 2: (6, 8), 4: range(-2, 9), 6: (14, 20)},
    ("attention", "Pool"): {2: (5, 7), 4: range(-4, 8), 6: (16, 22), 32: (64, 128)},

    ("perceiver", "PE"): {1: (-2, -1, 0, 2, 3), 2: range(0, 10, 2), 4: range(-4, 12)},
    ("perceiver", "ACT"): {1: (-2, -1, 0, 2, 3), 4: range(-3, 9)},
    ("perceiver", "DVE"): {1: (-1, 0), 2: (6, 8), 4: (*range(-2, 13), 14, 16, 18, 20),
                           12: (38, 40, 42, 44, 46, 50, 52, 54, 56, 58)},
    ("perceiver", "Pool"): {1: (1, 2), 2: range(2, 8), 4: (*range(-2, 8), 13, 15, 17, 19),
                            12: (36, 40, 46, 48, 52, 58)},
}


def build(nc, A, out):
    NT = A["x"].shape[0] // 2
    with ExitStack() as ctx:
        def sb(name, shape, dt=F32):
            return ctx.enter_context(nc.sbuf_tensor(name, shape, dt))
        resid = sb("resid", [P, NT * P])
        ident = sb("ident", [P, P])
        with ExitStack() as c2:
            def sb2(name, shape, dt=F32):
                return c2.enter_context(nc.sbuf_tensor(name, shape, dt))
            kvraw = sb2("kvraw", [P, 2 * NT * P])
            wts = {k: sb2("fold_" + k, [P, 2048]) for k in ("A", "V")}
            wts["gain"] = sb2("ln_gain", [P, P])
            wts["shift"] = sb2("ln_shift", [P, P])
            perceiver(nc, A, resid, kvraw, ident, wts)
        with ExitStack() as c3:
            K = attention_buffers(nc, c3)
            expert_choice(nc, A, resid, ident, K)
            attention(nc, A, resid, ident, K)
        mixture(nc, A, resid, ident, out)


_NAMES = {"x": "x", "ctx": "ctx_1024", "gp": "fside_BxSxS2_0", "mask": "mask_BxSxS2_ik1",
          "ln_m_g": "L0_xattn_ln_m_g", "ln_m_b": "L0_xattn_ln_m_b", "ln_l_g": "L0_xattn_ln_l_g",
          "ln_l_b": "L0_xattn_ln_l_b", "wq": "L0_xattn_Wq", "wkv": "L0_xattn_Wkv", "wout": "L0_xattn_Wout",
          "cw": "L0_ffn_choice_w", "w1": "L0_ffn_w1", "w2": "L0_ffn_w2",
          "aq_w": "L1_xattn_wq_k", "aq_b": "L1_xattn_wq_b", "ak_w": "L1_xattn_wk_k", "ak_b": "L1_xattn_wk_b",
          "av_w": "L1_xattn_wv_k", "av_b": "L1_xattn_wv_b", "ao_w": "L1_xattn_wo_k", "ao_b": "L1_xattn_wo_b",
          "Wr": "L1_ffn_Wr", "Wg": "L1_ffn_Wg", "Wu": "L1_ffn_Wu", "Wd": "L1_ffn_Wd",
          "Sg": "L1_ffn_Sg", "Su": "L1_ffn_Su", "Sd": "L1_ffn_Sd"}


def kernel(**inputs):
    import numpy as _np
    import concourse.bacc as _bacc
    from concourse.bass_utils import run_bass_kernel_spmd as _run

    nc = _bacc.Bacc("TRN2", target_bir_lowering=False, num_devices=1)
    arrays, A = {}, {}
    for short, name in _NAMES.items():
        a = _np.ascontiguousarray(inputs[name])
        arrays["in_" + short] = a
        A[short] = nc.dram_tensor("in_" + short, a.shape, mybir.dt.from_np(a.dtype), kind="ExternalInput").ap()
    out = nc.dram_tensor("out", A["x"].shape, F32, kind="ExternalOutput").ap()
    build(nc, A, out)
    r = _run(nc, [arrays], core_ids=[0])
    return r.results[0]["out"]
```
